# Optimizing a Trainium2 kernel written in Bass

```python
import numpy as np
import jax
import jax.numpy as jnp

def _softmax(x, axis=-1):
    return jax.nn.softmax(x, axis=axis)

def _gelu(x):
    return jax.nn.gelu(x, approximate=True)

def _silu(x):
    return jax.nn.silu(x)

def _sigmoid(x):
    return jax.nn.sigmoid(x)

def _layernorm(x, axis=-1, eps=1e-05):
    m = jnp.mean(x, axis=axis, keepdims=True)
    v = jnp.var(x, axis=axis, keepdims=True)
    return (x - m) / jnp.sqrt(v + eps)

def _scatter_add(tgt, idx, src, axis=0):
    return tgt.at[idx].add(src)

def _segment_sum(src, seg, n):
    return jax.ops.segment_sum(src, seg, n)
kernel_name = 'mk_flamingo_gated_d4_seqx_r4_97f1f4'

def setup_inputs(seed: int=0):
    np.random.seed(seed)
    _w = jnp.asarray

    def _rec_inputs():
        import jax
        import jax.numpy as jnp
        _rk = jax.random.key(seed)
        x = -0.0002928 + 1 * jax.random.normal(jax.random.fold_in(_rk, 1), (2, 1024, 256), jnp.float32)
        _lenS = 1024 - jax.random.randint(jax.random.fold_in(_rk, 7), (2,), 0, max(1, 1024 // 4) + 1, jnp.int32)
        _lenS2 = 77 - jax.random.randint(jax.random.fold_in(_rk, 8), (2,), 0, max(1, 77 // 4) + 1, jnp.int32)
        _ctx_1024P = jax.random.normal(jax.random.fold_in(_rk, 11), (2, 16, 256), jnp.float32)
        _ctx_1024c = jax.random.dirichlet(jax.random.fold_in(_rk, 511), 0.3 * jnp.ones((16,), jnp.float32), (2, 77))
        _ctx_1024t = jnp.einsum('bsk,bkd->bsd', _ctx_1024c, _ctx_1024P)
        _ctx_1024t = _ctx_1024t * jax.lax.rsqrt(jnp.mean(jnp.square(_ctx_1024t)) + 1e-12) * 0.953939
        ctx_1024 = -1.39393e-06 + 0.999914 * (_ctx_1024t + 0.3 * jax.random.normal(jax.random.fold_in(_rk, 611), (2, 77, 256), jnp.float32))
        _validS = jnp.arange(1024)[None, :] < _lenS[:, None]
        _validS2 = jnp.arange(77)[None, :] < _lenS2[:, None]
        _causal = jnp.tril(jnp.ones((1024, 1024), dtype=bool))
        mask_Bx1x1xS2_fk0 = jnp.where(jnp.broadcast_to(_validS2[:, None, None, :], (2, 1, 1, 77)), 0.0, 1.0).astype(jnp.float32)
        mask_BxS2_bf1 = jnp.ones((2, 77), dtype=bool)
        mask_BxS2_bk0 = jnp.logical_not(jnp.broadcast_to(_validS2[:, :], (2, 77)))
        _g = jax.random.normal(jax.random.fold_in(_rk, 9001), (2, 4), jnp.float32)
        _g = jnp.sign(_g) * jnp.maximum(jnp.abs(_g), 1.0) + (_g == 0) * 1.0
        g_xattn = _g[0]
        g_ffn = _g[1]
        return (x, ctx_1024, mask_Bx1x1xS2_fk0, mask_BxS2_bf1, mask_BxS2_bk0, g_xattn, g_ffn)
    x, ctx_1024, mask_Bx1x1xS2_fk0, mask_BxS2_bf1, mask_BxS2_bk0, g_xattn, g_ffn = _rec_inputs()

    def _L0_xattn_setup():
        import jax, jax.numpy as jnp
        import numpy as np
        B, S, D, H = (2, 512, 256, 16)
        DH = D // H

        def _split_heads(x):
            b, s, _ = x.shape
            return x.reshape(b, s, H, DH).transpose(0, 2, 1, 3)
        key = jax.random.key(seed)
        ks = jax.random.split(key, 8)
        scale = 0.02
        return {'query': jax.random.normal(ks[0], (B, S, D), jnp.float32), 'key': jax.random.normal(ks[1], (B, S, D), jnp.float32), 'value': jax.random.normal(ks[2], (B, S, D), jnp.float32), 'mask': jax.random.randint(ks[3], (B, 1, 1, S), 0, 2).astype(jnp.float32), 'Wq': jax.random.normal(ks[4], (D, D), jnp.float32) * scale, 'bq': jnp.zeros((D,), jnp.float32), 'Wk': jax.random.normal(ks[5], (D, D), jnp.float32) * scale, 'bk': jnp.zeros((D,), jnp.float32), 'Wv': jax.random.normal(ks[6], (D, D), jnp.float32) * scale, 'bv': jnp.zeros((D,), jnp.float32), 'Wo': jax.random.normal(ks[7], (D, D), jnp.float32) * scale, 'bo': jnp.zeros((D,), jnp.float32)}
    _L0_xattn_all = _L0_xattn_setup()
    _L0_xattn_in = {k: v for k, v in _L0_xattn_all.items() if k in ('Wq', 'bq', 'Wk', 'bk', 'Wv', 'bv', 'Wo', 'bo')}
    del _L0_xattn_all

    def _L0_ffn_setup():
        import jax, jax.numpy as jnp
        import numpy as np
        DIM = 256
        NUM_HEAVY = 256
        N_ITERS = 50
        EPS = 1.0
        FETCH_K_RATIO = 9.0 / 8.0

        def rms_norm(x, gamma):
            norm = jnp.maximum(jnp.linalg.norm(x, axis=-1, keepdims=True), 1e-12)
            return x / norm * x.shape[-1] ** 0.5 * gamma

        def feed_forward(x, gamma, w1, b1, w2, b2):
            h = jax.nn.gelu(rms_norm(x, gamma) @ w1 + b1, approximate=False)
            return h @ w2 + b2

        def coor_descent(s, k, n_iters, eps):
            logk = jnp.log(jnp.asarray(k, dtype=s.dtype))

            def step(ab, _):
                a, b = ab
                sb = (s + b) / eps
                a = eps * (logk - jax.scipy.special.logsumexp(sb, axis=-1, keepdims=True))
                b = -jax.nn.relu(s + a)
                return ((a, b), None)
            a0 = jnp.zeros_like(s[..., :1])
            b0 = -s
            (a, b), _ = jax.lax.scan(step, (a0, b0), None, length=n_iters)
            return jnp.exp((s + a + b) / eps)
        key = jax.random.key(seed)
        ks = jax.random.split(key, 8)
        b, n, d = (4, 2048, DIM)
        dl, dh = (int(d * 0.5), d * 4)
        u = lambda k, shape, fan_in: jax.random.uniform(k, shape, jnp.float32, -1.0, 1.0) / np.sqrt(fan_in)
        return {'x': jax.random.normal(ks[0], (b, n, d), jnp.float32), 'routing_token': jax.random.normal(ks[1], (d,), jnp.float32), 'light_gamma': jnp.ones((d,), jnp.float32), 'light_w1': u(ks[2], (d, dl), d), 'light_b1': jnp.zeros((dl,), jnp.float32), 'light_w2': u(ks[3], (dl, d), dl), 'light_b2': jnp.zeros((d,), jnp.float32), 'heavy_gamma': jnp.ones((d,), jnp.float32), 'heavy_w1': u(ks[4], (d, dh), d), 'heavy_b1': jnp.zeros((dh,), jnp.float32), 'heavy_w2': u(ks[5], (dh, d), dh), 'heavy_b2': jnp.zeros((d,), jnp.float32)}
    _L0_ffn_all = _L0_ffn_setup()
    _L0_ffn_in = {k: v for k, v in _L0_ffn_all.items() if k in ('routing_token', 'light_gamma', 'light_w1', 'light_b1', 'light_w2', 'light_b2', 'heavy_gamma', 'heavy_w1', 'heavy_b1', 'heavy_w2', 'heavy_b2')}
    del _L0_ffn_all

    def _L1_xattn_setup():
        import jax, jax.numpy as jnp
        import numpy as np
        DIM = 256
        HEADS = 16
        DIM_HEAD = 64
        INNER = HEADS * DIM_HEAD
        EPS = 1e-05

        def layer_norm(x, gamma, beta):
            mu = jnp.mean(x, axis=-1, keepdims=True)
            var = jnp.var(x, axis=-1, keepdims=True)
            return (x - mu) * jax.lax.rsqrt(var + EPS) * gamma + beta
        key = jax.random.key(seed)
        ks = jax.random.split(key, 8)
        b, n, m = (8, 1024, 64)
        x = jax.random.normal(ks[0], (b, n, DIM), dtype=jnp.float32)
        latents = jax.random.normal(ks[1], (b, m, DIM), dtype=jnp.float32)
        mask = jnp.ones((b, n), dtype=bool)
        s = 0.02
        Wq = jax.random.normal(ks[2], (DIM, INNER), dtype=jnp.float32) * s
        Wkv = jax.random.normal(ks[3], (DIM, 2 * INNER), dtype=jnp.float32) * s
        Wout = jax.random.normal(ks[4], (INNER, DIM), dtype=jnp.float32) * s
        g_x = jnp.ones((DIM,), jnp.float32)
        b_x = jnp.zeros((DIM,), jnp.float32)
        g_l = jnp.ones((DIM,), jnp.float32)
        b_l = jnp.zeros((DIM,), jnp.float32)
        g_o = jnp.ones((DIM,), jnp.float32)
        b_o = jnp.zeros((DIM,), jnp.float32)
        return {'x': x, 'latents': latents, 'mask': mask, 'g_x': g_x, 'b_x': b_x, 'g_l': g_l, 'b_l': b_l, 'Wq': Wq, 'Wkv': Wkv, 'Wout': Wout, 'g_o': g_o, 'b_o': b_o}
    _L1_xattn_all = _L1_xattn_setup()
    _L1_xattn_in = {k: v for k, v in _L1_xattn_all.items() if k in ('g_x', 'b_x', 'g_l', 'b_l', 'Wq', 'Wkv', 'Wout', 'g_o', 'b_o')}
    del _L1_xattn_all

    def _L1_ffn_setup():
        import jax, jax.numpy as jnp
        import numpy as np
        B, S, D_MODEL, D_HIDDEN = (4, 512, 256, 1024)

        def act_quant(x):
            scale = 127.0 / jnp.clip(jnp.max(jnp.abs(x), axis=-1, keepdims=True), 1e-05)
            return jnp.clip(jnp.round(x * scale), -128, 127) / scale

        def weight_quant(w):
            scale = 1.0 / jnp.clip(jnp.mean(jnp.abs(w)), 1e-05)
            return jnp.clip(jnp.round(w * scale), -1, 1) / scale

        def bit_linear(x, w):
            xq = x + jax.lax.stop_gradient(act_quant(x) - x)
            wq = w + jax.lax.stop_gradient(weight_quant(w) - w)
            return jnp.einsum('bsd,hd->bsh', xq, wq)

        def depthwise_conv1d(x_bcl, w, b):
            y = jax.lax.conv_general_dilated(x_bcl, w, window_strides=(1,), padding=[(1, 1)], dimension_numbers=('NCH', 'OIH', 'NCH'), feature_group_count=x_bcl.shape[1])
            return y + b[None, :, None]
        key = jax.random.key(seed)
        ks = jax.random.split(key, 5)
        lim1 = 1.0 / np.sqrt(D_MODEL)
        lim2 = 1.0 / np.sqrt(D_HIDDEN)
        limc = 1.0 / np.sqrt(3.0)
        return {'x': jax.random.normal(ks[0], (B, S, D_MODEL), dtype=jnp.float32), 'w1': jax.random.uniform(ks[1], (D_HIDDEN, D_MODEL), jnp.float32, -lim1, lim1), 'conv_w': jax.random.uniform(ks[2], (D_HIDDEN, 1, 3), jnp.float32, -limc, limc), 'conv_b': jax.random.uniform(ks[3], (D_HIDDEN,), jnp.float32, -limc, limc), 'w2': jax.random.uniform(ks[4], (D_MODEL, D_HIDDEN), jnp.float32, -lim2, lim2)}
    _L1_ffn_all = _L1_ffn_setup()
    _L1_ffn_in = {k: v for k, v in _L1_ffn_all.items() if k in ('w1', 'conv_w', 'conv_b', 'w2')}
    del _L1_ffn_all

    def _L2_xattn_setup():
        import jax, jax.numpy as jnp
        import numpy as np
        HIDDEN = 256
        HEADS = 16
        HEAD_DIM = HIDDEN // HEADS
        key = jax.random.key(seed)
        ks = jax.random.split(key, 11)
        B, S, D = (4, 512, 256)
        s = 0.02
        return {'query': jax.random.normal(ks[0], (B, S, D), jnp.float32), 'key': jax.random.normal(ks[1], (B, S, D), jnp.float32), 'value': jax.random.normal(ks[2], (B, S, D), jnp.float32), 'Wq': jax.random.normal(ks[3], (HIDDEN, D), jnp.float32) * s, 'bq': jnp.zeros((HIDDEN,), jnp.float32), 'Wk': jax.random.normal(ks[4], (HIDDEN, D), jnp.float32) * s, 'bk': jnp.zeros((HIDDEN,), jnp.float32), 'Wv': jax.random.normal(ks[5], (HIDDEN, D), jnp.float32) * s, 'bv': jnp.zeros((HIDDEN,), jnp.float32), 'Wo': jax.random.normal(ks[6], (HIDDEN, HIDDEN), jnp.float32) * s, 'bo': jnp.zeros((HIDDEN,), jnp.float32)}
    _L2_xattn_all = _L2_xattn_setup()
    _L2_xattn_in = {k: v for k, v in _L2_xattn_all.items() if k in ('Wq', 'bq', 'Wk', 'bk', 'Wv', 'bv', 'Wo', 'bo')}
    del _L2_xattn_all

    def _L2_ffn_setup():
        import jax, jax.numpy as jnp
        import numpy as np
        NUM_EXPERTS = 8
        TOP_K = 2
        DIM = 256
        HIDDEN = 1024
        B, S = (4, 512)
        key = jax.random.key(seed)
        ks = jax.random.split(key, 6)
        scale = 0.02
        x = jax.random.normal(ks[0], (B, S, DIM), dtype=jnp.float32)
        wg = jax.random.normal(ks[1], (NUM_EXPERTS, DIM), dtype=jnp.float32) * scale
        bg = jnp.zeros((NUM_EXPERTS,), dtype=jnp.float32)
        Wgate = jax.random.normal(ks[2], (NUM_EXPERTS, HIDDEN, DIM), dtype=jnp.float32) * scale
        Wup = jax.random.normal(ks[3], (NUM_EXPERTS, HIDDEN, DIM), dtype=jnp.float32) * scale
        Wdown = jax.random.normal(ks[4], (NUM_EXPERTS, DIM, HIDDEN), dtype=jnp.float32) * scale
        return {'x': x, 'wg': wg, 'bg': bg, 'Wgate': Wgate, 'Wup': Wup, 'Wdown': Wdown}
    _L2_ffn_all = _L2_ffn_setup()
    _L2_ffn_in = {k: v for k, v in _L2_ffn_all.items() if k in ('wg', 'bg', 'Wgate', 'Wup', 'Wdown')}
    del _L2_ffn_all

    def _L3_xattn_setup():
        import jax, jax.numpy as jnp
        import numpy as np
        DIM = 256
        DIM_LATENT = 256
        DIM_HEAD = 64
        INNER = max(DIM, DIM_LATENT)
        HEADS = INNER // DIM_HEAD
        SCALE = DIM_HEAD ** (-0.5)
        LN_EPS = 1e-05
        RMS_EPS = 1e-08

        def layernorm(x, g, b):
            mu = jnp.mean(x, axis=-1, keepdims=True)
            var = jnp.mean(jnp.square(x - mu), axis=-1, keepdims=True)
            return (x - mu) * jax.lax.rsqrt(var + LN_EPS) * g + b

        def rmsnorm(x, gamma):
            n = jnp.linalg.norm(x, axis=-1, keepdims=True) * x.shape[-1] ** (-0.5)
            return x / jnp.maximum(n, RMS_EPS) * gamma
        key = jax.random.key(seed)
        ks = jax.random.split(key, 8)
        b, n, nl = (8, 512, 128)
        x = jax.random.normal(ks[0], (b, n, DIM), dtype=jnp.float32)
        latents = jax.random.normal(ks[1], (b, nl, DIM_LATENT), dtype=jnp.float32)
        mask = jax.random.randint(ks[2], (b, n), 0, 2).astype(bool)
        init = lambda k, shape, fan_in: jax.random.normal(k, shape, jnp.float32) * fan_in ** (-0.5)
        return {'x': x, 'latents': latents, 'mask': mask, 'ln_x_g': jnp.ones((DIM,), jnp.float32), 'ln_x_b': jnp.zeros((DIM,), jnp.float32), 'ln_l_g': jnp.ones((DIM_LATENT,), jnp.float32), 'ln_l_b': jnp.zeros((DIM_LATENT,), jnp.float32), 'q_gamma': jnp.ones((DIM_HEAD,), jnp.float32), 'k_gamma': jnp.ones((DIM_HEAD,), jnp.float32), 'W_q': init(ks[3], (DIM_LATENT, INNER), DIM_LATENT), 'W_kv': init(ks[4], (DIM, 2 * INNER), DIM), 'W_out': init(ks[5], (INNER, DIM_LATENT), INNER), 'b_out': jnp.zeros((DIM_LATENT,), jnp.float32)}
    _L3_xattn_all = _L3_xattn_setup()
    _L3_xattn_in = {k: v for k, v in _L3_xattn_all.items() if k in ('ln_x_g', 'ln_x_b', 'ln_l_g', 'ln_l_b', 'q_gamma', 'k_gamma', 'W_q', 'W_kv', 'W_out', 'b_out')}
    del _L3_xattn_all

    def _L3_ffn_setup():
        import jax, jax.numpy as jnp
        import numpy as np
        B, N, D, H, E = (4, 256, 256, 16, 8)
        DK = D // H
        HID = 4 * D
        EPS = 1e-05

        def _layernorm(x, w, b):
            m = jnp.mean(x, axis=-1, keepdims=True)
            v = jnp.mean(jnp.square(x - m), axis=-1, keepdims=True)
            return (x - m) * jax.lax.rsqrt(v + EPS) * w + b

        def _msa(x, w_qkv, w_proj):
            b, n, d = x.shape
            qkv = (x @ w_qkv).reshape(b, n, 3, H, DK)
            q = qkv[:, :, 0].transpose(0, 2, 1, 3)
            k = qkv[:, :, 1].transpose(0, 2, 1, 3)
            v = qkv[:, :, 2].transpose(0, 2, 1, 3)
            attn = jnp.einsum('bhnd,bhmd->bhnm', q, k) * (1.0 / np.sqrt(DK))
            attn = jax.nn.softmax(attn, axis=-1)
            y = jnp.einsum('bhnm,bhmd->bhnd', attn, v)
            y = y.transpose(0, 2, 1, 3).reshape(b, n, d)
            return y @ w_proj

        def _moe_mlp(x, gate_w, gate_b, w1, w2):
            b, n, d = x.shape
            xf = x.reshape(b * n, d)
            logits = xf @ gate_w + gate_b
            one_hot = jax.nn.one_hot(jnp.argmax(logits, axis=-1), E, dtype=xf.dtype)
            h = jax.nn.gelu(jnp.einsum('td,edh->teh', xf, w1), approximate=True)
            y = jnp.einsum('teh,ehd->ted', h, w2)
            out = jnp.einsum('te,ted->td', one_hot, y)
            return out.reshape(b, n, d)
        key = jax.random.key(seed)
        ks = jax.random.split(key, 8)
        s = 0.02
        return {'x': jax.random.normal(ks[0], (B, N, D), jnp.float32), 'ln1_w': jnp.ones((D,), jnp.float32), 'ln1_b': jnp.zeros((D,), jnp.float32), 'w_qkv': jax.random.normal(ks[1], (D, 3 * D), jnp.float32) * s, 'w_proj': jax.random.normal(ks[2], (D, D), jnp.float32) * s, 'ln2_w': jnp.ones((D,), jnp.float32), 'ln2_b': jnp.zeros((D,), jnp.float32), 'gate_w': jax.random.normal(ks[3], (D, E), jnp.float32) * s, 'gate_b': jnp.zeros((E,), jnp.float32), 'w1': jax.random.normal(ks[4], (E, D, HID), jnp.float32) * s, 'w2': jax.random.normal(ks[5], (E, HID, D), jnp.float32) * s}
    _L3_ffn_all = _L3_ffn_setup()
    _L3_ffn_in = {k: v for k, v in _L3_ffn_all.items() if k in ('ln1_w', 'ln1_b', 'w_qkv', 'w_proj', 'ln2_w', 'ln2_b', 'gate_w', 'gate_b', 'w1', 'w2')}
    del _L3_ffn_all
    return {'x': x, 'ctx_1024': ctx_1024, 'mask_Bx1x1xS2_fk0': mask_Bx1x1xS2_fk0, 'mask_BxS2_bf1': mask_BxS2_bf1, 'mask_BxS2_bk0': mask_BxS2_bk0, 'g_xattn': g_xattn, 'g_ffn': g_ffn, 'L0_xattn_Wq': _L0_xattn_in['Wq'], 'L0_xattn_bq': _L0_xattn_in['bq'], 'L0_xattn_Wk': _L0_xattn_in['Wk'], 'L0_xattn_bk': _L0_xattn_in['bk'], 'L0_xattn_Wv': _L0_xattn_in['Wv'], 'L0_xattn_bv': _L0_xattn_in['bv'], 'L0_xattn_Wo': _L0_xattn_in['Wo'], 'L0_xattn_bo': _L0_xattn_in['bo'], 'L0_ffn_routing_token': _L0_ffn_in['routing_token'], 'L0_ffn_light_gamma': _L0_ffn_in['light_gamma'], 'L0_ffn_light_w1': _L0_ffn_in['light_w1'], 'L0_ffn_light_b1': _L0_ffn_in['light_b1'], 'L0_ffn_light_w2': _L0_ffn_in['light_w2'], 'L0_ffn_light_b2': _L0_ffn_in['light_b2'], 'L0_ffn_heavy_gamma': _L0_ffn_in['heavy_gamma'], 'L0_ffn_heavy_w1': _L0_ffn_in['heavy_w1'], 'L0_ffn_heavy_b1': _L0_ffn_in['heavy_b1'], 'L0_ffn_heavy_w2': _L0_ffn_in['heavy_w2'], 'L0_ffn_heavy_b2': _L0_ffn_in['heavy_b2'], 'L1_xattn_g_x': _L1_xattn_in['g_x'], 'L1_xattn_b_x': _L1_xattn_in['b_x'], 'L1_xattn_g_l': _L1_xattn_in['g_l'], 'L1_xattn_b_l': _L1_xattn_in['b_l'], 'L1_xattn_Wq': _L1_xattn_in['Wq'], 'L1_xattn_Wkv': _L1_xattn_in['Wkv'], 'L1_xattn_Wout': _L1_xattn_in['Wout'], 'L1_xattn_g_o': _L1_xattn_in['g_o'], 'L1_xattn_b_o': _L1_xattn_in['b_o'], 'L1_ffn_w1': _L1_ffn_in['w1'], 'L1_ffn_conv_w': _L1_ffn_in['conv_w'], 'L1_ffn_conv_b': _L1_ffn_in['conv_b'], 'L1_ffn_w2': _L1_ffn_in['w2'], 'L2_xattn_Wq': _L2_xattn_in['Wq'], 'L2_xattn_bq': _L2_xattn_in['bq'], 'L2_xattn_Wk': _L2_xattn_in['Wk'], 'L2_xattn_bk': _L2_xattn_in['bk'], 'L2_xattn_Wv': _L2_xattn_in['Wv'], 'L2_xattn_bv': _L2_xattn_in['bv'], 'L2_xattn_Wo': _L2_xattn_in['Wo'], 'L2_xattn_bo': _L2_xattn_in['bo'], 'L2_ffn_wg': _L2_ffn_in['wg'], 'L2_ffn_bg': _L2_ffn_in['bg'], 'L2_ffn_Wgate': _L2_ffn_in['Wgate'], 'L2_ffn_Wup': _L2_ffn_in['Wup'], 'L2_ffn_Wdown': _L2_ffn_in['Wdown'], 'L3_xattn_ln_x_g': _L3_xattn_in['ln_x_g'], 'L3_xattn_ln_x_b': _L3_xattn_in['ln_x_b'], 'L3_xattn_ln_l_g': _L3_xattn_in['ln_l_g'], 'L3_xattn_ln_l_b': _L3_xattn_in['ln_l_b'], 'L3_xattn_q_gamma': _L3_xattn_in['q_gamma'], 'L3_xattn_k_gamma': _L3_xattn_in['k_gamma'], 'L3_xattn_W_q': _L3_xattn_in['W_q'], 'L3_xattn_W_kv': _L3_xattn_in['W_kv'], 'L3_xattn_W_out': _L3_xattn_in['W_out'], 'L3_xattn_b_out': _L3_xattn_in['b_out'], 'L3_ffn_ln1_w': _L3_ffn_in['ln1_w'], 'L3_ffn_ln1_b': _L3_ffn_in['ln1_b'], 'L3_ffn_w_qkv': _L3_ffn_in['w_qkv'], 'L3_ffn_w_proj': _L3_ffn_in['w_proj'], 'L3_ffn_ln2_w': _L3_ffn_in['ln2_w'], 'L3_ffn_ln2_b': _L3_ffn_in['ln2_b'], 'L3_ffn_gate_w': _L3_ffn_in['gate_w'], 'L3_ffn_gate_b': _L3_ffn_in['gate_b'], 'L3_ffn_w1': _L3_ffn_in['w1'], 'L3_ffn_w2': _L3_ffn_in['w2']}

def reference(x, ctx_1024, mask_Bx1x1xS2_fk0, mask_BxS2_bf1, mask_BxS2_bk0, g_xattn, g_ffn, L0_xattn_Wq, L0_xattn_bq, L0_xattn_Wk, L0_xattn_bk, L0_xattn_Wv, L0_xattn_bv, L0_xattn_Wo, L0_xattn_bo, L0_ffn_routing_token, L0_ffn_light_gamma, L0_ffn_light_w1, L0_ffn_light_b1, L0_ffn_light_w2, L0_ffn_light_b2, L0_ffn_heavy_gamma, L0_ffn_heavy_w1, L0_ffn_heavy_b1, L0_ffn_heavy_w2, L0_ffn_heavy_b2, L1_xattn_g_x, L1_xattn_b_x, L1_xattn_g_l, L1_xattn_b_l, L1_xattn_Wq, L1_xattn_Wkv, L1_xattn_Wout, L1_xattn_g_o, L1_xattn_b_o, L1_ffn_w1, L1_ffn_conv_w, L1_ffn_conv_b, L1_ffn_w2, L2_xattn_Wq, L2_xattn_bq, L2_xattn_Wk, L2_xattn_bk, L2_xattn_Wv, L2_xattn_bv, L2_xattn_Wo, L2_xattn_bo, L2_ffn_wg, L2_ffn_bg, L2_ffn_Wgate, L2_ffn_Wup, L2_ffn_Wdown, L3_xattn_ln_x_g, L3_xattn_ln_x_b, L3_xattn_ln_l_g, L3_xattn_ln_l_b, L3_xattn_q_gamma, L3_xattn_k_gamma, L3_xattn_W_q, L3_xattn_W_kv, L3_xattn_W_out, L3_xattn_b_out, L3_ffn_ln1_w, L3_ffn_ln1_b, L3_ffn_w_qkv, L3_ffn_w_proj, L3_ffn_ln2_w, L3_ffn_ln2_b, L3_ffn_gate_w, L3_ffn_gate_b, L3_ffn_w1, L3_ffn_w2):
    import jax
    import jax.numpy as jnp

    def _L0_xattn_ref(query, key, value, mask, Wq, bq, Wk, bk, Wv, bv, Wo, bo):
        import jax, jax.numpy as jnp
        import numpy as np
        B, S, D, H = (2, 512, 256, 16)
        DH = D // H

        def _split_heads(x):
            b, s, _ = x.shape
            return x.reshape(b, s, H, DH).transpose(0, 2, 1, 3)
        q = _split_heads(query @ Wq + bq)
        k = _split_heads(key @ Wk + bk)
        v = _split_heads(value @ Wv + bv)
        logits = jnp.einsum('bhqd,bhkd->bhqk', q, k) / jnp.sqrt(jnp.float32(DH))
        logits = logits + mask * -1000000000.0
        attn = jax.nn.softmax(logits, axis=-1)
        out = jnp.einsum('bhqk,bhkd->bhqd', attn, v)
        out = out.transpose(0, 2, 1, 3).reshape(query.shape[0], -1, D)
        return out @ Wo + bo

    def _L0_ffn_ref(x, routing_token, light_gamma, light_w1, light_b1, light_w2, light_b2, heavy_gamma, heavy_w1, heavy_b1, heavy_w2, heavy_b2):
        import jax, jax.numpy as jnp
        import numpy as np
        DIM = 256
        NUM_HEAVY = 256
        N_ITERS = 50
        EPS = 1.0
        FETCH_K_RATIO = 9.0 / 8.0

        def rms_norm(x, gamma):
            norm = jnp.maximum(jnp.linalg.norm(x, axis=-1, keepdims=True), 1e-12)
            return x / norm * x.shape[-1] ** 0.5 * gamma

        def feed_forward(x, gamma, w1, b1, w2, b2):
            h = jax.nn.gelu(rms_norm(x, gamma) @ w1 + b1, approximate=False)
            return h @ w2 + b2

        def coor_descent(s, k, n_iters, eps):
            logk = jnp.log(jnp.asarray(k, dtype=s.dtype))

            def step(ab, _):
                a, b = ab
                sb = (s + b) / eps
                a = eps * (logk - jax.scipy.special.logsumexp(sb, axis=-1, keepdims=True))
                b = -jax.nn.relu(s + a)
                return ((a, b), None)
            a0 = jnp.zeros_like(s[..., :1])
            b0 = -s
            (a, b), _ = jax.lax.scan(step, (a0, b0), None, length=n_iters)
            return jnp.exp((s + a + b) / eps)
        b, n, d = x.shape
        light_out = feed_forward(x, light_gamma, light_w1, light_b1, light_w2, light_b2)
        s = jnp.einsum('bnd,d->bn', x, routing_token)
        effective_k = min(NUM_HEAVY * FETCH_K_RATIO, n)
        scores = coor_descent(s, effective_k, N_ITERS, EPS)
        sel_scores, sel_idx = jax.lax.top_k(scores, NUM_HEAVY)
        sel_scores = sel_scores + jax.lax.stop_gradient(1.0 - sel_scores)
        routed = jnp.take_along_axis(x, sel_idx[..., None], axis=1)
        routed_out = feed_forward(routed, heavy_gamma, heavy_w1, heavy_b1, heavy_w2, heavy_b2)
        routed_out = routed_out * sel_scores[..., None]
        batch_idx = jnp.arange(b)[:, None]
        heavy_out = jnp.zeros_like(x).at[batch_idx, sel_idx].set(routed_out)
        return light_out + heavy_out

    def _L1_xattn_ref(x, latents, mask, g_x, b_x, g_l, b_l, Wq, Wkv, Wout, g_o, b_o):
        import jax, jax.numpy as jnp
        import numpy as np
        DIM = 256
        HEADS = 16
        DIM_HEAD = 64
        INNER = HEADS * DIM_HEAD
        EPS = 1e-05

        def layer_norm(x, gamma, beta):
            mu = jnp.mean(x, axis=-1, keepdims=True)
            var = jnp.var(x, axis=-1, keepdims=True)
            return (x - mu) * jax.lax.rsqrt(var + EPS) * gamma + beta
        scale = DIM_HEAD ** (-0.5)
        xn = layer_norm(x, g_x, b_x)
        ln = layer_norm(latents, g_l, b_l)
        b, m = (ln.shape[0], ln.shape[1])
        q = jnp.einsum('bnd,de->bne', ln, Wq)
        kv_in = jnp.concatenate([xn, ln], axis=1)
        kv = jnp.einsum('bnd,de->bne', kv_in, Wkv)
        k, v = jnp.split(kv, 2, axis=-1)

        def split_heads(t):
            return t.reshape(t.shape[0], t.shape[1], HEADS, DIM_HEAD).transpose(0, 2, 1, 3)
        q, k, v = (split_heads(q), split_heads(k), split_heads(v))
        q = q * scale
        sim = jnp.einsum('bhid,bhjd->bhij', q, k)
        full_mask = jnp.concatenate([mask, jnp.ones((b, m), dtype=bool)], axis=1)
        max_neg = -jnp.finfo(sim.dtype).max
        sim = jnp.where(full_mask[:, None, None, :], sim, max_neg)
        attn = jax.nn.softmax(sim, axis=-1)
        out = jnp.einsum('bhij,bhjd->bhid', attn, v)
        out = out.transpose(0, 2, 1, 3).reshape(b, m, INNER)
        out = jnp.einsum('bne,ed->bnd', out, Wout)
        return layer_norm(out, g_o, b_o)

    def _L1_ffn_ref(x, w1, conv_w, conv_b, w2):
        import jax, jax.numpy as jnp
        import numpy as np
        B, S, D_MODEL, D_HIDDEN = (4, 512, 256, 1024)

        def act_quant(x):
            scale = 127.0 / jnp.clip(jnp.max(jnp.abs(x), axis=-1, keepdims=True), 1e-05)
            return jnp.clip(jnp.round(x * scale), -128, 127) / scale

        def weight_quant(w):
            scale = 1.0 / jnp.clip(jnp.mean(jnp.abs(w)), 1e-05)
            return jnp.clip(jnp.round(w * scale), -1, 1) / scale

        def bit_linear(x, w):
            xq = x + jax.lax.stop_gradient(act_quant(x) - x)
            wq = w + jax.lax.stop_gradient(weight_quant(w) - w)
            return jnp.einsum('bsd,hd->bsh', xq, wq)

        def depthwise_conv1d(x_bcl, w, b):
            y = jax.lax.conv_general_dilated(x_bcl, w, window_strides=(1,), padding=[(1, 1)], dimension_numbers=('NCH', 'OIH', 'NCH'), feature_group_count=x_bcl.shape[1])
            return y + b[None, :, None]
        h = bit_linear(x, w1)
        h = depthwise_conv1d(h.transpose(0, 2, 1), conv_w, conv_b)
        h = h.transpose(0, 2, 1)
        h = jax.nn.silu(h)
        return bit_linear(h, w2)

    def _L2_xattn_ref(query, key, value, Wq, bq, Wk, bk, Wv, bv, Wo, bo):
        import jax, jax.numpy as jnp
        import numpy as np
        HIDDEN = 256
        HEADS = 16
        HEAD_DIM = HIDDEN // HEADS
        B = query.shape[0]
        scale = jnp.sqrt(jnp.asarray(HEAD_DIM, query.dtype))
        Q = query @ Wq.T + bq
        K = key @ Wk.T + bk
        V = value @ Wv.T + bv

        def split(x):
            return x.reshape(B, -1, HEADS, HEAD_DIM).transpose(0, 2, 1, 3)
        Qh, Kh, Vh = (split(Q), split(K), split(V))
        energy = jnp.einsum('bhqd,bhkd->bhqk', Qh, Kh) / scale
        attn = jax.nn.softmax(energy, axis=-1)
        x = jnp.einsum('bhqk,bhkd->bhqd', attn, Vh)
        x = x.transpose(0, 2, 1, 3).reshape(B, -1, HIDDEN)
        return x @ Wo.T + bo

    def _L2_ffn_ref(x, wg, bg, Wgate, Wup, Wdown):
        import jax, jax.numpy as jnp
        import numpy as np
        NUM_EXPERTS = 8
        TOP_K = 2
        DIM = 256
        HIDDEN = 1024
        B, S = (4, 512)
        b, s, d = x.shape
        xf = x.reshape(-1, d)
        T = xf.shape[0]
        logits = xf @ wg.T + bg
        vals, idx = jax.lax.top_k(logits, TOP_K)
        masked = jnp.full_like(logits, -jnp.inf)
        rows = jnp.arange(T)[:, None]
        masked = masked.at[rows, idx].set(vals)
        weights = jax.nn.softmax(masked, axis=-1)
        out = jnp.zeros_like(xf)
        for e in range(NUM_EXPERTS):
            g = xf @ Wgate[e].T
            u = xf @ Wup[e].T
            h = g * jax.nn.sigmoid(g) * u
            out = out + h @ Wdown[e].T * weights[:, e:e + 1]
        return out.reshape(b, s, d)

    def _L3_xattn_ref(x, latents, mask, ln_x_g, ln_x_b, ln_l_g, ln_l_b, q_gamma, k_gamma, W_q, W_kv, W_out, b_out):
        import jax, jax.numpy as jnp
        import numpy as np
        DIM = 256
        DIM_LATENT = 256
        DIM_HEAD = 64
        INNER = max(DIM, DIM_LATENT)
        HEADS = INNER // DIM_HEAD
        SCALE = DIM_HEAD ** (-0.5)
        LN_EPS = 1e-05
        RMS_EPS = 1e-08

        def layernorm(x, g, b):
            mu = jnp.mean(x, axis=-1, keepdims=True)
            var = jnp.mean(jnp.square(x - mu), axis=-1, keepdims=True)
            return (x - mu) * jax.lax.rsqrt(var + LN_EPS) * g + b

        def rmsnorm(x, gamma):
            n = jnp.linalg.norm(x, axis=-1, keepdims=True) * x.shape[-1] ** (-0.5)
            return x / jnp.maximum(n, RMS_EPS) * gamma
        b, n, _ = x.shape
        nl = latents.shape[1]
        xn = layernorm(x, ln_x_g, ln_x_b)
        ln = layernorm(latents, ln_l_g, ln_l_b)
        q = ln @ W_q
        kv = jnp.concatenate([xn @ W_kv, ln @ W_kv], axis=1)
        k, v = (kv[..., :INNER], kv[..., INNER:])
        to_heads = lambda t: t.reshape(t.shape[0], t.shape[1], HEADS, DIM_HEAD).transpose(0, 2, 1, 3)
        q, k, v = (to_heads(q), to_heads(k), to_heads(v))
        qn = rmsnorm(q, q_gamma) * SCALE
        kn = rmsnorm(k, k_gamma)
        sim = jnp.einsum('bhid,bhjd->bhij', qn, kn)
        full_mask = jnp.pad(mask, ((0, 0), (0, nl)), constant_values=True)
        neg = -jnp.finfo(sim.dtype).max
        sim = jnp.where(full_mask[:, None, None, :], sim, neg)
        attn = jax.nn.softmax(sim.astype(jnp.float32), axis=-1).astype(sim.dtype)
        out = jnp.einsum('bhij,bhjd->bhid', attn, v)
        out = out.transpose(0, 2, 1, 3).reshape(b, nl, INNER)
        return out @ W_out + b_out

    def _L3_ffn_ref(x, ln1_w, ln1_b, w_qkv, w_proj, ln2_w, ln2_b, gate_w, gate_b, w1, w2):
        import jax, jax.numpy as jnp
        import numpy as np
        B, N, D, H, E = (4, 256, 256, 16, 8)
        DK = D // H
        HID = 4 * D
        EPS = 1e-05

        def _layernorm(x, w, b):
            m = jnp.mean(x, axis=-1, keepdims=True)
            v = jnp.mean(jnp.square(x - m), axis=-1, keepdims=True)
            return (x - m) * jax.lax.rsqrt(v + EPS) * w + b

        def _msa(x, w_qkv, w_proj):
            b, n, d = x.shape
            qkv = (x @ w_qkv).reshape(b, n, 3, H, DK)
            q = qkv[:, :, 0].transpose(0, 2, 1, 3)
            k = qkv[:, :, 1].transpose(0, 2, 1, 3)
            v = qkv[:, :, 2].transpose(0, 2, 1, 3)
            attn = jnp.einsum('bhnd,bhmd->bhnm', q, k) * (1.0 / np.sqrt(DK))
            attn = jax.nn.softmax(attn, axis=-1)
            y = jnp.einsum('bhnm,bhmd->bhnd', attn, v)
            y = y.transpose(0, 2, 1, 3).reshape(b, n, d)
            return y @ w_proj

        def _moe_mlp(x, gate_w, gate_b, w1, w2):
            b, n, d = x.shape
            xf = x.reshape(b * n, d)
            logits = xf @ gate_w + gate_b
            one_hot = jax.nn.one_hot(jnp.argmax(logits, axis=-1), E, dtype=xf.dtype)
            h = jax.nn.gelu(jnp.einsum('td,edh->teh', xf, w1), approximate=True)
            y = jnp.einsum('teh,ehd->ted', h, w2)
            out = jnp.einsum('te,ted->td', one_hot, y)
            return out.reshape(b, n, d)
        x = x + _msa(_layernorm(x, ln1_w, ln1_b), w_qkv, w_proj)
        x = x + _moe_mlp(_layernorm(x, ln2_w, ln2_b), gate_w, gate_b, w1, w2)
        return x
    x = x + jnp.tanh(g_xattn[0]) * _L0_xattn_ref(_layernorm(x, axis=-1), ctx_1024, ctx_1024, mask_Bx1x1xS2_fk0, L0_xattn_Wq, L0_xattn_bq, L0_xattn_Wk, L0_xattn_bk, L0_xattn_Wv, L0_xattn_bv, L0_xattn_Wo, L0_xattn_bo)
    x = x + jnp.tanh(g_ffn[0]) * _L0_ffn_ref(_layernorm(x, axis=-1), L0_ffn_routing_token, L0_ffn_light_gamma, L0_ffn_light_w1, L0_ffn_light_b1, L0_ffn_light_w2, L0_ffn_light_b2, L0_ffn_heavy_gamma, L0_ffn_heavy_w1, L0_ffn_heavy_b1, L0_ffn_heavy_w2, L0_ffn_heavy_b2)
    x = x + jnp.tanh(g_xattn[1]) * _L1_xattn_ref(ctx_1024, _layernorm(x, axis=-1), mask_BxS2_bf1, L1_xattn_g_x, L1_xattn_b_x, L1_xattn_g_l, L1_xattn_b_l, L1_xattn_Wq, L1_xattn_Wkv, L1_xattn_Wout, L1_xattn_g_o, L1_xattn_b_o)
    x = x + jnp.tanh(g_ffn[1]) * _L1_ffn_ref(_layernorm(x, axis=-1), L1_ffn_w1, L1_ffn_conv_w, L1_ffn_conv_b, L1_ffn_w2)
    x = x + jnp.tanh(g_xattn[2]) * _L2_xattn_ref(_layernorm(x, axis=-1), ctx_1024, ctx_1024, L2_xattn_Wq, L2_xattn_bq, L2_xattn_Wk, L2_xattn_bk, L2_xattn_Wv, L2_xattn_bv, L2_xattn_Wo, L2_xattn_bo)
    x = x + jnp.tanh(g_ffn[2]) * _L2_ffn_ref(_layernorm(x, axis=-1), L2_ffn_wg, L2_ffn_bg, L2_ffn_Wgate, L2_ffn_Wup, L2_ffn_Wdown)
    x = x + jnp.tanh(g_xattn[3]) * _L3_xattn_ref(ctx_1024, _layernorm(x, axis=-1), mask_BxS2_bk0, L3_xattn_ln_x_g, L3_xattn_ln_x_b, L3_xattn_ln_l_g, L3_xattn_ln_l_b, L3_xattn_q_gamma, L3_xattn_k_gamma, L3_xattn_W_q, L3_xattn_W_kv, L3_xattn_W_out, L3_xattn_b_out)
    x = x + jnp.tanh(g_ffn[3]) * _L3_ffn_ref(_layernorm(x, axis=-1), L3_ffn_ln1_w, L3_ffn_ln1_b, L3_ffn_w_qkv, L3_ffn_w_proj, L3_ffn_ln2_w, L3_ffn_ln2_b, L3_ffn_gate_w, L3_ffn_gate_b, L3_ffn_w1, L3_ffn_w2)
    return x

_drawn_inputs = setup_inputs


def setup_inputs(seed=0):
    import zlib

    import numpy as np

    out = dict(_drawn_inputs(seed))
    spreads = {'L0_xattn_bq': (0.0, 0.8),
     'L0_xattn_bk': (0.0, 2.0),
     'L0_xattn_bv': (0.0, 0.1),
     'L0_xattn_bo': (0.0, 0.1),
     'L0_ffn_light_gamma': (1.0, 0.592),
     'L0_ffn_light_b1': (0.0, 0.1),
     'L0_ffn_light_b2': (0.0, 0.1),
     'L0_ffn_heavy_gamma': (1.0, 0.6),
     'L0_ffn_heavy_b1': (0.0, 0.378),
     'L0_ffn_heavy_b2': (0.0, 0.1),
     'L1_xattn_g_x': (1.0, 0.548),
     'L1_xattn_b_x': (0.0, 0.284),
     'L1_xattn_g_l': (1.0, 0.2),
     'L1_xattn_b_l': (0.0, 0.1),
     'L1_xattn_g_o': (1.0, 0.2),
     'L1_xattn_b_o': (0.0, 0.1),
     'L2_xattn_bq': (0.0, 0.8),
     'L2_xattn_bk': (0.0, 2.0),
     'L2_xattn_bv': (0.0, 0.411),
     'L2_xattn_bo': (0.0, 0.1),
     'L2_ffn_bg': (0.0, 0.8),
     'L3_xattn_ln_x_g': (1.0, 0.6),
     'L3_xattn_ln_x_b': (0.0, 2.0),
     'L3_xattn_ln_l_g': (1.0, 0.537),
     'L3_xattn_ln_l_b': (0.0, 0.1),
     'L3_xattn_q_gamma': (1.0, 0.6),
     'L3_xattn_k_gamma': (1.0, 0.6),
     'L3_xattn_b_out': (0.0, 0.284),
     'L3_ffn_ln1_w': (1.0, 0.6),
     'L3_ffn_ln1_b': (0.0, 2.0),
     'L3_ffn_ln2_w': (1.0, 0.6),
     'L3_ffn_ln2_b': (0.0, 0.409),
     'L3_ffn_gate_b': (0.0, 0.332)}
    factors = {'g_ffn': 28.536,
     'L0_xattn_Wq': 8.0,
     'L0_xattn_Wk': 8.0,
     'L2_xattn_Wq': 8.0,
     'L2_xattn_Wk': 8.0,
     'L2_ffn_wg': 4.811,
     'L2_ffn_Wgate': 4.143,
     'L2_ffn_Wup': 4.087,
     'L2_ffn_Wdown': 4.18}
    for name, (base, spread) in spreads.items():
        noise = np.random.default_rng([zlib.crc32(name.encode()), seed]).standard_normal(out[name].shape)
        drawn = base * np.exp(spread * noise) if base else spread * noise
        out[name] = jnp.asarray(drawn.astype(out[name].dtype))
    for name, factor in factors.items():
        out[name] = (out[name] * factor).astype(out[name].dtype)
    return out
```

```python
from contextlib import ExitStack

import concourse.bass as bass
from concourse import mybir
import numpy as np

P = 128
B, S, D = 2, 1024, 256
TOK = B * S
KD = D // P
NT = S // P
TT = TOK // P
CH = 512
NC = TOK // CH
CT = CH // P
SC = 77
F32 = mybir.dt.float32
BF16 = mybir.dt.bfloat16
U8 = mybir.dt.uint8
ALU = mybir.AluOpType
ACT = mybir.ActivationFunctionType
AX = mybir.AxisListType
EPS = 1e-5
ROUND = 1.5 * 2.0 ** 23


class Tally:

    def __init__(self, eng, sem, per_pass=0, turn=0):
        self.eng, self.sem, self.per_pass, self.n = eng, sem, per_pass, 0
        self.base = turn * per_pass if per_pass else 0

    def add(self, ins):
        self.n += 1
        ins.then_inc(self.sem, 1)

    def wait(self, passed=None):
        if passed is None:
            self.eng.wait_ge(self.sem, self.base + self.n)
        else:
            pause(self.eng, self.sem, self.base + self.n, passed)

    def close(self):
        assert self.n == self.per_pass, f"{self.n} steps, {self.per_pass} declared"


def pause(eng, sem, value, passed):
    eng.wait_ge(sem, value)
    eng.sem_inc(passed, 1)


def tiles_of(dram, first, n):
    return dram[bass.ds(first, n * P), :].rearrange("(t p) d -> p t d", p=P)


def row_tile(dram, parts):
    return dram.partition_broadcast(parts)


class Consts:

    def __init__(self, nc):
        self.nc, self.taken = nc, []

    def semaphore(self, name):
        self.taken.append(self.nc.alloc_semaphore(name))
        return self.taken[-1]

    def end_stage(self):
        self.nc.clear_and_free_semaphores(self.taken)
        self.nc.all_engine_barrier()
        self.taken = []


class Kept:
    pass


def setup(nc, ctx, io):
    c = Consts(nc)

    def sb(name, shape, dt=F32):
        return ctx.enter_context(nc.sbuf_tensor(name, shape, dt))

    c.ident = sb("ident", [P, P])
    c.ones = sb("ones", [P, P])
    c.eps = sb("eps", [P, 1])
    c.gates = sb("gates", [P, 8])
    c.sel16 = sb("sel16", [P, P])
    c.half64 = sb("half64", [P, P])
    gates_loaded = c.semaphore("gates_loaded")
    consts_step = c.semaphore("consts_step")
    gates_done = c.semaphore("gates_done")
    with nc.Block() as block:
        @block.sync
        def _(sp):
            sp.dma_start(c.gates[:, 0:4], row_tile(io["g_xattn"], P)).then_inc(gates_loaded, 16)
            sp.dma_start(c.gates[:, 4:8], row_tile(io["g_ffn"], P)).then_inc(gates_loaded, 16)

        @block.gpsimd
        def _(pool):
            step = Tally(pool, consts_step)
            step.add(pool.memset(c.ident[:], 0.0))
            step.add(pool.memset(c.ones[:], 1.0))
            step.add(pool.memset(c.eps[:], EPS))
            step.add(pool.memset(c.sel16[:], 0.0))
            step.add(pool.memset(c.half64[:], 0.0))
            step.wait()
            step.add(pool.memset(c.half64[0:64, 0:64], 1.0))
            step.add(pool.memset(c.half64[64:128, 64:128], 1.0))
            step.wait()
            step.add(pool.affine_select(out=c.ident[:], in_=c.ident[:], compare_op=ALU.not_equal, fill=1.0,
                                        base=0, pattern=[[-1, P]], channel_multiplier=1))
            for j in range(4):
                step.add(pool.affine_select(out=c.sel16[:, 32 * j:32 * j + 32], in_=c.sel16[:, 32 * j:32 * j + 32],
                                            compare_op=ALU.not_equal, fill=1.0, base=-(32 * j + 16),
                                            pattern=[[0, 32]], channel_multiplier=1))
            step.wait()

        @block.scalar
        def _(act):
            act.wait_ge(gates_loaded, 32)
            nc.scalar.activation(c.gates[:], c.gates[:], ACT.Tanh).then_inc(gates_done, 1)
            act.wait_ge(gates_done, 1)
    c.end_stage()
    return c


def norm_stats(nc, dve, step, x, stats, mv, n, parts=P):
    for t in range(n):
        step.add(nc.vector.bn_stats(stats[0:parts, t, :], x[0:parts, t, :]))
    step.wait()
    for t in range(n):
        step.add(nc.vector.bn_aggr(mv[0:parts, t, :], stats[0:parts, t, :]))


def norm_apply(nc, dve, step, out, x, mv, rstd, std, n, parts=P):
    step.add(nc.vector.reciprocal(rstd[0:parts, 0:n], std[0:parts, 0:n]))
    step.wait()
    for t in range(n):
        step.add(nc.vector.tensor_scalar(out[0:parts, t, :], x[0:parts, t, :], mv[0:parts, t, 0:1],
                                         rstd[0:parts, t:t + 1], ALU.subtract, ALU.mult))


def attention16(nc, c, name, x_in, x_out, w_qkv, w_o, gate, ctx_t=None, mask=None, ln=None, twice=False):
    G = 4
    nk = SC if ctx_t is not None else S
    n_kt = 1 if ctx_t is not None else NT
    kw = nk if n_kt == 1 else P
    M = 4 * n_kt
    n_max = 4 if n_kt == 1 else 32
    with ExitStack() as ctx:
        def sb(n, shape, dt=F32):
            return ctx.enter_context(nc.sbuf_tensor(f"{name}_{n}", shape, dt))

        def sem(n):
            return c.semaphore(f"{name}_{n}")

        scores = ctx.enter_context(nc.psum_tensor(f"{name}_scores", [P, 4, 512], F32))
        pv = ctx.enter_context(nc.psum_tensor(f"{name}_pv", [P, 2, 512], F32))
        s2 = [scores[:, 2 * i:2 * i + 2, :].rearrange("p a n -> p (a n)") for i in range(2)]
        sall = scores[:].rearrange("p a n -> p (a n)")
        pvf = pv[:].rearrange("p a n -> p (a n)")

        x = sb("x", [P, NT, D])
        xn = sb("xn", [P, NT, D])
        xn2 = sb("xn2", [P, NT, D]) if twice else xn
        stats, mv = sb("stats", [P, NT, 6]), sb("mv", [P, NT, 2])
        std, rstd = sb("std", [P, NT]), sb("rstd", [P, NT])
        xT = sb("xT", [P, KD, S])
        acc = sb("acc", [P, NT * D])
        qkv = sb("qkv", [P, w_qkv.shape[2]])
        wq = qkv[:, 0:256].rearrange("p (k m) -> p k m", k=KD)
        wk = qkv[:, 256:512].rearrange("p (k m) -> p k m", k=KD)
        wv = qkv[:, 512:768].rearrange("p (k m) -> p k m", k=KD)
        bq, bk, bv = qkv[:, 768:769], qkv[:, 769:770], qkv[:, 770:898]
        wo = sb("wo", [P, D])
        QT, QTb = sb("QT", [P, S]), sb("QTb", [P, S], BF16)
        KT, KTb = sb("KT", [P, nk]), sb("KTb", [P, nk], BF16)
        V = sb("V", [P, n_kt, P])
        mx = sb("mx", [P, P])
        neg = sb("neg", [32, P])
        probs = sb("probs", [P, 2, S])
        raw, rsum, OT = sb("raw", [P, S]), sb("rsum", [P, S]), sb("OT", [P, S])
        if ctx_t is not None:
            cT = sb("cT", [P, KD, B * SC])
        if mask is not None:
            mrow = sb("mrow", [P, B, SC])
        if ln is not None:
            lnw = sb("lnw", [P, KD, 2])

        names = ("x_loaded cst_loaded w_loaded wo_loaded var_ready std_ready xn_ready xt_psum xt_ready q_proj k_proj v_proj "
                 "q_ready k_ready v_ready qb_ready kb_ready smax_ready max_done mxt_ready neg_ready max_placed s_ready "
                 "exp_done pv_done raw_ready sums_ready ot_ready wo_done acc_added out_ready stored dve_step act_step pool_step sp_passed dve_passed")
        s = {n: sem(n) for n in names.split()}
        n_cst = (ctx_t is not None) + (ln is not None) + 4 * B * (mask is not None)
        rounds = 2 if twice else 1

        block = ctx.enter_context(nc.Block())

        @block.sync
        def _(sp):
            if ctx_t is not None:
                sp.dma_start(cT[:], ctx_t.rearrange("(k p) n -> p k n", p=P)).then_inc(s["cst_loaded"], 16)
            if ln is not None:
                sp.dma_start(lnw[:], ln).then_inc(s["cst_loaded"], 16)
            if mask is not None:
                sp.wait_ge(s["pool_step"], 1)
                for j in range(4):
                    for b in range(B):
                        sp.dma_start(mrow[32 * j + 17:32 * j + 18, b, :], mask[b:b + 1, :]).then_inc(s["cst_loaded"], 16)
            with sp.Fori(0, B) as b:
                first = sp.snap(b * S)
                sp.dma_start(x[:], tiles_of(x_in, first, NT)).then_inc(s["x_loaded"], 16)
                with sp.Fori(0, G) as g:
                    sp.wait_ge(s["neg_ready"], b * G + g + 1)
                    for j in range(4):
                        sp.dma_start(QT[32 * j + 16:32 * j + 17, :], neg[NT * j:NT * j + NT, :]).then_inc(s["max_placed"], 16)
                sp.wait_ge(s["out_ready"], b + 1)
                sp.dma_start(tiles_of(x_out, first, NT), x[:]).then_inc(s["stored"], 16)
                pause(sp, s["stored"], b * 16 + 16, s["sp_passed"])

        @block.gpsimd
        def _(pool):
            if mask is not None:
                pool.memset(mrow[:], 0.0).then_inc(s["pool_step"], 1)
            pool.dma_start(qkv[:], w_qkv[0]).then_inc(s["w_loaded"], 16)
            pool.dma_start(wo[:], w_o[0]).then_inc(s["wo_loaded"], 16)
            with pool.Fori(0, B * G - 1) as i:
                nxt = pool.snap(i + 1)
                pool.wait_ge(s["q_ready"], i + 1)
                pool.wait_ge(s["k_ready"], i + 1)
                pool.wait_ge(s["v_ready"], i + 1)
                pool.dma_start(qkv[:], w_qkv[bass.ds(nxt, 1), :, :].rearrange("o p n -> (o p) n")).then_inc(s["w_loaded"], 16)
                pool.wait_ge(s["wo_done"], i + 1)
                pool.dma_start(wo[:], w_o[bass.ds(nxt, 1), :, :].rearrange("o p n -> (o p) n")).then_inc(s["wo_loaded"], 16)

        @block.tensor
        def _(pe):
            if n_cst:
                pe.wait_ge(s["cst_loaded"], 16 * n_cst)
            with pe.Fori(0, B) as b:
                pe.wait_ge(s["xn_ready"], (b + 1) * rounds)
                pe.wait_ge(s["acc_added"], b * G + 1)
                for k in range(KD):
                    for t in range(NT):
                        last = nc.tensor.transpose(s2[k][:, t * P:(t + 1) * P], xn2[:, t, k * P:(k + 1) * P], c.ident[:])
                last.then_inc(s["xt_psum"], 1)
                with pe.Fori(0, G) as g:
                    it = pe.snap(b * G + g)
                    pe.wait_ge(s["xt_ready"], b * 2 + 2)
                    pe.wait_ge(s["w_loaded"], it * 16 + 16)
                    pe.wait_ge(s["acc_added"], it + 1)
                    for h in range(2):
                        for k in range(KD):
                            last = nc.tensor.matmul(s2[0][:, h * CH:(h + 1) * CH], wq[:, k, :], xT[:, k, h * CH:(h + 1) * CH],
                                                    start=k == 0, stop=k == KD - 1)
                    last.then_inc(s["q_proj"], 1)
                    src = xT
                    if ctx_t is None:
                        spans = [(h * CH, CH) for h in range(2)]
                    else:
                        spans = [(0, SC)]
                    def key_cols(k, lo, n):
                        return xT[:, k, lo:lo + n] if ctx_t is None else cT[:, k, bass.ds(b * SC + lo, n)]
                    for lo, n in spans:
                        for k in range(KD):
                            last = nc.tensor.matmul(s2[1][:, lo:lo + n], wk[:, k, :], key_cols(k, lo, n),
                                                    start=k == 0, stop=k == KD - 1)
                    last.then_inc(s["k_proj"], 1)
                    if ctx_t is None:
                        for t in range(NT):
                            for k in range(KD):
                                last = nc.tensor.matmul(pvf[:, t * P:(t + 1) * P], xT[:, k, t * P:(t + 1) * P], wv[:, k, :],
                                                        start=k == 0, stop=k == KD - 1)
                    else:
                        for k in range(KD):
                            last = nc.tensor.matmul(pvf[:, 0:SC], wv[:, k, :], cT[:, k, bass.ds(b * SC, SC)],
                                                    start=k == 0, stop=k == KD - 1)
                    last.then_inc(s["v_proj"], 1)
                    if ctx_t is not None:
                        pe.wait_ge(s["raw_ready"], it * 2 + 1)
                        nc.tensor.transpose(pvf[0:SC, CH:CH + P], raw[:, 0:SC], c.ident[:]).then_inc(s["v_proj"], 1)
                    pe.wait_ge(s["qb_ready"], it + 1)
                    pe.wait_ge(s["kb_ready"], it + 1)
                    for n in range(n_max):
                        if n >= 2:
                            pe.wait_ge(s["max_done"], it * n_max + n - 1)
                        if n_kt == 1:
                            r = slice(32 * n, 32 * n + 32)
                            for t in range(NT):
                                last = nc.tensor.matmul(s2[n % 2][:, t * P:t * P + SC], QTb[r, t * P:(t + 1) * P], KTb[r, :],
                                                        start=True, stop=True, tile_position=(32 * n, 0))
                        else:
                            j, t = divmod(n, NT)
                            r = slice(32 * j, 32 * j + 32)
                            for h in range(2):
                                last = nc.tensor.matmul(s2[n % 2][:, h * CH:(h + 1) * CH], QTb[r, t * P:(t + 1) * P],
                                                        KTb[r, h * CH:(h + 1) * CH], start=True, stop=True,
                                                        tile_position=(32 * j, 0))
                        last.then_inc(s["smax_ready"], 1)
                    pe.wait_ge(s["max_done"], it * n_max + n_max)
                    pe.wait_ge(s["v_ready"], it + 1)
                    nc.tensor.transpose(pvf[:, 0:P], mx[:], c.ident[:]).then_inc(s["mxt_ready"], 1)
                    pe.wait_ge(s["max_placed"], it * 64 + 64)
                    pe.wait_ge(s["k_ready"], it + 1)

                    def values(m):
                        j, kt = divmod(m, n_kt)
                        pe.wait_ge(s["exp_done"], it * M + m + 1)
                        for h in range(2):
                            last = nc.tensor.matmul(pv[32 * j:32 * j + 32, h, :], V[0:kw, kt, 32 * j:32 * j + 32],
                                                    probs[0:kw, m % 2, h * CH:(h + 1) * CH],
                                                    start=kt == 0, stop=kt == n_kt - 1, tile_position=(0, 32 * j))
                        last.then_inc(s["pv_done"], 1)

                    for m in range(M):
                        j, kt = divmod(m, n_kt)
                        r = slice(32 * j, 32 * j + 32)
                        if m >= 2:
                            pe.wait_ge(s["exp_done"], it * M + m - 1)
                        for h in range(2):
                            last = nc.tensor.matmul(s2[m % 2][0:kw, h * CH:(h + 1) * CH], KT[r, kt * P:kt * P + kw],
                                                    QT[r, h * CH:(h + 1) * CH], start=True, stop=True,
                                                    tile_position=(32 * j, 0))
                        last.then_inc(s["s_ready"], 1)
                        if m >= 1:
                            values(m - 1)
                    values(M - 1)
                    pe.wait_ge(s["raw_ready"], it * 2 + 2)
                    for h in range(2):
                        last = nc.tensor.matmul(s2[0][:, h * CH:(h + 1) * CH], c.sel16[:], raw[:, h * CH:(h + 1) * CH],
                                                start=True, stop=True)
                    last.then_inc(s["sums_ready"], 1)
                    pe.wait_ge(s["ot_ready"], it + 1)
                    pe.wait_ge(s["wo_loaded"], it * 16 + 16)
                    for t in range(NT):
                        last = nc.tensor.matmul(sall[:, t * D:(t + 1) * D], OT[:, t * P:(t + 1) * P], wo[:],
                                                start=True, stop=True)
                    last.then_inc(s["wo_done"], 1)

        @block.scalar
        def _(act):
            if ln is not None:
                act.wait_ge(s["cst_loaded"], 16 * n_cst)
            with act.Fori(0, B) as b:
                for r in range(rounds):
                    act.wait_ge(s["var_ready"], b * rounds + r + 1)
                    nc.scalar.activation(std[:], mv[:, :, 1], ACT.Sqrt, bias=c.eps[:, 0:1]).then_inc(s["std_ready"], 1)
                act.wait_ge(s["xt_psum"], b + 1)
                for k in range(KD):
                    if ln is not None:
                        ins = nc.scalar.activation(xT[:, k, :], s2[k], ACT.Identity, bias=lnw[:, k, 1:2], scale=lnw[:, k, 0:1])
                    else:
                        ins = nc.scalar.activation(xT[:, k, :], s2[k], ACT.Copy)
                    ins.then_inc(s["xt_ready"], 1)
                with act.Fori(0, G) as g:
                    it = act.snap(b * G + g)
                    if mask is None:
                        act.wait_ge(s["k_proj"], it + 1)
                        nc.scalar.activation(KT[:], s2[1][:, 0:nk], ACT.Identity, bias=bk).then_inc(s["k_ready"], 1)
                    act.wait_ge(s["k_ready"], it + 1)
                    nc.scalar.activation(KTb[:], KT[:], ACT.Copy).then_inc(s["kb_ready"], 1)
                    for m in range(M):
                        act.wait_ge(s["s_ready"], it * M + m + 1)
                        if m >= 2:
                            act.wait_ge(s["pv_done"], it * M + m - 1)
                        nc.scalar.activation(probs[0:kw, m % 2, :], s2[m % 2][0:kw, :], ACT.Exp).then_inc(s["exp_done"], 1)

        @block.vector
        def _(dve):
            dve.memset(mx[:], 0.0).then_inc(s["acc_added"], 1)
            if mask is not None:
                dve.wait_ge(s["cst_loaded"], 16 * n_cst)
            with dve.Fori(0, B) as b:
                step = Tally(dve, s["dve_step"], (1 + NT + NT + 1 + NT) + (rounds - 1) * (NT + NT + 1 + NT) - 2 * rounds, b)
                dve.wait_ge(s["x_loaded"], b * 16 + 16)
                step.add(nc.vector.memset(acc[:], 0.0))
                for r in range(rounds):
                    src, dst = ((x, xn), (xn, xn2))[r]
                    for t in range(NT):
                        step.add(nc.vector.bn_stats(stats[:, t, :], src[:, t, :]))
                    step.wait(s["dve_passed"])
                    for t in range(NT):
                        ins = nc.vector.bn_aggr(mv[:, t, :], stats[:, t, :])
                        if t < NT - 1:
                            step.add(ins)
                    ins.then_inc(s["var_ready"], 1)
                    dve.wait_ge(s["std_ready"], b * rounds + r + 1)
                    step.add(nc.vector.reciprocal(rstd[:], std[:]))
                    step.wait()
                    for t in range(NT):
                        ins = nc.vector.tensor_scalar(dst[:, t, :], src[:, t, :], mv[:, t, 0:1], rstd[:, t:t + 1],
                                                      ALU.subtract, ALU.mult)
                        if t < NT - 1:
                            step.add(ins)
                    ins.then_inc(s["xn_ready"], 1)
                    if r < rounds - 1:
                        dve.wait_ge(s["xn_ready"], b * rounds + r + 1)
                step.close()
                with dve.Fori(0, G) as g:
                    it = dve.snap(b * G + g)
                    dve.wait_ge(s["q_proj"], it + 1)
                    nc.vector.tensor_scalar(QT[:], s2[0], bq, 0.25, ALU.add, ALU.mult).then_inc(s["q_ready"], 1)
                    if mask is not None:
                        dve.wait_ge(s["k_proj"], it + 1)
                        nc.vector.scalar_tensor_tensor(KT[:], s2[1][:, 0:nk], bk, mrow[:, bass.ds(b, 1), :].rearrange("p o n -> p (o n)"),
                                                       ALU.add, ALU.add).then_inc(s["k_ready"], 1)
                    dve.wait_ge(s["q_ready"], it + 1)
                    nc.vector.tensor_copy(QTb[:], QT[:]).then_inc(s["qb_ready"], 1)
                    if ctx_t is None:
                        dve.wait_ge(s["v_proj"], it + 1)
                        nc.vector.tensor_tensor(V[:], pvf.rearrange("p (t n) -> p t n", t=NT),
                                                bv.unsqueeze(1).broadcast_to([P, NT, P]), ALU.add).then_inc(s["v_ready"], 1)
                    else:
                        dve.wait_ge(s["v_proj"], it * 2 + 1)
                        nc.vector.tensor_copy(raw[:, 0:SC], pvf[:, 0:SC]).then_inc(s["raw_ready"], 1)
                        dve.wait_ge(s["v_proj"], it * 2 + 2)
                        nc.vector.tensor_tensor(V[0:SC, 0, :], pvf[0:SC, CH:CH + P], bv[0:SC, :], ALU.add).then_inc(s["v_ready"], 1)
                    for n in range(n_max):
                        dve.wait_ge(s["smax_ready"], it * n_max + n + 1)
                        if n_kt == 1:
                            ins = nc.vector.tensor_reduce(mx[:, NT * n:NT * n + NT], s2[n % 2].rearrange("p (t n) -> p t n", t=NT)[:, :, 0:SC],
                                                          AX.X, ALU.max)
                        else:
                            ins = nc.vector.tensor_reduce(mx[:, n:n + 1], s2[n % 2], AX.X, ALU.max)
                        ins.then_inc(s["max_done"], 1)
                    dve.wait_ge(s["mxt_ready"], it + 1)
                    nc.vector.tensor_scalar(neg[:], pvf[0:32, 0:P], -1.0, None, ALU.mult).then_inc(s["neg_ready"], 1)
                    dve.wait_ge(s["pv_done"], it * M + M)
                    if ctx_t is None:
                        nc.vector.tensor_copy(raw[:, 0:CH], pvf[:, 0:CH]).then_inc(s["raw_ready"], 1)
                        nc.vector.tensor_copy(raw[:, CH:S], pvf[:, CH:S]).then_inc(s["raw_ready"], 1)
                    else:
                        nc.vector.tensor_copy(raw[:], pvf).then_inc(s["raw_ready"], 1)
                    dve.wait_ge(s["sums_ready"], it + 1)
                    nc.vector.reciprocal(rsum[:], s2[0]).then_inc(s["act_step"], 1)
                    dve.wait_ge(s["act_step"], it + 1)
                    dve.wait_ge(s["raw_ready"], it * 2 + 2)
                    nc.vector.tensor_tensor(OT[:], raw[:], rsum[:], ALU.mult).then_inc(s["ot_ready"], 1)
                    dve.wait_ge(s["wo_done"], it + 1)
                    dve.wait_ge(s["acc_added"], it + 1)
                    nc.vector.tensor_tensor(acc[:], acc[:], sall, ALU.add).then_inc(s["acc_added"], 1)
                dve.wait_ge(s["acc_added"], b * G + G + 1)
                base = xn if twice else x
                xf, bf = x[:].rearrange("p t d -> p (t d)"), base[:].rearrange("p t d -> p (t d)")
                if gate is None:
                    ins = nc.vector.tensor_tensor(xf, acc[:], bf, ALU.add)
                else:
                    ins = nc.vector.scalar_tensor_tensor(xf, acc[:], c.gates[:, gate:gate + 1], bf, ALU.mult, ALU.add)
                ins.then_inc(s["out_ready"], 1)


def attention64(nc, c, name, x_in, x_out, w_qkv, w_o, gate, ctx_in, mask, ln, rms=None, out_ln=None, out_b=None):
    HG = 4
    G = w_qkv.shape[0] // B
    n_keys = S + SC
    n_kt = NT + 1
    M = HG * n_kt
    n_max = HG * NT
    with ExitStack() as ctx:
        def sb(n, shape, dt=F32):
            return ctx.enter_context(nc.sbuf_tensor(f"{name}_{n}", shape, dt))

        def sem(n):
            return c.semaphore(f"{name}_{n}")

        scores = ctx.enter_context(nc.psum_tensor(f"{name}_scores", [P, 4, 512], F32))
        out_ps = ctx.enter_context(nc.psum_tensor(f"{name}_out_ps", [P, 4, 512], F32))
        s2 = [scores[:, 2 * i:2 * i + 2, :].rearrange("p a n -> p (a n)") for i in range(2)]
        o2 = [out_ps[:, 2 * i:2 * i + 2, :].rearrange("p a n -> p (a n)") for i in range(2)]
        sall = scores[:].rearrange("p a n -> p (a n)")

        x = sb("x", [P, NT, D])
        xn = sb("xn", [P, NT, D])
        cx = sb("cx", [SC, 1, D])
        stats, mv = sb("stats", [P, NT, 6]), sb("mv", [P, NT, 2])
        std, rstd = sb("std", [P, NT]), sb("rstd", [P, NT])
        lT = sb("lT", [P, KD, S])
        cT = sb("cT", [P, KD, SC])
        lnw = sb("lnw", [P, KD, 4])
        acc = sb("acc", [P, NT, D])
        accf = acc[:].rearrange("p t d -> p (t d)")
        qkv = sb("qkv", [P, 3, KD, D])
        wo = sb("wo", [P, 2, D])
        Q = [sb(f"Q{h}", [66, S]) for h in range(HG)]
        K = [sb(f"K{h}", [66, n_keys]) for h in range(HG)]
        Qb = [sb(f"Qb{h}", [65, S], BF16) for h in range(HG)]
        Kb = [sb(f"Kb{h}", [65, n_keys], BF16) for h in range(HG)]
        V = sb("V", [P, n_kt, HG, P])
        mx, mxc = sb("mx", [P, P]), sb("mxc", [P, P])
        neg = sb("neg", [HG * NT, P])
        probs = sb("probs", [P, 2, S])
        rsum = sb("rsum", [P, S])
        OT = [sb(f"OT{i}", [P, S]) for i in range(2)]
        mask_in = sb("mask_in", [1, SC], U8)
        mrow = sb("mrow", [1, n_keys])
        if rms is not None:
            gam = sb("gam", [P, 2])
            sq = sb("sq", [P, S])
        if out_ln is not None:
            og, ob = sb("og", [P, D]), sb("ob", [P, D])
        if out_b is not None:
            ob = sb("ob", [P, D])

        names = ("x_loaded c_loaded cst_loaded mask_loaded mask_placed w_loaded wo_loaded var_ready std_ready xn_ready "
                 "xt_psum xt_ready proj evacuated qb_ready kb_ready sq_ready sumsq norm_ready root_ready v_ready "
                 "smax_ready max_done mxt_ready neg_ready max_placed s_ready exp_done pv_done head_ready wo_done "
                 "acc_added out_ready stored dve_step rec_done sp_passed dve_passed act_passed pool_passed pool_step mrow_ready "
                 "dve_tail tail_var tail_std")
        s = {n: sem(n) for n in names.split()}
        n_cst = 1 + (rms is not None) + 2 * (out_ln is not None) + (out_b is not None)
        n_proj = 5

        block = ctx.enter_context(nc.Block())

        @block.sync
        def _(sp):
            sp.dma_start(lnw[:], ln).then_inc(s["cst_loaded"], 16)
            if rms is not None:
                sp.dma_start(gam[:], rms).then_inc(s["cst_loaded"], 16)
            if out_ln is not None:
                sp.dma_start(og[:], row_tile(out_ln[0], P)).then_inc(s["cst_loaded"], 16)
                sp.dma_start(ob[:], row_tile(out_ln[1], P)).then_inc(s["cst_loaded"], 16)
            if out_b is not None:
                sp.dma_start(ob[:], row_tile(out_b, P)).then_inc(s["cst_loaded"], 16)
            sp.wait_ge(s["pool_step"], 2 + 2 * HG + 1)
            with sp.Fori(0, B) as b:
                first = sp.snap(b * S)
                first_c = sp.snap(b * SC)
                sp.dma_start(x[:], tiles_of(x_in, first, NT)).then_inc(s["x_loaded"], 16)
                sp.dma_start(cx[:, 0, :], ctx_in[bass.ds(first_c, SC), :]).then_inc(s["c_loaded"], 16)
                sp.dma_start(mask_in[:], mask[bass.ds(b, 1), :]).then_inc(s["mask_loaded"], 16)
                sp.wait_ge(s["mrow_ready"], b + 1)
                for h in range(HG):
                    sp.dma_start(K[h][64:65, :], mrow[:]).then_inc(s["mask_placed"], 16)
                with sp.Fori(0, G) as g:
                    sp.wait_ge(s["neg_ready"], b * G + g + 1)
                    for h in range(HG):
                        sp.dma_start(Q[h][65:66, :], neg[NT * h:NT * h + NT, :]).then_inc(s["max_placed"], 16)
                sp.wait_ge(s["out_ready"], b + 1)
                sp.dma_start(tiles_of(x_out, first, NT), x[:]).then_inc(s["stored"], 16)
                pause(sp, s["stored"], b * 16 + 16, s["sp_passed"])

        @block.gpsimd
        def _(pool):
            pool.dma_start(qkv[:], w_qkv[0]).then_inc(s["w_loaded"], 16)
            pool.dma_start(wo[:], w_o[0]).then_inc(s["wo_loaded"], 16)
            step = Tally(pool, s["pool_step"])
            step.add(pool.memset(V[:], 1.0))
            step.add(pool.memset(mrow[:], 0.0))
            step.wait()
            for h in range(HG):
                step.add(pool.memset(Q[h][64:66, :], -1e30))
                step.add(pool.memset(K[h][64:66, :], 1.0))
            step.wait()
            step.add(pool.memset(mxc[:], 0.0))
            if B * G > 1:
                with pool.Fori(0, B * G - 1) as i:
                    nxt = pool.snap(i + 1)
                    pool.wait_ge(s["proj"], i * n_proj + n_proj)
                    pool.dma_start(qkv[:], w_qkv[bass.ds(nxt, 1)].rearrange("o p a k d -> (o p) a k d")).then_inc(s["w_loaded"], 16)
                    pool.wait_ge(s["wo_done"], i + 1)
                    pool.dma_start(wo[:], w_o[bass.ds(nxt, 1)].rearrange("o p k d -> (o p) k d")).then_inc(s["wo_loaded"], 16)

        @block.tensor
        def _(pe):
            with pe.Fori(0, B) as b:
                pe.wait_ge(s["xn_ready"], b * 3 + 3)
                pe.wait_ge(s["acc_added"], b * G + 1)
                for k in range(KD):
                    for t in range(NT):
                        last = nc.tensor.transpose(s2[k][:, t * P:(t + 1) * P], xn[:, t, k * P:(k + 1) * P], c.ident[:])
                    last = nc.tensor.transpose(out_ps[:, k, 0:SC], cx[:, 0, k * P:(k + 1) * P], c.ident[0:SC, 0:SC])
                last.then_inc(s["xt_psum"], 1)
                with pe.Fori(0, G) as g:
                    it = pe.snap(b * G + g)
                    ev = it * 5
                    pe.wait_ge(s["xt_ready"], b * 4 + 4)
                    pe.wait_ge(s["w_loaded"], it * 16 + 16)
                    pe.wait_ge(s["acc_added"], it + 1)
                    for i in range(2):
                        for hp in range(2):
                            n = 2 * i + hp
                            if i == 1:
                                pe.wait_ge(s["evacuated"], ev + hp + 1)
                            for h in range(2):
                                for k in range(KD):
                                    last = nc.tensor.matmul(s2[hp][:, h * CH:(h + 1) * CH], qkv[:, i, k, hp * P:(hp + 1) * P],
                                                            lT[:, k, h * CH:(h + 1) * CH], start=k == 0, stop=k == KD - 1)
                            if i == 1:
                                for k in range(KD):
                                    last = nc.tensor.matmul(out_ps[:, 2 + hp, 0:SC], qkv[:, i, k, hp * P:(hp + 1) * P],
                                                            cT[:, k, :], start=k == 0, stop=k == KD - 1)
                            last.then_inc(s["proj"], 1)
                            if rms is not None:
                                pe.wait_ge(s["sq_ready"], it * 6 + (n + 1 if i == 0 else 2 * hp + 3))
                                if n >= 1:
                                    pe.wait_ge(s["root_ready"], it * 6 + (n if n <= 2 else 4))
                                for h in range(2):
                                    last = nc.tensor.matmul(o2[0][:, h * CH:(h + 1) * CH], c.half64[:], sq[:, h * CH:(h + 1) * CH],
                                                            start=True, stop=True)
                                last.then_inc(s["sumsq"], 1)
                                if i == 1:
                                    pe.wait_ge(s["sq_ready"], it * 6 + 2 * hp + 4)
                                    pe.wait_ge(s["root_ready"], it * 6 + 2 * hp + 3)
                                    nc.tensor.matmul(o2[0][:, 0:SC], c.half64[:], sq[:, 0:SC],
                                                     start=True, stop=True).then_inc(s["sumsq"], 1)
                    pe.wait_ge(s["evacuated"], ev + 4)
                    for t in range(NT):
                        for k in range(KD):
                            last = nc.tensor.matmul(sall[:, t * D:(t + 1) * D], lT[:, k, t * P:(t + 1) * P], qkv[:, 2, k, :],
                                                    start=k == 0, stop=k == KD - 1)
                    for k in range(KD):
                        last = nc.tensor.matmul(out_ps[0:SC, 2, 0:D], cT[:, k, :], qkv[:, 2, k, :], start=k == 0, stop=k == KD - 1)
                    last.then_inc(s["proj"], 1)
                    pe.wait_ge(s["evacuated"], ev + 5)
                    pe.wait_ge(s["qb_ready"], it * HG + HG)
                    pe.wait_ge(s["kb_ready"], it * HG + HG)
                    for n in range(n_max):
                        h, t = divmod(n, NT)
                        if n >= 2:
                            pe.wait_ge(s["max_done"], it * n_max + n - 1)
                        for j in range(2):
                            nc.tensor.matmul(s2[n % 2][:, j * CH:(j + 1) * CH], Qb[h][:, t * P:(t + 1) * P],
                                             Kb[h][:, j * CH:(j + 1) * CH], start=True, stop=True)
                        nc.tensor.matmul(out_ps[:, n % 2, 0:SC], Qb[h][:, t * P:(t + 1) * P], Kb[h][:, S:n_keys],
                                         start=True, stop=True).then_inc(s["smax_ready"], 1)
                    pe.wait_ge(s["rec_done"], it * (HG + 1) + 1)
                    nc.tensor.transpose(out_ps[:, 2, 0:P], mx[:], c.ident[:]).then_inc(s["mxt_ready"], 1)
                    pe.wait_ge(s["max_placed"], it * 16 * HG + 16 * HG)
                    pe.wait_ge(s["mask_placed"], b * 16 * HG + 16 * HG)

                    def values(m):
                        h, kt = divmod(m, n_kt)
                        kw = P if kt < NT else SC
                        if kt == 0 and h >= 2:
                            pe.wait_ge(s["head_ready"], it * HG + h - 1)
                        pe.wait_ge(s["exp_done"], it * M + m + 1)
                        for j in range(2):
                            last = nc.tensor.matmul(o2[h % 2][:, j * CH:(j + 1) * CH], V[0:kw, kt, h, :],
                                                    probs[0:kw, m % 2, j * CH:(j + 1) * CH], start=kt == 0, stop=kt == n_kt - 1)
                        last.then_inc(s["pv_done"], 1)

                    for m in range(M):
                        h, kt = divmod(m, n_kt)
                        kw = P if kt < NT else SC
                        if m >= 2:
                            pe.wait_ge(s["exp_done"], it * M + m - 1)
                        for j in range(2):
                            last = nc.tensor.matmul(s2[m % 2][0:kw, j * CH:(j + 1) * CH], K[h][:, kt * P:kt * P + kw],
                                                    Q[h][:, j * CH:(j + 1) * CH], start=True, stop=True)
                        last.then_inc(s["s_ready"], 1)
                        if m >= 1:
                            values(m - 1)
                    values(M - 1)
                    pe.wait_ge(s["head_ready"], it * HG + HG)
                    pe.wait_ge(s["wo_loaded"], it * 16 + 16)
                    for t in range(NT):
                        for k in range(2):
                            last = nc.tensor.matmul(sall[:, t * D:(t + 1) * D], OT[k][:, t * P:(t + 1) * P], wo[:, k, :],
                                                    start=k == 0, stop=k == 1)
                    last.then_inc(s["wo_done"], 1)

        @block.scalar
        def _(act):
            act.wait_ge(s["cst_loaded"], 16 * n_cst)
            act.wait_ge(s["pool_step"], 2 + 2 * HG)
            with act.Fori(0, B) as b:
                act.wait_ge(s["var_ready"], b * 3 + 1)
                nc.scalar.activation(std[0:SC, 0:1], mv[0:SC, 0:1, 1], ACT.Sqrt, bias=c.eps[0:SC, 0:1]).then_inc(s["std_ready"], 1)
                for r in range(2):
                    act.wait_ge(s["var_ready"], b * 3 + 2 + r)
                    nc.scalar.activation(std[:], mv[:, :, 1], ACT.Sqrt, bias=c.eps[:, 0:1]).then_inc(s["std_ready"], 1)
                act.wait_ge(s["xt_psum"], b + 1)
                for k in range(KD):
                    nc.scalar.activation(lT[:, k, :], s2[k], ACT.Identity, bias=lnw[:, k, 1:2], scale=lnw[:, k, 0:1]).then_inc(s["xt_ready"], 1)
                    nc.scalar.activation(cT[:, k, :], out_ps[:, k, 0:SC], ACT.Identity, bias=lnw[:, k, 3:4],
                                         scale=lnw[:, k, 2:3]).then_inc(s["xt_ready"], 1)
                with act.Fori(0, G) as g:
                    it = act.snap(b * G + g)
                    for n in range(4):
                        i, hp = divmod(n, 2)
                        dst = (Q, K)[i]
                        act.wait_ge(s["proj"], it * n_proj + n + 1)
                        if rms is None:
                            for e in range(2):
                                r = slice(64 * e, 64 * e + 64)
                                ins = nc.scalar.activation(dst[2 * hp + e][0:64, 0:S], s2[hp][r, :], ACT.Copy, scale=0.125 if i == 0 else 1.0)
                                if i == 1:
                                    ins = nc.scalar.activation(dst[2 * hp + e][0:64, S:n_keys], out_ps[r, 2 + hp, 0:SC], ACT.Copy)
                            ins.then_inc(s["evacuated"], 1)
                        else:
                            first = n + 1 if i == 0 else 2 * hp + 3
                            if n >= 1:
                                act.wait_ge(s["sumsq"], it * 6 + first - 1)
                            nc.scalar.activation(sq[:], s2[hp], ACT.Square).then_inc(s["sq_ready"], 1)
                            act.wait_ge(s["sumsq"], it * 6 + first)
                            if n >= 1:
                                act.wait_ge(s["norm_ready"], it * 6 + first - 1)
                            nc.scalar.activation(rsum[:], o2[0], ACT.Sqrt).then_inc(s["root_ready"], 1)
                            if i == 1:
                                nc.scalar.activation(sq[:, 0:SC], out_ps[:, 2 + hp, 0:SC], ACT.Square).then_inc(s["sq_ready"], 1)
                                act.wait_ge(s["sumsq"], it * 6 + first + 1)
                                act.wait_ge(s["norm_ready"], it * 6 + first)
                                nc.scalar.activation(rsum[:, 0:SC], o2[0][:, 0:SC], ACT.Sqrt).then_inc(s["root_ready"], 1)
                    act.wait_ge(s["proj"], it * n_proj + 5)
                    v5 = V[:].rearrange("p t (a e) n -> p t a e n", e=2)
                    p4 = sall.rearrange("p (t a e n) -> p t a e n", t=NT, a=2, e=2)
                    c4 = out_ps[0:SC, 2, 0:D].rearrange("p (a e n) -> p a e n", a=2, e=2)
                    for e in range(2):
                        cols = slice(64 * e, 64 * e + 64)
                        nc.scalar.activation(v5[0:SC, NT, :, e, cols], c4[:, :, e, :], ACT.Copy)
                        ins = nc.scalar.activation(v5[:, 0:NT, :, e, cols], p4[:, :, :, e, :], ACT.Copy)
                    ins.then_inc(s["evacuated" if rms is None else "v_ready"], 1)
                    for h in range(HG):
                        act.wait_ge(s["evacuated"], it * 5 + 3 + h // 2)
                        if h == 0:
                            act.wait_ge(s["mask_placed"], b * 16 * HG + 16 * HG)
                        nc.scalar.activation(Kb[h][:], K[h][0:65, :], ACT.Copy).then_inc(s["kb_ready"], 1)
                    for m in range(M):
                        kw = P if m % n_kt < NT else SC
                        act.wait_ge(s["s_ready"], it * M + m + 1)
                        if m >= 2:
                            act.wait_ge(s["pv_done"], it * M + m - 1)
                        nc.scalar.activation(probs[0:kw, m % 2, :], s2[m % 2][0:kw, :], ACT.Exp).then_inc(s["exp_done"], 1)
                if out_ln is not None:
                    act.wait_ge(s["tail_var"], b + 1)
                    nc.scalar.activation(std[:], mv[:, :, 1], ACT.Sqrt, bias=c.eps[:, 0:1]).then_inc(s["tail_std"], 1)

        @block.vector
        def _(dve):
            dve.memset(mx[:], 0.0).then_inc(s["acc_added"], 1)
            dve.wait_ge(s["cst_loaded"], 16 * n_cst)
            dve.wait_ge(s["pool_step"], 2 + 2 * HG + 1)
            with dve.Fori(0, B) as b:
                def norm(src, dst, n, parts, r, step):
                    for t in range(n):
                        step.add(nc.vector.bn_stats(stats[0:parts, t, :], src[0:parts, t, :]))
                    step.wait(s["dve_passed"])
                    for t in range(n):
                        ins = nc.vector.bn_aggr(mv[0:parts, t, :], stats[0:parts, t, :])
                        if t < n - 1:
                            step.add(ins)
                    ins.then_inc(s["var_ready"], 1)
                    dve.wait_ge(s["std_ready"], b * 3 + r + 1)
                    step.add(nc.vector.reciprocal(rstd[0:parts, 0:n], std[0:parts, 0:n]))
                    step.wait()
                    for t in range(n):
                        ins = nc.vector.tensor_scalar(dst[0:parts, t, :], src[0:parts, t, :], mv[0:parts, t, 0:1],
                                                      rstd[0:parts, t:t + 1], ALU.subtract, ALU.mult)
                        if t < n - 1:
                            step.add(ins)
                    ins.then_inc(s["xn_ready"], 1)
                    if r == 1:
                        dve.wait_ge(s["xn_ready"], b * 3 + r + 1)

                per = 1 + 2 + 2 * (3 * NT - 1)
                step = Tally(dve, s["dve_step"], per, b)
                dve.wait_ge(s["mask_loaded"], b * 16 + 16)
                nc.vector.tensor_scalar(mrow[:, S:n_keys], mask_in[:], -1.0, 1.0, ALU.mult, ALU.add).then_inc(s["mrow_ready"], 1)
                dve.wait_ge(s["x_loaded"], b * 16 + 16)
                step.add(nc.vector.memset(accf, 0.0))
                dve.wait_ge(s["c_loaded"], b * 16 + 16)
                norm(cx, cx, 1, SC, 0, step)
                norm(x, xn, NT, P, 1, step)
                norm(xn, xn, NT, P, 2, step)
                step.close()
                with dve.Fori(0, G) as g:
                    it = dve.snap(b * G + g)
                    if rms is not None:
                        turn = Tally(dve, s["dve_tail"], 12, it)
                        for n in range(4):
                            i, hp = divmod(n, 2)
                            first = n + 1 if i == 0 else 2 * hp + 3
                            parts = [(0, S, s2[hp])] if i == 0 else [(0, S, s2[hp]), (S, SC, out_ps[:, 2 + hp, 0:SC])]
                            for j, (lo, w, ps) in enumerate(parts):
                                dve.wait_ge(s["root_ready"], it * 6 + first + j)
                                turn.add(nc.vector.tensor_scalar(rsum[:, 0:w], rsum[:, 0:w], 0.125 if i else 1.0, 1e-8 if i else 8e-8,
                                                                 ALU.mult, ALU.max))
                                turn.wait()
                                turn.add(nc.vector.reciprocal(rsum[:, 0:w], rsum[:, 0:w]))
                                turn.wait()
                                for e in range(2):
                                    r = slice(64 * e, 64 * e + 64)
                                    ins = nc.vector.scalar_tensor_tensor((Q, K)[i][2 * hp + e][0:64, lo:lo + w], ps[r, :], gam[r, i:i + 1],
                                                                         rsum[r, 0:w], ALU.mult, ALU.mult)
                                ins.then_inc(s["norm_ready"], 1)
                            dve.wait_ge(s["norm_ready"], it * 6 + first + len(parts) - 1)
                            dve.sem_inc(s["evacuated"], 1)
                        turn.close()
                        pause(dve, s["v_ready"], it + 1, s["evacuated"])
                    for h in range(HG):
                        dve.wait_ge(s["evacuated"], it * 5 + 1 + h // 2)
                        nc.vector.tensor_copy(Qb[h][:], Q[h][0:65, :]).then_inc(s["qb_ready"], 1)
                    for n in range(n_max):
                        dve.wait_ge(s["smax_ready"], it * n_max + n + 1)
                        nc.vector.tensor_reduce(mxc[:, n:n + 1], out_ps[:, n % 2, 0:SC], AX.X, ALU.max)
                        nc.vector.tensor_reduce(mx[:, n:n + 1], s2[n % 2], AX.X, ALU.max).then_inc(s["max_done"], 1)
                        if n == n_max - 1:
                            dve.wait_ge(s["max_done"], it * n_max + n + 1)
                    nc.vector.tensor_tensor(mx[:, 0:n_max], mx[:, 0:n_max], mxc[:, 0:n_max], ALU.max).then_inc(s["rec_done"], 1)
                    dve.wait_ge(s["mxt_ready"], it + 1)
                    nc.vector.tensor_scalar(neg[:], out_ps[0:n_max, 2, 0:P], -1.0, None, ALU.mult).then_inc(s["neg_ready"], 1)
                    for h in range(HG):
                        out_r, sum_r = slice(64 * (h % 2), 64 * (h % 2) + 64), slice(64 - 64 * (h % 2), 128 - 64 * (h % 2))
                        dve.wait_ge(s["pv_done"], it * M + n_kt * (h + 1))
                        nc.vector.reciprocal(rsum[out_r, :], o2[h % 2][sum_r, :]).then_inc(s["rec_done"], 1)
                        dve.wait_ge(s["rec_done"], it * (HG + 1) + h + 2)
                        nc.vector.tensor_tensor(OT[h // 2][out_r, :], o2[h % 2][out_r, :], rsum[out_r, :], ALU.mult).then_inc(s["head_ready"], 1)
                    dve.wait_ge(s["wo_done"], it + 1)
                    dve.wait_ge(s["acc_added"], it + 1)
                    nc.vector.tensor_tensor(accf, accf, sall, ALU.add).then_inc(s["acc_added"], 1)
                gate_col = c.gates[:, gate:gate + 1]
                dve.wait_ge(s["acc_added"], b * G + G + 1)
                tail = Tally(dve, s["root_ready"] if rms is None else s["tail_var"], (5 * NT) if out_ln is not None else NT, b)
                if out_ln is not None:
                    for t in range(NT):
                        tail.add(nc.vector.bn_stats(stats[:, t, :], acc[:, t, :]))
                    tail.wait(s["dve_passed"])
                    for t in range(NT):
                        ins = nc.vector.bn_aggr(mv[:, t, :], stats[:, t, :])
                        if t < NT - 1:
                            tail.add(ins)
                    ins.then_inc(s["tail_var"], 1)
                    dve.wait_ge(s["tail_std"], b + 1)
                    tail.add(nc.vector.reciprocal(rstd[:], std[:]))
                    tail.wait()
                    for t in range(NT):
                        tail.add(nc.vector.tensor_scalar(acc[:, t, :], acc[:, t, :], mv[:, t, 0:1], rstd[:, t:t + 1],
                                                         ALU.subtract, ALU.mult))
                    tail.wait()
                    for t in range(NT):
                        tail.add(nc.vector.tensor_tensor(acc[:, t, :], acc[:, t, :], og[:], ALU.mult))
                    tail.wait()
                for t in range(NT):
                    tail.add(nc.vector.tensor_tensor(acc[:, t, :], acc[:, t, :], ob[:], ALU.add))
                tail.wait()
                tail.close()
                nc.vector.scalar_tensor_tensor(x[:].rearrange("p t d -> p (t d)"), accf, gate_col,
                                               x[:].rearrange("p t d -> p (t d)"), ALU.mult, ALU.add).then_inc(s["out_ready"], 1)


def normed(nc, ctx, c, name, x_in, mode="plain", ln=None, outs=(), token=None):
    keep = Kept()

    def sb(n, shape, dt=F32):
        return ctx.enter_context(nc.sbuf_tensor(f"{name}_{n}", shape, dt))

    keep.x = x = sb("x", [P, TT, D])
    with ExitStack() as inner:
        def tmp(n, shape, dt=F32):
            return inner.enter_context(nc.sbuf_tensor(f"{name}_{n}", shape, dt))

        def sem(n):
            return c.semaphore(f"{name}_{n}")

        if mode == "rms":
            keep.route = sb("route", [P, TT])
        if mode == "quant":
            keep.step_size = sb("step_size", [P, TT])
        xn = tmp("xn", [P, TT, D])
        work = tmp("work", [P, CT, D])
        stats, mv = tmp("stats", [P, TT, 6]), tmp("mv", [P, TT, 2])
        std, rstd = tmp("std", [P, TT]), tmp("rstd", [P, TT])
        size, scale = tmp("size", [P, TT]), tmp("scale", [P, TT])
        if token is not None:
            tok = tmp("tok", [P, D])
        if ln is not None:
            lnw = tmp("lnw", list(ln.shape))
        turned = inner.enter_context(nc.psum_tensor(f"{name}_turned", [P, NC, KD, 512], F32))
        s = {n: sem(n) for n in ("cst_loaded var_ready std_ready sq_ready len_ready xn_ready turned_ready "
                                 "step evacuated").split()}
        x_loaded = [sem(f"x_loaded{n}") for n in range(NC)]
        n_cst = (token is not None) + (ln is not None)
        block = inner.enter_context(nc.Block())

        @block.sync
        def _(sp):
            for n in range(NC):
                sp.dma_start(x[:, n * CT:(n + 1) * CT, :], tiles_of(x_in, n * CH, CT)).then_inc(x_loaded[n], 16)
                if n == 0:
                    if token is not None:
                        sp.dma_start(tok[:], row_tile(token, P)).then_inc(s["cst_loaded"], 16)
                    if ln is not None:
                        sp.dma_start(lnw[:], ln).then_inc(s["cst_loaded"], 16)

        @block.vector
        def _(dve):
            step = Tally(dve, s["step"])
            for n in range(NC):
                ts = range(n * CT, (n + 1) * CT)
                cols = slice(n * CT, (n + 1) * CT)
                dve.wait_ge(x_loaded[n], 16)
                for t in ts:
                    step.add(nc.vector.bn_stats(stats[:, t, :], x[:, t, :]))
                step.wait()
                for t in ts:
                    ins = nc.vector.bn_aggr(mv[:, t, :], stats[:, t, :])
                ins.then_inc(s["var_ready"], 1)
                dve.wait_ge(s["std_ready"], n + 1)
                step.add(nc.vector.reciprocal(rstd[:, cols], std[:, cols]))
                step.wait()
                for t in ts:
                    ins = nc.vector.tensor_scalar(xn[:, t, :], x[:, t, :], mv[:, t, 0:1], rstd[:, t:t + 1],
                                                  ALU.subtract, ALU.mult)
                    if t < ts[-1] or mode != "plain":
                        step.add(ins)
                if mode == "plain":
                    ins.then_inc(s["xn_ready"], 1)
                    continue
                step.wait()
                if mode == "rms":
                    if n == 0:
                        dve.wait_ge(s["cst_loaded"], 16 * n_cst)
                    for t in ts:
                        step.add(nc.vector.tensor_tensor_reduce(work[:, t % CT, :], xn[:, t, :], tok[:], 1.0, 0.0,
                                                                ALU.mult, ALU.add, keep.route[:, t:t + 1]))
                    step.wait()
                    for t in ts:
                        ins = nc.vector.tensor_tensor_reduce(work[:, t % CT, :], xn[:, t, :], xn[:, t, :], 1.0, 0.0,
                                                             ALU.mult, ALU.add, size[:, t:t + 1])
                    ins.then_inc(s["sq_ready"], 1)
                    dve.wait_ge(s["len_ready"], n + 1)
                    step.add(nc.vector.tensor_scalar(scale[:, cols], scale[:, cols], 1e-12, None, ALU.max))
                    step.wait()
                    step.add(nc.vector.reciprocal(scale[:, cols], scale[:, cols]))
                    step.wait()
                    for t in ts:
                        ins = nc.vector.tensor_scalar(xn[:, t, :], xn[:, t, :], scale[:, t:t + 1], float(D) ** 0.5,
                                                      ALU.mult, ALU.mult)
                    ins.then_inc(s["xn_ready"], 1)
                else:
                    step.add(nc.vector.tensor_reduce(size[:, cols], xn[:, cols, :], AX.X, ALU.max, apply_absolute_value=True))
                    step.wait()
                    step.add(nc.vector.tensor_scalar(size[:, cols], size[:, cols], 1e-5, None, ALU.max))
                    step.wait()
                    step.add(nc.vector.tensor_scalar(keep.step_size[:, cols], size[:, cols], 1.0 / 127.0, None, ALU.mult))
                    step.add(nc.vector.reciprocal(scale[:, cols], size[:, cols]))
                    step.wait()
                    step.add(nc.vector.tensor_scalar(scale[:, cols], scale[:, cols], 127.0, None, ALU.mult))
                    step.wait()
                    for t in ts:
                        step.add(nc.vector.tensor_scalar(xn[:, t, :], xn[:, t, :], scale[:, t:t + 1], ROUND, ALU.mult, ALU.add))
                    step.wait()
                    step.add(nc.vector.tensor_scalar(xn[:, cols, :], xn[:, cols, :], -ROUND, -128.0, ALU.add, ALU.max))
                    step.wait()
                    nc.vector.tensor_scalar(xn[:, cols, :], xn[:, cols, :], 127.0, None, ALU.min).then_inc(s["xn_ready"], 1)

        @block.tensor
        def _(pe):
            for n in range(NC):
                pe.wait_ge(s["xn_ready"], n + 1)
                for k in range(KD):
                    for t in range(CT):
                        last = nc.tensor.transpose(turned[:, n, k, t * P:(t + 1) * P], xn[:, n * CT + t, k * P:(k + 1) * P], c.ident[:])
                last.then_inc(s["turned_ready"], 1)

        @block.scalar
        def _(act):
            if n_cst:
                act.wait_ge(s["cst_loaded"], 16 * n_cst)

            def root(n):
                cols = slice(n * CT, (n + 1) * CT)
                act.wait_ge(s["var_ready"], n + 1)
                nc.scalar.activation(std[:, cols], mv[:, cols, 1], ACT.Sqrt, bias=c.eps[:, 0:1]).then_inc(s["std_ready"], 1)
                if mode == "rms":
                    act.wait_ge(s["sq_ready"], n + 1)
                    nc.scalar.activation(scale[:, cols], size[:, cols], ACT.Sqrt).then_inc(s["len_ready"], 1)

            root(0)
            for n in range(NC):
                if n + 1 < NC:
                    root(n + 1)
                act.wait_ge(s["turned_ready"], n + 1)
                for i, (dst, off) in enumerate(outs):
                    for k in range(KD):
                        d = dst[:, k, n * CH:(n + 1) * CH]
                        if ln is None:
                            nc.scalar.activation(d, turned[:, n, k, :], ACT.Copy)
                        elif off:
                            nc.scalar.activation(d, turned[:, n, k, :], ACT.Identity, scale=lnw[:, k, 0:1], bias=lnw[:, k, 1:2])
                        else:
                            nc.scalar.activation(d, turned[:, n, k, :], ACT.Copy, scale=lnw[:, k, i:i + 1])
    return keep


def route_tokens(nc, ctx, c, name, route, scratch, weight):
    n_iter, k_eff, heavy = 50, min(256 * 9.0 / 8.0, S), 256
    log_k = float(np.log(np.float32(k_eff)))
    with ExitStack() as inner:
        def tmp(n, shape, dt=F32):
            return inner.enter_context(nc.sbuf_tensor(f"{name}_{n}", shape, dt))

        def sem(n):
            return c.semaphore(f"{name}_{n}")

        r3 = route[:].rearrange("p (b t) -> p b t", b=B)
        best, best_all = tmp("best", [P, B]), tmp("best_all", [P, B])
        na, top = tmp("na", [P, B]), tmp("top", [P, B])
        part, total_ln = tmp("part", [P, B]), tmp("total_ln", [P, B])
        sbm, ex = tmp("sbm", [P, B, NT]), tmp("ex", [P, B, NT])
        t_col = tmp("t_col", [P, P])
        t_row = tmp("t_row", [TT, P])
        t_all = tmp("t_all", [P, TOK])
        e_col, g_col = tmp("e_col", [P, TT]), tmp("g_col", [P, TT])
        before = tmp("before", [P, 2 * S])
        junk = tmp("junk", [P, 2, S])
        above, equal = tmp("above", [P, TT]), tmp("equal", [P, TT])
        ps = inner.enter_context(nc.psum_tensor(f"{name}_ps", [P, 512], F32))
        pt = inner.enter_context(nc.psum_tensor(f"{name}_pt", [P, 512], F32))
        s = {n: sem(n) for n in ("best_ready best_done ex_ready sbm_ready part_ready sum_ready ln_ready na_ready tcol_ready trow_ps "
                                 "trow_ready stored t_loaded e_ready before_ready step loop_step tail_step").split()}
        block = inner.enter_context(nc.Block())

        def wide(v):
            return v[:].unsqueeze(2).broadcast_to([P, B, NT])

        @block.gpsimd
        def _(pool):
            pool.wait_ge(s["best_ready"], 1)
            pool.partition_all_reduce(best_all[:], best[:], P, bass.bass_isa.ReduceOp.max).then_inc(s["best_done"], 1)
            pool.wait_ge(s["best_done"], 1)
            pool.memset(before[:], 1.0).then_inc(s["before_ready"], 1)
            pool.wait_ge(s["before_ready"], 1)
            pool.affine_select(out=before[:], in_=before[:], compare_op=ALU.is_gt, fill=0.0, base=S, pattern=[[-1, 2 * S]],
                               channel_multiplier=1).then_inc(s["before_ready"], 1)

        @block.tensor
        def _(pe):
            with pe.Fori(0, n_iter - 1) as i:
                pe.wait_ge(s["part_ready"], i + 1)
                nc.tensor.matmul(ps[:, 0:B], c.ones[:], part[:], start=True, stop=True).then_inc(s["sum_ready"], 1)
            pe.wait_ge(s["tcol_ready"], 1)
            nc.tensor.transpose(pt[:, 0:P], t_col[:], c.ident[:]).then_inc(s["trow_ps"], 1)

        @block.scalar
        def _(act):
            with act.Fori(0, n_iter - 1) as i:
                act.wait_ge(s["sbm_ready"], i + 1)
                nc.scalar.activation(ex[:], sbm[:], ACT.Exp).then_inc(s["ex_ready"], 1)
                act.wait_ge(s["sum_ready"], i + 1)
                nc.scalar.activation(total_ln[:], ps[:, 0:B], ACT.Ln).then_inc(s["ln_ready"], 1)
            act.wait_ge(s["tcol_ready"], 1)
            nc.scalar.activation(e_col[:], t_col[:, 0:TT], ACT.Exp).then_inc(s["e_ready"], 1)

        @block.sync
        def _(sp):
            sp.wait_ge(s["trow_ready"], 1)
            sp.dma_start(scratch, t_row[:]).then_inc(s["stored"], 16)
            sp.wait_ge(s["stored"], 16)
            sp.dma_start(t_all[:], row_tile(scratch.rearrange("t p -> (t p)"), P)).then_inc(s["t_loaded"], 16)
            sp.wait_ge(s["t_loaded"], 16)

        @block.vector
        def _(dve):
            step = Tally(dve, s["step"])
            step.add(nc.vector.memset(t_col[:], 0.0))
            step.add(nc.vector.memset(na[:], float(np.log(np.float32(S))) - log_k))
            nc.vector.tensor_reduce(best[:], r3, AX.X, ALU.max).then_inc(s["best_ready"], 1)
            dve.wait_ge(s["best_done"], 1)
            step.wait()
            dve.sem_inc(s["na_ready"], 1)
            with dve.Fori(0, n_iter - 1) as i:
                dve.wait_ge(s["na_ready"], i + 1)
                nc.vector.tensor_tensor(sbm[:], r3, wide(na), ALU.min).then_inc(s["loop_step"], 1)
                nc.vector.tensor_tensor(top[:], best_all[:], na[:], ALU.min).then_inc(s["loop_step"], 1)
                dve.wait_ge(s["loop_step"], i * 2 + 2)
                nc.vector.tensor_tensor(sbm[:], sbm[:], wide(top), ALU.subtract).then_inc(s["sbm_ready"], 1)
                dve.wait_ge(s["ex_ready"], i + 1)
                nc.vector.tensor_reduce(part[:], ex[:], AX.X, ALU.add).then_inc(s["part_ready"], 1)
                dve.wait_ge(s["ln_ready"], i + 1)
                nc.vector.scalar_tensor_tensor(na[:], top[:], -log_k, total_ln[:], ALU.add, ALU.add).then_inc(s["na_ready"], 1)
            tail = Tally(dve, s["tail_step"])
            dve.wait_ge(s["na_ready"], n_iter)
            t3 = t_col[:, 0:TT].rearrange("p (b t) -> p b t", b=B)
            tail.add(nc.vector.tensor_tensor(t3, r3, wide(na), ALU.subtract))
            tail.wait()
            nc.vector.tensor_scalar(t_col[:, 0:TT], t_col[:, 0:TT], 0.0, None, ALU.min).then_inc(s["tcol_ready"], 1)
            dve.wait_ge(s["trow_ps"], 1)
            nc.vector.tensor_copy(t_row[:], pt[0:TT, 0:P]).then_inc(s["trow_ready"], 1)
            dve.wait_ge(s["e_ready"], 1)
            tail.add(nc.vector.tensor_scalar(g_col[:], e_col[:], -1.0, 1.0, ALU.mult, ALU.add))
            tail.wait()
            tail.add(nc.vector.tensor_tensor(g_col[:], g_col[:], e_col[:], ALU.add))
            dve.wait_ge(s["before_ready"], 2)
            dve.wait_ge(s["t_loaded"], 16)
            dve.wait_ge(s["tcol_ready"], 1)
            for t in range(TT):
                b, own = divmod(t, NT)
                row = t_all[:, b * S:(b + 1) * S]
                if t:
                    tail.wait()
                tail.add(nc.vector.scalar_tensor_tensor(junk[:, 0, :], row, t_col[:, t:t + 1], before[:, 0:S],
                                                        ALU.is_gt, ALU.mult, accum_out=above[:, t:t + 1]))
                tail.add(nc.vector.scalar_tensor_tensor(junk[:, 1, :], row, t_col[:, t:t + 1], before[:, S - P * own:2 * S - P * own],
                                                        ALU.is_equal, ALU.mult, accum_out=equal[:, t:t + 1]))
            tail.wait()
            tail.add(nc.vector.tensor_tensor(above[:], above[:], equal[:], ALU.add))
            tail.wait()
            nc.vector.scalar_tensor_tensor(weight[:], above[:], heavy - 0.5, g_col[:], ALU.is_lt, ALU.mult)


def ffn0(nc, c, name, x_in, x_out, gate, io):
    DH = io["l0_w1h"].shape[1]
    MH = DH // P
    with ExitStack() as ctx:
        def sb(n, shape, dt=F32):
            return ctx.enter_context(nc.sbuf_tensor(f"{name}_{n}", shape, dt))

        light_in, heavy_in = sb("light_in", [P, KD, TOK]), sb("heavy_in", [P, KD, TOK])
        weight = sb("weight", [P, TT])
        keep = normed(nc, ctx, c, f"{name}n", x_in, "rms", io["l0_gammas"], ((light_in, 0), (heavy_in, 0)), io["l0_token"])
        x = keep.x
        route_tokens(nc, ctx, c, f"{name}r", keep.route, io["scratch"], weight)

        w1l, w2l = sb("w1l", [P, KD, P]), sb("w2l", [P, D])
        w1h, w2h = sb("w1h", [P, KD, DH]), sb("w2h", [P, MH, D])
        b1 = sb("b1", [P, 1 + MH])
        b2l, b2h = sb("b2l", [P, D]), sb("b2h", [P, D])
        hl, hh = sb("hl", [P, CH]), sb("hh", [P, MH, CH])
        yl, yh = sb("yl", [P, CT, D]), sb("yh", [P, CT, D])
        hid = ctx.enter_context(nc.psum_tensor(f"{name}_hid", [P, 3, 512], F32))
        out_l = ctx.enter_context(nc.psum_tensor(f"{name}_out_l", [P, CT, D], F32))
        out_h = ctx.enter_context(nc.psum_tensor(f"{name}_out_h", [P, CT, D], F32))
        s = {n: c.semaphore(f"{name}_{n}") for n in
             "w_loaded hid_ready act_done light_done heavy_done out_free step x_ready stored dve_passed".split()}
        H = 1 + MH
        block = ctx.enter_context(nc.Block())

        @block.sync
        def _(sp):
            for dst, src in ((w1l, io["l0_w1l"].rearrange("(k p) m -> p k m", p=P)), (b1, io["l0_b1"]),
                             (w1h, io["l0_w1h"].rearrange("(k p) m -> p k m", p=P)), (w2l, io["l0_w2l"]),
                             (w2h, io["l0_w2h"].rearrange("(k p) m -> p k m", p=P)),
                             (b2l, row_tile(io["l0_b2l"], P)), (b2h, row_tile(io["l0_b2h"], P))):
                sp.dma_start(dst[:], src).then_inc(s["w_loaded"], 16)
            with sp.Fori(0, NC) as n:
                tile, tok = sp.snap(n * CT), sp.snap(n * CH)
                sp.wait_ge(s["x_ready"], n + 1)
                sp.dma_start(tiles_of(x_out, tok, CT), x[:, bass.ds(tile, CT), :]).then_inc(s["stored"], 16)
            sp.wait_ge(s["stored"], 16 * NC)

        @block.tensor
        def _(pe):
            pe.wait_ge(s["w_loaded"], 16 * 7)
            with pe.Fori(0, NC) as n:
                for i in range(H):
                    if i >= 3:
                        pe.wait_ge(s["act_done"], n * H + i - 2)
                    src = light_in if i == 0 else heavy_in
                    for k in range(KD):
                        w = w1l[:, k, :] if i == 0 else w1h[:, k, (i - 1) * P:i * P]
                        last = nc.tensor.matmul(hid[:, i % 3, :], w, src[:, k, bass.ds(n * CH, CH)], start=k == 0, stop=k == KD - 1)
                    last.then_inc(s["hid_ready"], 1)
                pe.wait_ge(s["out_free"], n + 1)
                pe.wait_ge(s["act_done"], n * H + 1)
                for t in range(CT):
                    last = nc.tensor.matmul(out_l[:, t, :], hl[:, t * P:(t + 1) * P], w2l[:], start=True, stop=True)
                last.then_inc(s["light_done"], 1)
                for t in range(CT):
                    for k in range(MH):
                        if t == 0:
                            pe.wait_ge(s["act_done"], n * H + k + 2)
                        last = nc.tensor.matmul(out_h[:, t, :], hh[:, k, t * P:(t + 1) * P], w2h[:, k, :], start=k == 0, stop=k == MH - 1)
                last.then_inc(s["heavy_done"], 1)

        @block.scalar
        def _(act):
            act.wait_ge(s["w_loaded"], 16 * 7)
            with act.Fori(0, NC) as n:
                for i in range(H):
                    act.wait_ge(s["hid_ready"], n * H + i + 1)
                    dst = hl[:] if i == 0 else hh[:, i - 1, :]
                    nc.scalar.activation(dst, hid[:, i % 3, :], ACT.Gelu, bias=b1[:, i:i + 1]).then_inc(s["act_done"], 1)

        @block.vector
        def _(dve):
            dve.wait_ge(s["w_loaded"], 16 * 7)
            dve.sem_inc(s["out_free"], 1)
            with dve.Fori(0, NC) as n:
                tile = dve.snap(n * CT)
                step = Tally(dve, s["step"], 1 + CT, n)
                dve.wait_ge(s["light_done"], n + 1)
                step.add(nc.vector.tensor_tensor(yl[:], out_l[:], b2l[:].unsqueeze(1).broadcast_to([P, CT, D]), ALU.add))
                dve.wait_ge(s["heavy_done"], n + 1)
                nc.vector.tensor_tensor(yh[:], out_h[:], b2h[:].unsqueeze(1).broadcast_to([P, CT, D]), ALU.add).then_inc(s["out_free"], 1)
                dve.wait_ge(s["out_free"], n + 2)
                step.wait()
                for t in range(CT):
                    step.add(nc.vector.scalar_tensor_tensor(yl[:, t, :], yh[:, t, :], weight[:, bass.ds(tile + t, 1)], yl[:, t, :],
                                                            ALU.mult, ALU.add))
                step.wait()
                step.close()
                xs = x[:, bass.ds(tile, CT), :]
                nc.vector.scalar_tensor_tensor(xs, yl[:], c.gates[:, gate:gate + 1], xs, ALU.mult, ALU.add).then_inc(s["x_ready"], 1)
                pause(dve, s["x_ready"], n + 1, s["dve_passed"])


def ffn1(nc, c, name, x_in, x_out, gate, io):
    DH = io["l1_w1"].shape[1]
    MH = DH // P
    with ExitStack() as ctx:
        def sb(n, shape, dt=F32):
            return ctx.enter_context(nc.sbuf_tensor(f"{name}_{n}", shape, dt))

        xq = sb("xq", [P, KD, TOK], BF16)
        keep = normed(nc, ctx, c, f"{name}n", x_in, "quant", None, ((xq, 0),))
        x, step_size = keep.x, keep.step_size

        w1, w2 = sb("w1", [P, KD, DH]), sb("w2", [P, MH, D])
        w1t, w2t = sb("w1t", [P, KD, DH], BF16), sb("w2t", [P, MH, D], BF16)
        part, mean, scale = sb("part", [P, 2]), sb("mean", [P, 2]), sb("scale", [P, 2])
        conv = sb("conv", [P, MH, 4])
        diag = sb("diag", [P, P * TT])
        row = sb("row", [P, B, S])
        h = sb("h", [P, S + 2])
        y = sb("y", [P, S])
        act_out = sb("act_out", [P, MH, S])
        big = sb("big", [P, S])
        mag = sb("mag", [P, 2, S])
        size, back, inv = sb("size", [P, NT]), sb("back", [P, NT]), sb("inv", [P, NT])
        diag2 = sb("diag2", [P, P * NT])
        hq = sb("hq", [P, MH, S], BF16)
        ps = [ctx.enter_context(nc.psum_tensor(f"{name}_ps{i}", [P, 2, 512], F32)) for i in range(2)]
        out_ps = ctx.enter_context(nc.psum_tensor(f"{name}_out_ps", [P, NT, D], F32))
        psf = [p[:].rearrange("p a n -> p (a n)") for p in ps]
        outf = out_ps[:].rearrange("p t d -> p (t d)")
        s = {n: c.semaphore(f"{name}_{n}") for n in
             "w1_loaded w2_loaded conv_loaded part_ready total_ready tern_ready diag_ready row_ps row_ready hid_ready h_ready conv_ready silu_done mag_ready big_done "
             "big_ready big_turned diag2_ready row2_ps hq_ready out_ready x_ready stored step body_step sp_passed dve_passed".split()}
        block = ctx.enter_context(nc.Block())

        @block.sync
        def _(sp):
            sp.dma_start(w1[:], io["l1_w1"].rearrange("(k p) m -> p k m", p=P)).then_inc(s["w1_loaded"], 16)
            sp.dma_start(w2[:], io["l1_w2"].rearrange("(k p) m -> p k m", p=P)).then_inc(s["w2_loaded"], 16)
            sp.dma_start(conv[:], io["l1_conv"]).then_inc(s["conv_loaded"], 16)
            with sp.Fori(0, B) as b:
                tile, tok = sp.snap(b * NT), sp.snap(b * S)
                sp.wait_ge(s["x_ready"], b + 1)
                sp.dma_start(tiles_of(x_out, tok, NT), x[:, bass.ds(tile, NT), :]).then_inc(s["stored"], 16)
            sp.wait_ge(s["stored"], 16 * B)

        @block.tensor
        def _(pe):
            pe.wait_ge(s["part_ready"], 2)
            nc.tensor.matmul(ps[0][:, 0, 0:2], c.ones[:], part[:], start=True, stop=True).then_inc(s["total_ready"], 1)
            pe.wait_ge(s["diag_ready"], TT)
            for b in range(B):
                for t in range(NT):
                    n = b * NT + t
                    last = nc.tensor.matmul(outf[:, n * P:(n + 1) * P], c.ones[:], diag[:, n * P:(n + 1) * P], start=True, stop=True)
            last.then_inc(s["row_ps"], 1)
            pe.wait_ge(s["tern_ready"], 2)
            pe.wait_ge(s["row_ready"], 1)
            with pe.Fori(0, B) as b:
                for m in range(MH):
                    if m >= 2:
                        pe.wait_ge(s["h_ready"], b * MH + m - 1)
                    for j in range(2):
                        for k in range(KD):
                            last = nc.tensor.matmul(ps[m % 2][:, j, :], w1t[:, k, m * P:(m + 1) * P],
                                                    xq[:, k, bass.ds(b * S + j * CH, CH)], start=k == 0, stop=k == KD - 1)
                    last.then_inc(s["hid_ready"], 1)
                pe.wait_ge(s["big_ready"], b + 1)
                for t in range(NT):
                    last = nc.tensor.transpose(psf[0][:, t * P:(t + 1) * P], big[:, t * P:(t + 1) * P], c.ident[:])
                last.then_inc(s["big_turned"], 1)
                pe.wait_ge(s["diag2_ready"], b + 1)
                for t in range(NT):
                    last = nc.tensor.matmul(psf[1][:, t * P:(t + 1) * P], c.ones[:], diag2[:, t * P:(t + 1) * P], start=True, stop=True)
                last.then_inc(s["row2_ps"], 1)
                for t in range(NT):
                    for k in range(MH):
                        if t == 0:
                            pe.wait_ge(s["hq_ready"], b * MH + k + 1)
                        last = nc.tensor.matmul(out_ps[:, t, :], hq[:, k, t * P:(t + 1) * P], w2t[:, k, :], start=k == 0, stop=k == MH - 1)
                last.then_inc(s["out_ready"], 1)

        @block.scalar
        def _(act):
            act.wait_ge(s["row_ps"], 1)
            act.wait_ge(s["tern_ready"], 2)
            nc.scalar.activation(row[:].rearrange("p b n -> p (b n)"), outf, ACT.Copy, scale=mean[:, 0:1]).then_inc(s["row_ready"], 1)
            with act.Fori(0, B) as b:
                for m in range(MH):
                    act.wait_ge(s["conv_ready"], b * MH + m + 1)
                    nc.scalar.activation(act_out[:, m, :], y[:], ACT.Silu).then_inc(s["silu_done"], 1)
                    act.wait_ge(s["silu_done"], b * MH + m + 1)
                    if m >= 2:
                        act.wait_ge(s["big_done"], b * MH + m - 1)
                    nc.scalar.activation(mag[:, m % 2, :], act_out[:, m, :], ACT.Abs).then_inc(s["mag_ready"], 1)

        @block.vector
        def _(dve):
            step = Tally(dve, s["step"])
            step.add(nc.vector.memset(h[:], 0.0))
            for t in range(TT):
                nc.vector.tensor_scalar(diag[:, t * P:(t + 1) * P], c.ident[:], step_size[:, t:t + 1], None, ALU.mult).then_inc(s["diag_ready"], 1)
            for i, (w, loaded) in enumerate(((w1, "w1_loaded"), (w2, "w2_loaded"))):
                dve.wait_ge(s[loaded], 16)
                nc.vector.tensor_reduce(part[:, i:i + 1], w[:], AX.XY, ALU.add, apply_absolute_value=True).then_inc(s["part_ready"], 1)
            dve.wait_ge(s["total_ready"], 1)
            step.add(nc.vector.tensor_scalar(mean[:], ps[0][:, 0, 0:2], 1.0 / (D * DH), 1e-5, ALU.mult, ALU.max))
            step.wait()
            step.add(nc.vector.reciprocal(scale[:], mean[:]))
            step.wait()
            for i, w in enumerate((w1, w2)):
                step.add(nc.vector.tensor_scalar(w[:], w[:], scale[:, i:i + 1], ROUND, ALU.mult, ALU.add))
            step.wait()
            for w in (w1, w2):
                step.add(nc.vector.tensor_scalar(w[:], w[:], -ROUND, -1.0, ALU.add, ALU.max))
            step.wait()
            for w, wt in ((w1, w1t), (w2, w2t)):
                nc.vector.tensor_scalar(wt[:], w[:], 1.0, None, ALU.min).then_inc(s["tern_ready"], 1)
            dve.wait_ge(s["conv_loaded"], 16)
            dve.wait_ge(s["row_ready"], 1)
            with dve.Fori(0, B) as b:
                body = Tally(dve, s["body_step"], 1 + 2 * MH + 4 + NT - 1 + 2 + 2 * MH + NT - 1, b)
                body.add(nc.vector.memset(big[:], 0.0))
                body.wait()

                def largest(m):
                    dve.wait_ge(s["mag_ready"], b * MH + m + 1)
                    if m >= 1:
                        dve.wait_ge(s["big_done"], b * MH + m)
                    nc.vector.tensor_tensor(big[:], mag[:, m % 2, :], big[:], ALU.max).then_inc(s["big_done"], 1)

                for m in range(MH):
                    dve.wait_ge(s["hid_ready"], b * MH + m + 1)
                    if m >= 1:
                        dve.wait_ge(s["conv_ready"], b * MH + m)
                    rowb = row[:, bass.ds(b, 1), :].rearrange("p o n -> p (o n)")
                    nc.vector.tensor_tensor(h[:, 1:S + 1], psf[m % 2], rowb, ALU.mult).then_inc(s["h_ready"], 1)
                    dve.wait_ge(s["h_ready"], b * MH + m + 1)
                    if m >= 1:
                        dve.wait_ge(s["silu_done"], b * MH + m)
                        largest(m - 1)
                    body.add(nc.vector.tensor_scalar(y[:], h[:, 1:S + 1], conv[:, m, 1:2], conv[:, m, 3:4], ALU.mult, ALU.add))
                    body.wait()
                    body.add(nc.vector.scalar_tensor_tensor(y[:], h[:, 0:S], conv[:, m, 0:1], y[:], ALU.mult, ALU.add))
                    body.wait()
                    nc.vector.scalar_tensor_tensor(y[:], h[:, 2:S + 2], conv[:, m, 2:3], y[:], ALU.mult, ALU.add).then_inc(s["conv_ready"], 1)
                largest(MH - 1)
                dve.wait_ge(s["big_done"], b * MH + MH)
                dve.sem_inc(s["big_ready"], 1)
                dve.wait_ge(s["big_turned"], b + 1)
                body.add(nc.vector.tensor_reduce(size[:], psf[0].rearrange("p (t n) -> p t n", t=NT), AX.X, ALU.max))
                body.wait()
                body.add(nc.vector.tensor_scalar(size[:], size[:], 1e-5, None, ALU.max))
                body.wait()
                body.add(nc.vector.reciprocal(inv[:], size[:]))
                body.wait()
                body.add(nc.vector.tensor_scalar(inv[:], inv[:], 127.0, None, ALU.mult))
                body.wait()
                for t in range(NT):
                    ins = nc.vector.tensor_scalar(diag2[:, t * P:(t + 1) * P], c.ident[:], inv[:, t:t + 1], None, ALU.mult)
                    if t < NT - 1:
                        body.add(ins)
                ins.then_inc(s["diag2_ready"], 1)
                body.add(nc.vector.tensor_scalar(back[:], size[:], mean[:, 1:2], 1.0 / 127.0, ALU.mult, ALU.mult))
                body.wait()
                body.add(nc.vector.tensor_scalar(back[:], back[:], c.gates[:, gate:gate + 1], None, ALU.mult))
                dve.wait_ge(s["row2_ps"], b + 1)
                for m in range(MH):
                    body.add(nc.vector.tensor_tensor(act_out[:, m, :], act_out[:, m, :], psf[1], ALU.mult))
                    body.wait()
                    body.add(nc.vector.tensor_scalar(act_out[:, m, :], act_out[:, m, :], ROUND, -ROUND, ALU.add, ALU.add))
                    body.wait()
                    nc.vector.tensor_scalar(hq[:, m, :], act_out[:, m, :], 127.0, -128.0, ALU.min, ALU.max).then_inc(s["hq_ready"], 1)
                dve.wait_ge(s["out_ready"], b + 1)
                for t in range(NT):
                    xs = x[:, bass.ds(b * NT + t, 1), :].rearrange("p o d -> p (o d)")
                    ins = nc.vector.scalar_tensor_tensor(xs, out_ps[:, t, :], back[:, t:t + 1], xs, ALU.mult, ALU.add)
                    if t < NT - 1:
                        body.add(ins)
                ins.then_inc(s["x_ready"], 1)
                body.close()
                pause(dve, s["x_ready"], b + 1, s["dve_passed"])


def moe(nc, c, name, x_in, x_out, gate, top, w_gate, w_up, w_down, w_route, b_route, ln=None, base=None):
    E = w_gate.shape[0]
    DH = w_gate.shape[2]
    MH = DH // P
    with ExitStack() as ctx:
        def sb(n, shape, dt=F32):
            return ctx.enter_context(nc.sbuf_tensor(f"{name}_{n}", shape, dt))

        xT = sb("xT", [P, KD, TOK])
        acc = sb("acc", [P, TT, D])
        wt = sb("wt", [P, TT, E])
        keep = normed(nc, ctx, c, f"{name}n", x_in, "plain", ln, ((xT, ln is not None),))
        x = keep.x

        with ExitStack() as inner:
            def tmp(n, shape, dt=F32):
                return inner.enter_context(nc.sbuf_tensor(f"{name}r_{n}", shape, dt))

            wr, br = tmp("wr", [P, KD, E]), tmp("br", [P, E])
            lg, rank = tmp("lg", [P, TT, E]), tmp("rank", [P, TT, E])
            cmp_ = tmp("cmp", [P, E, TT, E])
            lead, total = tmp("lead", [P, TT]), tmp("total", [P, TT])
            lps = inner.enter_context(nc.psum_tensor(f"{name}r_lps", [P, TT, E], F32))
            s = {n: c.semaphore(f"{name}r_{n}") for n in "w_loaded lg_ps step sh_ready ex_ready".split()}
            block = inner.enter_context(nc.Block())

            @block.sync
            def _(sp):
                sp.dma_start(wr[:], w_route.rearrange("(k p) e -> p k e", p=P)).then_inc(s["w_loaded"], 16)
                sp.dma_start(br[:], row_tile(b_route, P)).then_inc(s["w_loaded"], 16)

            @block.tensor
            def _(pe):
                pe.wait_ge(s["w_loaded"], 32)
                for t in range(TT):
                    for k in range(KD):
                        last = nc.tensor.matmul(lps[:, t, :], xT[:, k, t * P:(t + 1) * P], wr[:, k, :], start=k == 0, stop=k == KD - 1)
                last.then_inc(s["lg_ps"], 1)

            @block.scalar
            def _(act):
                if top > 1:
                    act.wait_ge(s["sh_ready"], 1)
                    nc.scalar.activation(wt[:], wt[:], ACT.Exp).then_inc(s["ex_ready"], 1)

            @block.vector
            def _(dve):
                step = Tally(dve, s["step"])
                dve.wait_ge(s["w_loaded"], 32)
                dve.wait_ge(s["lg_ps"], 1)
                step.add(nc.vector.tensor_tensor(lg[:], lps[:], br[:].unsqueeze(1).broadcast_to([P, TT, E]), ALU.add))
                step.wait()
                for f in range(E):
                    n = f + 1
                    step.add(nc.vector.tensor_tensor(cmp_[:, f, :, 0:n], lg[:, :, f:n].broadcast_to([P, TT, n]), lg[:, :, 0:n], ALU.is_gt))
                    if n < E:
                        step.add(nc.vector.tensor_tensor(cmp_[:, f, :, n:E], lg[:, :, f:n].broadcast_to([P, TT, E - n]), lg[:, :, n:E], ALU.is_ge))
                if top > 1:
                    step.add(nc.vector.tensor_reduce(lead[:], lg[:], AX.X, ALU.max))
                step.wait()
                step.add(nc.vector.tensor_reduce(rank[:], cmp_[:].rearrange("p f t e -> p t e f"), AX.X, ALU.add))
                step.wait()
                if top == 1:
                    nc.vector.tensor_scalar(wt[:], rank[:], top - 0.5, None, ALU.is_lt)
                else:
                    step.add(nc.vector.tensor_scalar(rank[:], rank[:], top - 0.5, None, ALU.is_lt))
                    nc.vector.tensor_tensor(wt[:], lg[:], lead[:].unsqueeze(2).broadcast_to([P, TT, E]), ALU.subtract).then_inc(s["sh_ready"], 1)
                    dve.wait_ge(s["ex_ready"], 1)
                    step.wait()
                    step.add(nc.vector.tensor_tensor(wt[:], wt[:], rank[:], ALU.mult))
                    step.wait()
                    step.add(nc.vector.tensor_reduce(total[:], wt[:], AX.X, ALU.add))
                    step.wait()
                    step.add(nc.vector.reciprocal(total[:], total[:]))
                    step.wait()
                    nc.vector.tensor_tensor(wt[:], wt[:], total[:].unsqueeze(2).broadcast_to([P, TT, E]), ALU.mult)

        n_w = 3 if w_up is not None else 2
        wg = [sb(f"wg{i}", [P, KD, DH]) for i in range(2)]
        wu = [sb(f"wu{i}", [P, KD, DH]) for i in range(2)] if w_up is not None else None
        wd = [sb(f"wd{i}", [P, MH, D]) for i in range(2)]
        hh = sb("hh", [P, MH, CH])
        sg = sb("sg", [P, 2, CH])
        keep_base = sb("base", [P, TT, D]) if base is not None else None
        hid = ctx.enter_context(nc.psum_tensor(f"{name}_hid", [P, 2, 2, 512], F32))
        out_ps = [ctx.enter_context(nc.psum_tensor(f"{name}_out{i}", [P, CT, D], F32)) for i in range(2)]
        names = "w_loaded0 w_loaded1 x_loaded hid_ready silu_done h_ready down_done summed out_ready stored tail dve_passed pe_passed".split()
        s = {n: c.semaphore(f"{name}_{n}") for n in names}
        block = ctx.enter_context(nc.Block())
        h_done = s["h_ready"]

        @block.sync
        def _(sp):
            def load(i, e):
                pick = lambda w: w[bass.ds(e, 1)].rearrange("o (k p) n -> p (o k) n", p=P)
                sp.dma_start(wg[i][:], pick(w_gate)).then_inc(s[f"w_loaded{i}"], 16)
                if wu is not None:
                    sp.dma_start(wu[i][:], pick(w_up)).then_inc(s[f"w_loaded{i}"], 16)
                sp.dma_start(wd[i][:], pick(w_down)).then_inc(s[f"w_loaded{i}"], 16)

            load(0, 0)
            load(1, 1)
            with sp.Fori(0, E // 2 - 1) as r:
                for i in range(2):
                    e = sp.snap(r * 2 + 2 + i)
                    sp.wait_ge(s["down_done"], r * 2 * NC + (i + 1) * NC)
                    load(i, e)
            for n in range(NC):
                sp.wait_ge(s["out_ready"], n + 1)
                sp.dma_start(tiles_of(x_out, n * CH, CT), x[:, n * CT:(n + 1) * CT, :]).then_inc(s["stored"], 16)
            sp.wait_ge(s["stored"], 16 * NC)

        @block.tensor
        def _(pe):
            with pe.Fori(0, E // 2) as r:
                for i in range(2):
                    pause(pe, s[f"w_loaded{i}"], r * 16 * n_w + 16 * n_w, s["pe_passed"])
                    with pe.Fori(0, NC // 2) as q:
                        for half in range(2):
                            v = (r * 2 + i) * NC + q * 2 + half
                            for m in range(MH):
                                if m >= 2:
                                    pe.wait_ge(h_done, v * MH + m - 1)
                                for j in range(n_w - 1):
                                    w = (wg, wu)[j][i]
                                    for k in range(KD):
                                        last = nc.tensor.matmul(hid[:, m % 2, j, :], w[:, k, m * P:(m + 1) * P],
                                                                xT[:, k, bass.ds(q * 2 * CH + half * CH, CH)], start=k == 0, stop=k == KD - 1)
                                last.then_inc(s["hid_ready"], 1)
                            pe.wait_ge(s["summed"], v + 1)
                            for t in range(CT):
                                for k in range(MH):
                                    if t == 0:
                                        pe.wait_ge(h_done, v * MH + k + 1)
                                    last = nc.tensor.matmul(out_ps[half][:, t, :], hh[:, k, t * P:(t + 1) * P], wd[i][:, k, :],
                                                            start=k == 0, stop=k == MH - 1)
                            last.then_inc(s["down_done"], 1)

        @block.scalar
        def _(act):
            with act.Fori(0, E * NC) as v:
                for m in range(MH):
                    act.wait_ge(s["hid_ready"], v * MH + m + 1)
                    if wu is None:
                        nc.scalar.activation(hh[:, m, :], hid[:, m % 2, 0, :], ACT.Gelu_apprx_tanh).then_inc(h_done, 1)
                    else:
                        if m >= 2:
                            act.wait_ge(h_done, v * MH + m - 1)
                        nc.scalar.activation(sg[:, m % 2, :], hid[:, m % 2, 0, :], ACT.Silu).then_inc(s["silu_done"], 1)

        @block.vector
        def _(dve):
            nc.vector.memset(acc[:], 0.0).then_inc(s["summed"], 1)
            dve.wait_ge(s["summed"], 1)
            dve.sem_inc(s["summed"], 1)
            with dve.Fori(0, E // 2) as r:
                for i in range(2):
                    with dve.Fori(0, NC // 2) as q:
                        for half in range(2):
                            v = (r * 2 + i) * NC + q * 2 + half
                            if wu is not None:
                                for m in range(MH):
                                    dve.wait_ge(s["silu_done"], v * MH + m + 1)
                                    nc.vector.tensor_tensor(hh[:, m, :], sg[:, m % 2, :], hid[:, m % 2, 1, :], ALU.mult).then_inc(h_done, 1)
                            dve.wait_ge(s["down_done"], v + 1)
                            for t in range(CT):
                                tile = q * 2 * CT + half * CT + t
                                a = acc[:, bass.ds(tile, 1), :].rearrange("p o d -> p (o d)")
                                w = wt[:, bass.ds(tile, 1), bass.ds(r * 2 + i, 1)].rearrange("p o e -> p (o e)")
                                ins = nc.vector.scalar_tensor_tensor(a, out_ps[half][:, t, :], w, a, ALU.mult, ALU.add)
                            ins.then_inc(s["summed"], 1)
                            pause(dve, s["summed"], v + 3, s["dve_passed"])
            tail = Tally(dve, s["tail"])
            g = c.gates[:, gate:gate + 1]
            if base is not None:
                dve.wait_ge(s["x_loaded"], 16)
                tail.add(nc.vector.tensor_tensor(acc[:], acc[:], x[:], ALU.add))
                tail.wait()
            for n in range(NC):
                ts = slice(n * CT, (n + 1) * CT)
                r0 = x if base is None else keep_base
                nc.vector.scalar_tensor_tensor(x[:, ts, :], acc[:, ts, :], g, r0[:, ts, :], ALU.mult, ALU.add).then_inc(s["out_ready"], 1)

        if base is not None:
            @block.gpsimd
            def _(pool):
                pool.dma_start(keep_base[:], tiles_of(base, 0, TT)).then_inc(s["x_loaded"], 16)


def pack64(wq, wk, wv, wo):
    groups = wq.shape[1] // D
    qkv = np.stack([np.stack([by_partition(w[:, g * D:(g + 1) * D]) for w in (wq, wk, wv)], 1) for g in range(groups)])
    out = np.stack([by_partition(wo[g * D:(g + 1) * D]) for g in range(groups)])
    return np.concatenate([qkv, qkv]), np.concatenate([out, out])


def columns(*vectors):
    return np.stack([v.reshape(-1, P).T for v in vectors], 2)


def spread_heads(w):
    out = np.zeros((w.shape[0], 16, 32), w.dtype)
    out[:, :, 0:16] = w.reshape(w.shape[0], 16, 16)
    return out.reshape(w.shape[0], 512)


def by_partition(w):
    return w.reshape(-1, P, w.shape[1]).transpose(1, 0, 2)


def pack16(wq, bq, wk, bk, wv, bv, wo, bo, masked):
    qkv = np.zeros((4, P, 898), np.float32)
    out = np.zeros((4, P, D), np.float32)
    cols = [spread_heads(w) for w in (wq, wk, wv)]
    bias = np.zeros((3, 16, 32), np.float32)
    for i, v in enumerate((bq, bk, bv)):
        if v is not None:
            bias[i, :, 0:16] = v.reshape(16, 16)
    if masked:
        bias[0, :, 17] = -4e9
    bias[1, :, 16] = 1.0
    bias[2, :, 16] = 1.0
    bias = bias.reshape(3, 512)
    for g in range(4):
        part = slice(g * P, (g + 1) * P)
        for i in range(3):
            qkv[g, :, 256 * i:256 * i + 256] = by_partition(cols[i][:, part]).reshape(P, 256)
        qkv[g, :, 768] = bias[0, part]
        qkv[g, :, 769] = bias[1, part]
        qkv[g, :, 770:898] = bias[2, part]
        for j in range(4):
            h = 4 * g + j
            out[g, 32 * j:32 * j + 16] = wo[16 * h:16 * h + 16]
    if bo is not None:
        out[0, 16] = bo
    return np.concatenate([qkv, qkv]), np.concatenate([out, out])


def kernel(**inputs):
    import concourse.bacc as _bacc
    from concourse.bass_utils import run_bass_kernel_spmd as _run

    a = {k: np.ascontiguousarray(v) for k, v in inputs.items()}
    arrays = lay_out(a)
    nc = _bacc.Bacc("TRN2", target_bir_lowering=False, num_devices=1)
    io = {}
    feed = {}
    for n, v in arrays.items():
        v = np.ascontiguousarray(v)
        feed[f"in_{n}"] = v
        io[n] = nc.dram_tensor(f"in_{n}", v.shape, mybir.dt.from_np(v.dtype), kind="ExternalInput").ap()
    io["out"] = nc.dram_tensor("out_0", (TOK, D), F32, kind="ExternalOutput").ap()
    for i in range(9):
        io[f"x{i}"] = nc.dram_tensor(f"x_{i}", (TOK, D), F32, kind="Internal").ap()
    program(nc, io)
    r = _run(nc, [feed], core_ids=[0])
    return r.results[0]["out_0"].reshape(B, S, D)


def program(nc, io):
    with ExitStack() as ctx:
        c = setup(nc, ctx, io)
        io["scratch"] = nc.dram_tensor("scratch", (TT, P), F32, kind="Internal").ap()
        attention16(nc, c, "l0x", io["x"], io["x0"], io["l0_qkv"], io["l0_wo"], 0, ctx_t=io["ctx_t"], mask=io["mask0"])
        c.end_stage()
        ffn0(nc, c, "l0f", io["x0"], io["x1"], 4, io)
        c.end_stage()
        attention64(nc, c, "l1x", io["x1"], io["x2"], io["l1_qkv"], io["l1_wo"], 1, io["ctx"], io["mask1"], io["l1_ln"],
                    out_ln=(io["l1_go"], io["l1_bo"]))
        c.end_stage()
        ffn1(nc, c, "l1f", io["x2"], io["x3"], 5, io)
        c.end_stage()
        attention16(nc, c, "l2x", io["x3"], io["x4"], io["l2_qkv"], io["l2_wo"], 2, ctx_t=io["ctx_t"])
        c.end_stage()
        moe(nc, c, "l2f", io["x4"], io["x5"], 6, 2, io["l2_wg"], io["l2_wu"], io["l2_wd"], io["l2_wr"], io["l2_br"])
        c.end_stage()
        attention64(nc, c, "l3x", io["x5"], io["x6"], io["l3_qkv"], io["l3_wo"], 3, io["ctx"], io["mask3"], io["l3_ln"],
                    rms=io["l3_gam"], out_b=io["l3_bo"])
        c.end_stage()
        attention16(nc, c, "l3a", io["x6"], io["x7"], io["l3_aqkv"], io["l3_awo"], None, ln=io["l3_ln1"], twice=True)
        c.end_stage()
        moe(nc, c, "l3f", io["x7"], io["out"], 7, 1, io["l3_w1"], None, io["l3_w2"], io["l3_wr"], io["l3_br"], io["l3_ln2"], io["x6"])
        c.end_stage()


def lay_out(a):
    arrays = {"x": a["x"].reshape(TOK, D), "ctx": a["ctx_1024"].reshape(B * SC, D), "ctx_t": a["ctx_1024"].reshape(B * SC, D).T,
              "g_xattn": a["g_xattn"], "g_ffn": a["g_ffn"], "mask0": a["mask_Bx1x1xS2_fk0"].reshape(B, SC),
              "mask1": a["mask_BxS2_bf1"], "mask3": a["mask_BxS2_bk0"]}
    n = "L0_xattn_"
    arrays["l0_qkv"], arrays["l0_wo"] = pack16(*[a[n + k] for k in ("Wq", "bq", "Wk", "bk", "Wv", "bv", "Wo", "bo")], True)
    n = "L0_ffn_"
    arrays["l0_gammas"] = columns(a[n + "light_gamma"], a[n + "heavy_gamma"])
    arrays["l0_token"] = a[n + "routing_token"]
    for k, m in (("w1l", "light_w1"), ("w2l", "light_w2"), ("w1h", "heavy_w1"), ("w2h", "heavy_w2"), ("b2l", "light_b2"), ("b2h", "heavy_b2")):
        arrays["l0_" + k] = a[n + m]
    arrays["l0_b1"] = np.concatenate([a[n + "light_b1"], a[n + "heavy_b1"]]).reshape(-1, P).T
    n = "L1_xattn_"
    wkv = a[n + "Wkv"]
    half = wkv.shape[1] // 2
    arrays["l1_qkv"], arrays["l1_wo"] = pack64(a[n + "Wq"], wkv[:, :half], wkv[:, half:], a[n + "Wout"])
    arrays["l1_ln"] = columns(a[n + "g_l"], a[n + "b_l"], a[n + "g_x"], a[n + "b_x"])
    arrays["l1_go"], arrays["l1_bo"] = a[n + "g_o"], a[n + "b_o"]
    n = "L1_ffn_"
    arrays["l1_w1"], arrays["l1_w2"] = a[n + "w1"].T, a[n + "w2"].T
    cw = a[n + "conv_w"]
    arrays["l1_conv"] = columns(cw[:, 0, 0], cw[:, 0, 1], cw[:, 0, 2], a[n + "conv_b"])
    n = "L2_xattn_"
    arrays["l2_qkv"], arrays["l2_wo"] = pack16(a[n + "Wq"].T, a[n + "bq"], a[n + "Wk"].T, a[n + "bk"], a[n + "Wv"].T, a[n + "bv"],
                                               a[n + "Wo"].T, a[n + "bo"], False)
    n = "L2_ffn_"
    for k, m in (("wg", "Wgate"), ("wu", "Wup"), ("wd", "Wdown")):
        arrays["l2_" + k] = a[n + m].transpose(0, 2, 1)
    arrays["l2_wr"], arrays["l2_br"] = a[n + "wg"].T, a[n + "bg"]
    n = "L3_xattn_"
    wkv = a[n + "W_kv"]
    half = wkv.shape[1] // 2
    arrays["l3_qkv"], arrays["l3_wo"] = pack64(a[n + "W_q"], wkv[:, :half], wkv[:, half:], a[n + "W_out"])
    arrays["l3_ln"] = columns(a[n + "ln_l_g"], a[n + "ln_l_b"], a[n + "ln_x_g"], a[n + "ln_x_b"])
    arrays["l3_gam"] = np.stack([np.concatenate([a[n + "q_gamma"]] * 2), np.concatenate([a[n + "k_gamma"]] * 2)], 1)
    arrays["l3_bo"] = a[n + "b_out"]
    n = "L3_ffn_"
    w = a[n + "w_qkv"]
    arrays["l3_aqkv"], arrays["l3_awo"] = pack16(w[:, :D], None, w[:, D:2 * D], None, w[:, 2 * D:], None, a[n + "w_proj"], None, False)
    arrays["l3_ln1"] = columns(a[n + "ln1_w"], a[n + "ln1_b"])
    arrays["l3_ln2"] = columns(a[n + "ln2_w"], a[n + "ln2_b"])
    arrays["l3_w1"], arrays["l3_w2"] = a[n + "w1"], a[n + "w2"]
    arrays["l3_wr"], arrays["l3_br"] = a[n + "gate_w"], a[n + "gate_b"]
    return arrays
```

```python
from contextlib import ExitStack

import concourse.bass as bass
from concourse import mybir
import numpy as np

P = 128
B, S, D = 2, 1024, 256
TOK = B * S
KD = D // P
NT = S // P
TT = TOK // P
CH = 512
NC = TOK // CH
CT = CH // P
SC = 77
F32 = mybir.dt.float32
BF16 = mybir.dt.bfloat16
U32 = mybir.dt.uint32
U8 = mybir.dt.uint8
ALU = mybir.AluOpType
ACT = mybir.ActivationFunctionType
AX = mybir.AxisListType
EPS = 1e-5
EXPERTS = 8
SLOTS = 256
ROUND = 1.5 * 2.0 ** 23


class Tally:

    def __init__(self, eng, sem, per_pass=0, turn=0):
        self.eng, self.sem, self.per_pass, self.n = eng, sem, per_pass, 0
        self.base = turn * per_pass if per_pass else 0

    def add(self, ins):
        self.n += 1
        ins.then_inc(self.sem, 1)

    def wait(self, passed=None):
        if passed is None:
            self.eng.wait_ge(self.sem, self.base + self.n)
        else:
            pause(self.eng, self.sem, self.base + self.n, passed)

    def close(self):
        assert self.n == self.per_pass, f"{self.n} steps, {self.per_pass} declared"


def pause(eng, sem, value, passed):
    eng.wait_ge(sem, value)
    eng.sem_inc(passed, 1)


def tiles_of(dram, first, n):
    return dram[bass.ds(first, n * P), :].rearrange("(t p) d -> p t d", p=P)


def row_tile(dram, parts):
    return dram.partition_broadcast(parts)


class Consts:

    def __init__(self, nc):
        self.nc, self.taken = nc, []

    def semaphore(self, name):
        self.taken.append(self.nc.alloc_semaphore(name))
        return self.taken[-1]

    def end_stage(self):
        self.nc.clear_and_free_semaphores(self.taken)
        self.nc.all_engine_barrier()
        self.taken = []


def slot_tiles(top):
    return (TOK * top + EXPERTS * (SLOTS - 1)) // SLOTS


class Kept:
    pass


def setup(nc, ctx, io):
    c = Consts(nc)

    def sb(name, shape, dt=F32):
        return ctx.enter_context(nc.sbuf_tensor(name, shape, dt))

    c.ident = sb("ident", [P, P])
    c.ones = sb("ones", [P, P])
    c.earlier = sb("earlier", [P, P])
    c.zeros = sb("zeros", [P, D])
    c.eps = sb("eps", [P, 1])
    c.gates = sb("gates", [P, 8])
    c.sel16 = sb("sel16", [P, P])
    c.half64 = sb("half64", [P, P])
    gates_loaded = c.semaphore("gates_loaded")
    consts_step = c.semaphore("consts_step")
    gates_done = c.semaphore("gates_done")
    c.cleared = nc.alloc_semaphore("cleared")
    io["slots_in"] = nc.dram_tensor("slots_in", (slot_tiles(2) * SLOTS, D), F32, kind="Internal").ap()
    io["slots_out"] = nc.dram_tensor("slots_out", (slot_tiles(2) * SLOTS, D), F32, kind="Internal").ap()
    with nc.Block() as block:
        @block.sync
        def _(sp):
            sp.dma_start(c.gates[:, 0:4], row_tile(io["g_xattn"], P)).then_inc(gates_loaded, 16)
            sp.dma_start(c.gates[:, 4:8], row_tile(io["g_ffn"], P)).then_inc(gates_loaded, 16)

        @block.gpsimd
        def _(pool):
            step = Tally(pool, consts_step)
            step.add(pool.memset(c.ident[:], 0.0))
            step.add(pool.memset(c.ones[:], 1.0))
            step.add(pool.memset(c.zeros[:], 0.0))
            step.add(pool.memset(c.earlier[:], 1.0))
            step.add(pool.memset(c.eps[:], EPS))
            step.add(pool.memset(c.sel16[:], 0.0))
            step.add(pool.memset(c.half64[:], 0.0))
            step.wait()
            step.add(pool.memset(c.half64[0:64, 0:64], 1.0))
            step.add(pool.memset(c.half64[64:128, 64:128], 1.0))
            step.wait()
            step.add(pool.affine_select(out=c.ident[:], in_=c.ident[:], compare_op=ALU.not_equal, fill=1.0,
                                        base=0, pattern=[[-1, P]], channel_multiplier=1))
            step.add(pool.affine_select(out=c.earlier[:], in_=c.earlier[:], compare_op=ALU.is_gt, fill=0.0,
                                        base=0, pattern=[[1, P]], channel_multiplier=-1))
            for j in range(4):
                step.add(pool.affine_select(out=c.sel16[:, 32 * j:32 * j + 32], in_=c.sel16[:, 32 * j:32 * j + 32],
                                            compare_op=ALU.not_equal, fill=1.0, base=-(32 * j + 16),
                                            pattern=[[0, 32]], channel_multiplier=1))
            step.wait()

        @block.scalar
        def _(act):
            act.wait_ge(gates_loaded, 32)
            nc.scalar.activation(c.gates[:], c.gates[:], ACT.Tanh).then_inc(gates_done, 1)
            act.wait_ge(gates_done, 1)
    c.end_stage()
    return c


def norm_stats(nc, dve, step, x, stats, mv, n, parts=P):
    for t in range(n):
        step.add(nc.vector.bn_stats(stats[0:parts, t, :], x[0:parts, t, :]))
    step.wait()
    for t in range(n):
        step.add(nc.vector.bn_aggr(mv[0:parts, t, :], stats[0:parts, t, :]))


def norm_apply(nc, dve, step, out, x, mv, rstd, std, n, parts=P):
    step.add(nc.vector.reciprocal(rstd[0:parts, 0:n], std[0:parts, 0:n]))
    step.wait()
    for t in range(n):
        step.add(nc.vector.tensor_scalar(out[0:parts, t, :], x[0:parts, t, :], mv[0:parts, t, 0:1],
                                         rstd[0:parts, t:t + 1], ALU.subtract, ALU.mult))


Q_TERMS = (0, 1, 2, 0, 1, 0)
K_TERMS = (0, 0, 0, 1, 1, 2)
TERM_ROWS = 16 * len(Q_TERMS)
FAR_PARTS = (-998244352.0, -1753088.0, -2560.0)


def attention16(nc, c, name, x_in, x_out, w, gate, ctx_t=None, mask=None, ln=None, twice=False, slots=None):
    H, QUADS = 16, 4
    cross = ctx_t is not None
    nk = SC if cross else S
    n_kt = 1 if cross else NT
    kw = nk if cross else P
    mask_rows = 3 if mask is not None else 0
    max_at = TERM_ROWS + mask_rows
    rows = max_at + 3
    ITEMS = 4 * n_kt
    BURSTS = ITEMS // 2
    HALVES = 2 * ITEMS
    IB, HB = QUADS * ITEMS, QUADS * HALVES
    rounds = 2 if twice else 1
    with ExitStack() as ctx:
        def sb(n, shape, dt=F32):
            return ctx.enter_context(nc.sbuf_tensor(f"{name}_{n}", shape, dt))

        def sem(n):
            return c.semaphore(f"{name}_{n}")

        scores = ctx.enter_context(nc.psum_tensor(f"{name}_scores", [P, 4, 512], F32))
        for_max = ctx.enter_context(nc.psum_tensor(f"{name}_for_max", [P, 2, 512], F32))
        pv = ctx.enter_context(nc.psum_tensor(f"{name}_pv", [P, 2, 512], F32))
        s2 = [scores[:, 2 * i:2 * i + 2, :].rearrange("p a n -> p (a n)") for i in range(2)]
        sall = scores[:].rearrange("p a n -> p (a n)")

        x, xn = sb("x", [P, NT, D]), sb("xn", [P, NT, D])
        stats, mv = sb("stats", [P, NT, 6]), sb("mv", [P, NT, 2])
        std, rstd = sb("std", [P, NT]), sb("rstd", [P, NT])
        xT = sb("xT", [P, KD, S])
        wq, wk = sb("wq", [P, KD, D]), sb("wk", [P, KD, D])
        wv, wo = sb("wv", [P, KD, 2 * D]), sb("wo", [P, QUADS, D])
        bqk, bv = sb("bqk", [P, 4]), sb("bv", [P, 2 * D])
        full, rest = sb("full", [P, S]), sb("rest", [P, S])
        parts = sb("parts", [P, 3, S], BF16)
        QS, KS = sb("QS", [rows, H, S], BF16), sb("KS", [rows, H, nk], BF16)
        V = sb("V", [P, n_kt, 2 * D])
        halves = sb("halves", [P, 2, P])
        mx = sb("mx", [P, P])
        neg, neg_parts = sb("neg", [32, 2, P]), sb("neg_parts", [32, 3, P], BF16)
        probs = sb("probs", [P, 4, S])
        raw, rsum = sb("raw", [P, CH]), sb("rsum", [P, CH])
        OT = sb("OT", [P, QUADS, S])
        if cross:
            cT, cb = sb("cT", [P, KD, B * SC]), sb("cb", [P, KD, SC])
        if mask is not None:
            mask_in, mask_b = sb("mask_in", [1, B * SC]), sb("mask_b", [1, SC], BF16)
            far = sb("far", [1, 2, S], BF16)
        if ln is not None:
            lnw = sb("lnw", [P, KD, 2])

        names = ("x_loaded cst_loaded rows_set far_placed var_ready std_ready xn_ready xt_psum xt_ready c_ready proj full_ready high_ready rest_ready "
                 "mid_ready low_ready stacked mask_ready mask_placed v_ready max_psum max_done mxt_ready mx_ready rsum_ready neg_ready max_placed s_ready "
                 "exp_done pv_done raw_ready ot_ready wo_done out_ready stored step quad_step sp_passed dve_passed").split()
        s = {n: sem(n) for n in names}
        consts = [(wq, w["q"]), (wk, w["k"]), (wv, w["v"]), (wo, w["o"]), (bqk, w["bqk"]), (bv, row_tile(w["bv"], P))]
        if cross:
            consts.append((cT, ctx_t.rearrange("(k p) n -> p k n", p=P)))
        if mask is not None:
            consts.append((mask_in, mask.rearrange("b n -> (b n)").unsqueeze(0)))
        if ln is not None:
            consts.append((lnw, ln))
        n_cst = 16 * len(consts)
        STACKS = 4
        block = ctx.enter_context(nc.Block())

        def quad_items(q):
            for h in range(2):
                for kt in range(n_kt):
                    for pair in range(2):
                        yield (h * n_kt + kt) * 2 + pair, 4 * q + 2 * pair, h, kt

        @block.sync
        def _(sp):
            for dst, src in consts:
                sp.dma_start(dst[:], src).then_inc(s["cst_loaded"], 16)
            sp.wait_ge(s["rows_set"], 2 + (2 if mask is not None else 0))
            if mask is not None:
                for i in range(2):
                    sp.dma_start(QS[TERM_ROWS + 1 + i:TERM_ROWS + 2 + i, :, :],
                                 far[:, i, :].unsqueeze(1).broadcast_to([1, H, S])).then_inc(s["far_placed"], 16)
            with sp.Fori(0, B) as b:
                first = sp.snap(b * S)
                sp.dma_start(x[:], tiles_of(x_in, first, NT)).then_inc(s["x_loaded"], 16)
                if mask is not None:
                    sp.wait_ge(s["mask_ready"], b + 1)
                    for i in range(3):
                        sp.dma_start(KS[TERM_ROWS + i:TERM_ROWS + i + 1, :, :],
                                     mask_b[:].unsqueeze(1).broadcast_to([1, H, SC])).then_inc(s["mask_placed"], 16)
                for i in range(STACKS):
                    half, key = divmod(i, 2)
                    heads = slice(8 * half, 8 * half + 8)
                    sp.wait_ge(s["low_ready"], b * STACKS + i + 1)
                    for r, term in enumerate(K_TERMS if key else Q_TERMS):
                        n = nk if key else S
                        sp.dma_start((KS if key else QS)[16 * r:16 * r + 16, heads, :], parts[:, term, 0:n]).then_inc(s["stacked"], 16)
                for q in range(QUADS):
                    sp.wait_ge(s["neg_ready"], b * QUADS + q + 1)
                    for i in range(3):
                        sp.dma_start(QS[max_at + i:max_at + i + 1, 4 * q:4 * q + 4, :], neg_parts[:, i, :]).then_inc(s["max_placed"], 16)
                sp.wait_ge(s["out_ready"], b + 2)
                sp.dma_start(tiles_of(x_out, first, NT), x[:]).then_inc(s["stored"], 16)
                pause(sp, s["stored"], b * 16 + 16, s["sp_passed"])

        @block.gpsimd
        def _(pool):
            pool.memset(KS[TERM_ROWS:rows, :, :], 1.0).then_inc(s["rows_set"], 1)
            pool.memset(QS[TERM_ROWS:rows, :, :], FAR_PARTS[0] if mask is not None else 0.0).then_inc(s["rows_set"], 1)
            if mask is not None:
                pool.memset(far[:, 0, :], FAR_PARTS[1]).then_inc(s["rows_set"], 1)
                pool.memset(far[:, 1, :], FAR_PARTS[2]).then_inc(s["rows_set"], 1)
            if slots is not None:
                pool.dma_start(slots.rearrange("(n p) d -> p n d", p=P),
                               c.zeros[:].unsqueeze(1).broadcast_to([P, slots.shape[0] // P, D])).then_inc(c.cleared, 16)

        @block.tensor
        def _(pe):
            pe.wait_ge(s["cst_loaded"], n_cst)
            with pe.Fori(0, B) as b:
                pe.wait_ge(s["xn_ready"], (b + 1) * rounds)
                pe.wait_ge(s["out_ready"], b + 1)
                for k in range(KD):
                    for t in range(NT):
                        last = nc.tensor.transpose(s2[k][:, t * P:(t + 1) * P], xn[:, t, k * P:(k + 1) * P] if not twice else x[:, t, k * P:(k + 1) * P],
                                                   c.ident[:])
                last.then_inc(s["xt_psum"], 1)
                pe.wait_ge(s["xt_ready"], b * KD + KD)
                if cross:
                    pe.wait_ge(s["c_ready"], b + 1)
                for i in range(STACKS):
                    half, key = divmod(i, 2)
                    if i >= 2:
                        pe.wait_ge(s["full_ready"], b * STACKS + i - 1)
                    src, n = (cb, SC) if key and cross else (xT, S)
                    for lo in range(0, n, CH):
                        wide = min(CH, n - lo)
                        for k in range(KD):
                            last = nc.tensor.matmul(s2[key][:, lo:lo + wide], (wk if key else wq)[:, k, half * P:(half + 1) * P],
                                                    src[:, k, lo:lo + wide], start=k == 0, stop=k == KD - 1)
                    last.then_inc(s["proj"], 1)
                for t in range(n_kt):
                    if t >= 2:
                        pe.wait_ge(s["v_ready"], b * n_kt + t - 1)
                    for k in range(KD):
                        last = nc.tensor.matmul(pv[0:kw, t % 2, :], (cb if cross else xT)[:, k, t * P:t * P + kw], wv[:, k, :],
                                                start=k == 0, stop=k == KD - 1)
                    last.then_inc(s["proj"], 1)

                def half_step(q, i):
                    n = q * HALVES + i
                    if n >= 2:
                        pe.wait_ge(s["max_done"], b * HB + n - 1)
                    if n == 0 or n == 2 * HALVES:
                        pe.wait_ge(s["stacked"], b * STACKS * 96 + (192 if n == 0 else 384))
                        if n == 0 and mask is not None:
                            pe.wait_ge(s["mask_placed"], b * 48 + 48)
                            pe.wait_ge(s["far_placed"], 32)
                        if n == 0:
                            pe.wait_ge(s["rows_set"], 2)
                    if cross:
                        h = 4 * q + i // 2
                        for t in range(4):
                            at = (i % 2 * 4 + t) * P
                            last = nc.tensor.matmul(for_max[:, i % 2, t * P:t * P + SC], QS[0:max_at, h, at:at + P], KS[0:max_at, h, :],
                                                    start=True, stop=True)
                    else:
                        h, at = 4 * q + i // 16, i % 16 // 2 * P
                        last = nc.tensor.matmul(for_max[:, i % 2, :], QS[0:max_at, h, at:at + P], KS[0:max_at, h, i % 2 * CH:i % 2 * CH + CH],
                                                start=True, stop=True)
                    last.then_inc(s["max_psum"], 1)

                def turn_max(q):
                    pe.wait_ge(s["mx_ready"], b * QUADS + q + 1)
                    nc.tensor.transpose(for_max[:, 0, 0:P], mx[:], c.ident[:]).then_inc(s["mxt_ready"], 1)

                def values(q, burst):
                    h, kt = divmod(burst, n_kt)
                    chunk = 2 * q + h
                    if kt == 0 and chunk >= 2:
                        pe.wait_ge(s["raw_ready"], b * 2 * QUADS + chunk - 1)
                    pe.wait_ge(s["exp_done"], b * IB + q * ITEMS + 2 * burst + 2)
                    for j in range(4):
                        col = 32 * (4 * q + j)
                        last = nc.tensor.matmul(pv[32 * j:32 * j + 32, h, :], V[0:kw, kt, col:col + 32],
                                                probs[0:kw, (2 * burst + j // 2) % 4, j % 2 * CH:j % 2 * CH + CH],
                                                start=kt == 0, stop=kt == n_kt - 1, tile_position=(0, 32 * j))
                    last.then_inc(s["pv_done"], 1)

                for i in range(HALVES):
                    half_step(0, i)
                turn_max(0)
                pe.wait_ge(s["v_ready"], b * n_kt + n_kt)
                for q in range(QUADS):
                    pe.wait_ge(s["max_placed"], b * QUADS * 48 + q * 48 + 48)
                    for i, h0, h, kt in quad_items(q):
                        if q + 1 < QUADS:
                            half_step(q + 1, 2 * i)
                        n = q * ITEMS + i
                        if n >= 2:
                            pe.wait_ge(s["exp_done"], b * IB + n - 1)
                        for j in range(2):
                            last = nc.tensor.matmul(s2[i % 2][0:kw, j * CH:(j + 1) * CH], KS[:, h0 + j, kt * P:kt * P + kw],
                                                    QS[:, h0 + j, h * CH:(h + 1) * CH], start=True, stop=True)
                        last.then_inc(s["s_ready"], 1)
                        if q + 1 < QUADS:
                            half_step(q + 1, 2 * i + 1)
                        if i >= 2 and i % 2 == 0:
                            values(q, i // 2 - 1)
                    if q + 1 < QUADS:
                        turn_max(q + 1)
                    values(q, BURSTS - 1)
                pe.wait_ge(s["ot_ready"], b * 2 * QUADS + 2 * QUADS)
                for t in range(NT):
                    for q in range(QUADS):
                        last = nc.tensor.matmul(sall[:, t * D:(t + 1) * D], OT[:, q, t * P:(t + 1) * P], wo[:, q, :],
                                                start=q == 0, stop=q == QUADS - 1)
                last.then_inc(s["wo_done"], 1)

        @block.scalar
        def _(act):
            act.wait_ge(s["cst_loaded"], n_cst)
            with act.Fori(0, B) as b:
                if cross:
                    nc.scalar.activation(cb[:], cT[:, :, bass.ds(b * SC, SC)], ACT.Copy).then_inc(s["c_ready"], 1)
                for r in range(rounds):
                    act.wait_ge(s["var_ready"], b * rounds + r + 1)
                    nc.scalar.activation(std[:], mv[:, :, 1], ACT.Sqrt, bias=c.eps[:, 0:1]).then_inc(s["std_ready"], 1)
                act.wait_ge(s["xt_psum"], b + 1)
                for k in range(KD):
                    if ln is not None:
                        ins = nc.scalar.activation(xT[:, k, :], s2[k], ACT.Identity, bias=lnw[:, k, 1:2], scale=lnw[:, k, 0:1])
                    else:
                        ins = nc.scalar.activation(xT[:, k, :], s2[k], ACT.Copy)
                    ins.then_inc(s["xt_ready"], 1)
                for i in range(STACKS):
                    n = nk if i % 2 else S
                    u = b * STACKS + i
                    act.wait_ge(s["full_ready"], u + 1)
                    if i >= 1:
                        act.wait_ge(s["stacked"], b * STACKS * 96 + 96 * i)
                    nc.scalar.activation(parts[:, 0, 0:n], full[:, 0:n], ACT.Copy).then_inc(s["high_ready"], 1)
                    act.wait_ge(s["rest_ready"], u + 1)
                    nc.scalar.activation(parts[:, 1, 0:n], rest[:, 0:n], ACT.Copy).then_inc(s["mid_ready"], 1)
                for n in range(IB):
                    i = n % ITEMS
                    act.wait_ge(s["s_ready"], b * IB + n + 1)
                    if n >= 4:
                        act.wait_ge(s["pv_done"], b * QUADS * BURSTS + n // 2 - 1)
                    nc.scalar.activation(probs[0:kw, i % 4, :], s2[i % 2][0:kw, :], ACT.Exp).then_inc(s["exp_done"], 1)

        @block.vector
        def _(dve):
            dve.memset(mx[:], 0.0).then_inc(s["out_ready"], 1)
            dve.wait_ge(s["cst_loaded"], n_cst)
            with dve.Fori(0, B) as b:
                step = Tally(dve, s["step"], rounds * (3 * NT - 1), b)
                if mask is not None:
                    nc.vector.tensor_copy(mask_b[:], mask_in[:, bass.ds(b * SC, SC)]).then_inc(s["mask_ready"], 1)
                dve.wait_ge(s["x_loaded"], b * 16 + 16)
                for r in range(rounds):
                    src, dst = ((x, xn), (xn, x))[r]
                    for t in range(NT):
                        step.add(nc.vector.bn_stats(stats[:, t, :], src[:, t, :]))
                    step.wait(s["dve_passed"])
                    for t in range(NT):
                        ins = nc.vector.bn_aggr(mv[:, t, :], stats[:, t, :])
                        if t < NT - 1:
                            step.add(ins)
                    ins.then_inc(s["var_ready"], 1)
                    dve.wait_ge(s["std_ready"], b * rounds + r + 1)
                    step.add(nc.vector.reciprocal(rstd[:], std[:]))
                    step.wait()
                    for t in range(NT):
                        ins = nc.vector.tensor_scalar(dst[:, t, :], src[:, t, :], mv[:, t, 0:1], rstd[:, t:t + 1],
                                                      ALU.subtract, ALU.mult)
                        if t < NT - 1:
                            step.add(ins)
                    ins.then_inc(s["xn_ready"], 1)
                    if r < rounds - 1:
                        dve.wait_ge(s["xn_ready"], b * rounds + r + 1)
                step.close()
                for i in range(STACKS):
                    half, key = divmod(i, 2)
                    n = nk if key else S
                    u = b * STACKS + i
                    dve.wait_ge(s["proj"], b * (STACKS + n_kt) + i + 1)
                    if i >= 1:
                        dve.wait_ge(s["low_ready"], u)
                    bias = bqk[:, 2 * key + half:2 * key + half + 1]
                    nc.vector.tensor_scalar(full[:, 0:n], s2[key][:, 0:n], bias, 1.0 if key else 0.25, ALU.add, ALU.mult).then_inc(s["full_ready"], 1)
                    dve.wait_ge(s["full_ready"], u + 1)
                    dve.wait_ge(s["high_ready"], u + 1)
                    nc.vector.tensor_tensor(rest[:, 0:n], full[:, 0:n], parts[:, 0, 0:n], ALU.subtract).then_inc(s["rest_ready"], 1)
                    dve.wait_ge(s["mid_ready"], u + 1)
                    dve.wait_ge(s["rest_ready"], u + 1)
                    nc.vector.tensor_tensor(parts[:, 2, 0:n], rest[:, 0:n], parts[:, 1, 0:n], ALU.subtract).then_inc(s["low_ready"], 1)
                for t in range(n_kt):
                    dve.wait_ge(s["proj"], b * (STACKS + n_kt) + STACKS + t + 1)
                    nc.vector.tensor_tensor(V[0:kw, t, :], pv[0:kw, t % 2, :], bv[0:kw, :], ALU.add).then_inc(s["v_ready"], 1)

                turn = Tally(dve, s["quad_step"], QUADS * 6, b)

                def half_step(q, i):
                    dve.wait_ge(s["max_psum"], b * HB + q * HALVES + i + 1)
                    if cross:
                        ins = nc.vector.tensor_reduce(mx[:, 4 * i:4 * i + 4], for_max[:, i % 2, :].rearrange("p (t n) -> p t n", t=4)[:, :, 0:SC],
                                                      AX.X, ALU.max)
                    else:
                        ins = nc.vector.tensor_reduce(halves[:, i % 2, i // 2:i // 2 + 1], for_max[:, i % 2, :], AX.X, ALU.max)
                    ins.then_inc(s["max_done"], 1)

                def negate(q):
                    dve.wait_ge(s["max_done"], b * HB + (q + 1) * HALVES)
                    if cross:
                        dve.sem_inc(s["mx_ready"], 1)
                    else:
                        nc.vector.tensor_tensor(mx[:, 0:32], halves[:, 0, 0:32], halves[:, 1, 0:32], ALU.max).then_inc(s["mx_ready"], 1)
                    dve.wait_ge(s["mxt_ready"], b * QUADS + q + 1)
                    if q >= 1:
                        dve.wait_ge(s["max_placed"], b * QUADS * 48 + q * 48)
                    turn.add(nc.vector.tensor_scalar(neg[:, 0, :], for_max[0:32, 0, 0:P], -1.0, None, ALU.mult))
                    turn.wait()
                    turn.add(nc.vector.tensor_copy(neg_parts[:, 0, :], neg[:, 0, :]))
                    turn.wait()
                    turn.add(nc.vector.tensor_tensor(neg[:, 1, :], neg[:, 0, :], neg_parts[:, 0, :], ALU.subtract))
                    turn.wait()
                    turn.add(nc.vector.tensor_copy(neg_parts[:, 1, :], neg[:, 1, :]))
                    turn.wait()
                    nc.vector.tensor_tensor(neg_parts[:, 2, :], neg[:, 1, :], neg_parts[:, 1, :], ALU.subtract).then_inc(s["neg_ready"], 1)

                def norm_heads(q, h):
                    chunk = 2 * q + h
                    dve.wait_ge(s["pv_done"], b * QUADS * BURSTS + q * BURSTS + (h + 1) * n_kt)
                    if chunk >= 1:
                        dve.wait_ge(s["ot_ready"], b * 2 * QUADS + chunk)
                    nc.vector.tensor_copy(raw[:], pv[:, h, :]).then_inc(s["raw_ready"], 1)
                    pause(dve, s["raw_ready"], b * 2 * QUADS + chunk + 1, s["dve_passed"])
                    turn.add(nc.vector.stream_shuffle(rsum[:], raw[:], [16] * 32))
                    turn.wait()
                    nc.vector.reciprocal(rsum[:], rsum[:]).then_inc(s["rsum_ready"], 1)
                    dve.wait_ge(s["rsum_ready"], b * 2 * QUADS + chunk + 1)
                    nc.vector.tensor_tensor(OT[:, q, h * CH:(h + 1) * CH], raw[:], rsum[:], ALU.mult).then_inc(s["ot_ready"], 1)

                for i in range(HALVES):
                    half_step(0, i)
                negate(0)
                for q in range(QUADS):
                    for i in range(HALVES):
                        if q + 1 < QUADS:
                            half_step(q + 1, i)
                        if i == HALVES // 2 + HALVES // 8:
                            norm_heads(q, 0)
                    if q + 1 < QUADS:
                        negate(q + 1)
                    norm_heads(q, 1)
                turn.close()
                dve.wait_ge(s["wo_done"], b + 1)
                base = xn if twice else x
                xf, bf = x[:].rearrange("p t d -> p (t d)"), base[:].rearrange("p t d -> p (t d)")
                if gate is None:
                    ins = nc.vector.tensor_tensor(xf, sall, bf, ALU.add)
                else:
                    ins = nc.vector.scalar_tensor_tensor(xf, sall, c.gates[:, gate:gate + 1], bf, ALU.mult, ALU.add)
                ins.then_inc(s["out_ready"], 1)




def attention64(nc, c, name, x_in, x_out, w_qkv, w_o, gate, ctx_in, mask, ln, rms=None, out_ln=None, out_b=None):
    HG = 4
    G = w_qkv.shape[0] // B
    n_keys = S + SC
    n_kt = NT + 1
    M = HG * n_kt
    n_max = HG * NT
    with ExitStack() as ctx:
        def sb(n, shape, dt=F32):
            return ctx.enter_context(nc.sbuf_tensor(f"{name}_{n}", shape, dt))

        def sem(n):
            return c.semaphore(f"{name}_{n}")

        scores = ctx.enter_context(nc.psum_tensor(f"{name}_scores", [P, 4, 512], F32))
        out_ps = ctx.enter_context(nc.psum_tensor(f"{name}_out_ps", [P, 4, 512], F32))
        s2 = [scores[:, 2 * i:2 * i + 2, :].rearrange("p a n -> p (a n)") for i in range(2)]
        o2 = [out_ps[:, 2 * i:2 * i + 2, :].rearrange("p a n -> p (a n)") for i in range(2)]
        sall = scores[:].rearrange("p a n -> p (a n)")

        x = sb("x", [P, NT, D])
        xn = sb("xn", [P, NT, D])
        cx = sb("cx", [SC, 1, D])
        stats, mv = sb("stats", [P, NT, 6]), sb("mv", [P, NT, 2])
        std, rstd = sb("std", [P, NT]), sb("rstd", [P, NT])
        lT = sb("lT", [P, KD, S])
        cT = sb("cT", [P, KD, SC])
        lnw = sb("lnw", [P, KD, 4])
        acc = sb("acc", [P, NT, D])
        accf = acc[:].rearrange("p t d -> p (t d)")
        qkv = sb("qkv", [P, 3, KD, D])
        wo = sb("wo", [P, 2, D])
        Q = [sb(f"Q{h}", [66, S]) for h in range(HG)]
        K = [sb(f"K{h}", [66, n_keys]) for h in range(HG)]
        Qb = [sb(f"Qb{h}", [65, S], BF16) for h in range(HG)]
        Kb = [sb(f"Kb{h}", [65, n_keys], BF16) for h in range(HG)]
        V = sb("V", [P, n_kt, HG, P])
        mx, mxc = sb("mx", [P, P]), sb("mxc", [P, P])
        neg = sb("neg", [HG * NT, P])
        probs = sb("probs", [P, 2, S])
        rsum = sb("rsum", [P, S])
        OT = [sb(f"OT{i}", [P, S]) for i in range(2)]
        mask_in = sb("mask_in", [1, SC], U8)
        mrow = sb("mrow", [1, n_keys])
        if rms is not None:
            gam = sb("gam", [P, 2])
            sq = sb("sq", [P, S])
        if out_ln is not None:
            og, ob = sb("og", [P, D]), sb("ob", [P, D])
        if out_b is not None:
            ob = sb("ob", [P, D])

        names = ("x_loaded c_loaded cst_loaded mask_loaded mask_placed w_loaded wo_loaded var_ready std_ready xn_ready "
                 "xt_psum xt_ready proj evacuated qb_ready kb_ready sq_ready sumsq norm_ready root_ready v_ready "
                 "smax_ready max_done mxt_ready neg_ready max_placed s_ready exp_done pv_done head_ready wo_done "
                 "acc_added out_ready stored dve_step rec_done sp_passed dve_passed act_passed pool_passed pool_step mrow_ready "
                 "dve_tail tail_var tail_std")
        s = {n: sem(n) for n in names.split()}
        n_cst = 1 + (rms is not None) + 2 * (out_ln is not None) + (out_b is not None)
        n_proj = 5

        block = ctx.enter_context(nc.Block())

        @block.sync
        def _(sp):
            sp.dma_start(lnw[:], ln).then_inc(s["cst_loaded"], 16)
            if rms is not None:
                sp.dma_start(gam[:], rms).then_inc(s["cst_loaded"], 16)
            if out_ln is not None:
                sp.dma_start(og[:], row_tile(out_ln[0], P)).then_inc(s["cst_loaded"], 16)
                sp.dma_start(ob[:], row_tile(out_ln[1], P)).then_inc(s["cst_loaded"], 16)
            if out_b is not None:
                sp.dma_start(ob[:], row_tile(out_b, P)).then_inc(s["cst_loaded"], 16)
            sp.wait_ge(s["pool_step"], 2 + 2 * HG + 1)
            with sp.Fori(0, B) as b:
                first = sp.snap(b * S)
                first_c = sp.snap(b * SC)
                sp.dma_start(x[:], tiles_of(x_in, first, NT)).then_inc(s["x_loaded"], 16)
                sp.dma_start(cx[:, 0, :], ctx_in[bass.ds(first_c, SC), :]).then_inc(s["c_loaded"], 16)
                sp.dma_start(mask_in[:], mask[bass.ds(b, 1), :]).then_inc(s["mask_loaded"], 16)
                sp.wait_ge(s["mrow_ready"], b + 1)
                for h in range(HG):
                    sp.dma_start(K[h][64:65, :], mrow[:]).then_inc(s["mask_placed"], 16)
                with sp.Fori(0, G) as g:
                    sp.wait_ge(s["neg_ready"], b * G + g + 1)
                    for h in range(HG):
                        sp.dma_start(Q[h][65:66, :], neg[NT * h:NT * h + NT, :]).then_inc(s["max_placed"], 16)
                sp.wait_ge(s["out_ready"], b + 1)
                sp.dma_start(tiles_of(x_out, first, NT), x[:]).then_inc(s["stored"], 16)
                pause(sp, s["stored"], b * 16 + 16, s["sp_passed"])

        @block.gpsimd
        def _(pool):
            pool.dma_start(qkv[:], w_qkv[0]).then_inc(s["w_loaded"], 16)
            pool.dma_start(wo[:], w_o[0]).then_inc(s["wo_loaded"], 16)
            step = Tally(pool, s["pool_step"])
            step.add(pool.memset(V[:], 1.0))
            step.add(pool.memset(mrow[:], 0.0))
            step.wait()
            for h in range(HG):
                step.add(pool.memset(Q[h][64:66, :], -1e30))
                step.add(pool.memset(K[h][64:66, :], 1.0))
            step.wait()
            step.add(pool.memset(mxc[:], 0.0))
            if B * G > 1:
                with pool.Fori(0, B * G - 1) as i:
                    nxt = pool.snap(i + 1)
                    pool.wait_ge(s["proj"], i * n_proj + n_proj)
                    pool.dma_start(qkv[:], w_qkv[bass.ds(nxt, 1)].rearrange("o p a k d -> (o p) a k d")).then_inc(s["w_loaded"], 16)
                    pool.wait_ge(s["wo_done"], i + 1)
                    pool.dma_start(wo[:], w_o[bass.ds(nxt, 1)].rearrange("o p k d -> (o p) k d")).then_inc(s["wo_loaded"], 16)

        @block.tensor
        def _(pe):
            with pe.Fori(0, B) as b:
                pe.wait_ge(s["xn_ready"], b * 3 + 3)
                pe.wait_ge(s["acc_added"], b * G + 1)
                for k in range(KD):
                    for t in range(NT):
                        last = nc.tensor.transpose(s2[k][:, t * P:(t + 1) * P], xn[:, t, k * P:(k + 1) * P], c.ident[:])
                    last = nc.tensor.transpose(out_ps[:, k, 0:SC], cx[:, 0, k * P:(k + 1) * P], c.ident[0:SC, 0:SC])
                last.then_inc(s["xt_psum"], 1)
                with pe.Fori(0, G) as g:
                    it = pe.snap(b * G + g)
                    ev = it * 5
                    pe.wait_ge(s["xt_ready"], b * 4 + 4)
                    pe.wait_ge(s["w_loaded"], it * 16 + 16)
                    pe.wait_ge(s["acc_added"], it + 1)
                    for i in range(2):
                        for hp in range(2):
                            n = 2 * i + hp
                            if i == 1:
                                pe.wait_ge(s["evacuated"], ev + hp + 1)
                            for h in range(2):
                                for k in range(KD):
                                    last = nc.tensor.matmul(s2[hp][:, h * CH:(h + 1) * CH], qkv[:, i, k, hp * P:(hp + 1) * P],
                                                            lT[:, k, h * CH:(h + 1) * CH], start=k == 0, stop=k == KD - 1)
                            if i == 1:
                                for k in range(KD):
                                    last = nc.tensor.matmul(out_ps[:, 2 + hp, 0:SC], qkv[:, i, k, hp * P:(hp + 1) * P],
                                                            cT[:, k, :], start=k == 0, stop=k == KD - 1)
                            last.then_inc(s["proj"], 1)
                            if rms is not None:
                                pe.wait_ge(s["sq_ready"], it * 6 + (n + 1 if i == 0 else 2 * hp + 3))
                                if n >= 1:
                                    pe.wait_ge(s["root_ready"], it * 6 + (n if n <= 2 else 4))
                                for h in range(2):
                                    last = nc.tensor.matmul(o2[0][:, h * CH:(h + 1) * CH], c.half64[:], sq[:, h * CH:(h + 1) * CH],
                                                            start=True, stop=True)
                                last.then_inc(s["sumsq"], 1)
                                if i == 1:
                                    pe.wait_ge(s["sq_ready"], it * 6 + 2 * hp + 4)
                                    pe.wait_ge(s["root_ready"], it * 6 + 2 * hp + 3)
                                    nc.tensor.matmul(o2[0][:, 0:SC], c.half64[:], sq[:, 0:SC],
                                                     start=True, stop=True).then_inc(s["sumsq"], 1)
                    pe.wait_ge(s["evacuated"], ev + 4)
                    for t in range(NT):
                        for k in range(KD):
                            last = nc.tensor.matmul(sall[:, t * D:(t + 1) * D], lT[:, k, t * P:(t + 1) * P], qkv[:, 2, k, :],
                                                    start=k == 0, stop=k == KD - 1)
                    for k in range(KD):
                        last = nc.tensor.matmul(out_ps[0:SC, 2, 0:D], cT[:, k, :], qkv[:, 2, k, :], start=k == 0, stop=k == KD - 1)
                    last.then_inc(s["proj"], 1)
                    pe.wait_ge(s["evacuated"], ev + 5)
                    pe.wait_ge(s["qb_ready"], it * HG + HG)
                    pe.wait_ge(s["kb_ready"], it * HG + HG)
                    for n in range(n_max):
                        h, t = divmod(n, NT)
                        if n >= 2:
                            pe.wait_ge(s["max_done"], it * n_max + n - 1)
                        for j in range(2):
                            nc.tensor.matmul(s2[n % 2][:, j * CH:(j + 1) * CH], Qb[h][:, t * P:(t + 1) * P],
                                             Kb[h][:, j * CH:(j + 1) * CH], start=True, stop=True)
                        nc.tensor.matmul(out_ps[:, n % 2, 0:SC], Qb[h][:, t * P:(t + 1) * P], Kb[h][:, S:n_keys],
                                         start=True, stop=True).then_inc(s["smax_ready"], 1)
                    pe.wait_ge(s["rec_done"], it * (HG + 1) + 1)
                    nc.tensor.transpose(out_ps[:, 2, 0:P], mx[:], c.ident[:]).then_inc(s["mxt_ready"], 1)
                    pe.wait_ge(s["max_placed"], it * 16 * HG + 16 * HG)
                    pe.wait_ge(s["mask_placed"], b * 16 * HG + 16 * HG)

                    def values(m):
                        h, kt = divmod(m, n_kt)
                        kw = P if kt < NT else SC
                        if kt == 0 and h >= 2:
                            pe.wait_ge(s["head_ready"], it * HG + h - 1)
                        pe.wait_ge(s["exp_done"], it * M + m + 1)
                        for j in range(2):
                            last = nc.tensor.matmul(o2[h % 2][:, j * CH:(j + 1) * CH], V[0:kw, kt, h, :],
                                                    probs[0:kw, m % 2, j * CH:(j + 1) * CH], start=kt == 0, stop=kt == n_kt - 1)
                        last.then_inc(s["pv_done"], 1)

                    for m in range(M):
                        h, kt = divmod(m, n_kt)
                        kw = P if kt < NT else SC
                        if m >= 2:
                            pe.wait_ge(s["exp_done"], it * M + m - 1)
                        for j in range(2):
                            last = nc.tensor.matmul(s2[m % 2][0:kw, j * CH:(j + 1) * CH], K[h][:, kt * P:kt * P + kw],
                                                    Q[h][:, j * CH:(j + 1) * CH], start=True, stop=True)
                        last.then_inc(s["s_ready"], 1)
                        if m >= 1:
                            values(m - 1)
                    values(M - 1)
                    pe.wait_ge(s["head_ready"], it * HG + HG)
                    pe.wait_ge(s["wo_loaded"], it * 16 + 16)
                    for t in range(NT):
                        for k in range(2):
                            last = nc.tensor.matmul(sall[:, t * D:(t + 1) * D], OT[k][:, t * P:(t + 1) * P], wo[:, k, :],
                                                    start=k == 0, stop=k == 1)
                    last.then_inc(s["wo_done"], 1)

        @block.scalar
        def _(act):
            act.wait_ge(s["cst_loaded"], 16 * n_cst)
            act.wait_ge(s["pool_step"], 2 + 2 * HG)
            with act.Fori(0, B) as b:
                act.wait_ge(s["var_ready"], b * 3 + 1)
                nc.scalar.activation(std[0:SC, 0:1], mv[0:SC, 0:1, 1], ACT.Sqrt, bias=c.eps[0:SC, 0:1]).then_inc(s["std_ready"], 1)
                for r in range(2):
                    act.wait_ge(s["var_ready"], b * 3 + 2 + r)
                    nc.scalar.activation(std[:], mv[:, :, 1], ACT.Sqrt, bias=c.eps[:, 0:1]).then_inc(s["std_ready"], 1)
                act.wait_ge(s["xt_psum"], b + 1)
                for k in range(KD):
                    nc.scalar.activation(lT[:, k, :], s2[k], ACT.Identity, bias=lnw[:, k, 1:2], scale=lnw[:, k, 0:1]).then_inc(s["xt_ready"], 1)
                    nc.scalar.activation(cT[:, k, :], out_ps[:, k, 0:SC], ACT.Identity, bias=lnw[:, k, 3:4],
                                         scale=lnw[:, k, 2:3]).then_inc(s["xt_ready"], 1)
                with act.Fori(0, G) as g:
                    it = act.snap(b * G + g)
                    for n in range(4):
                        i, hp = divmod(n, 2)
                        dst = (Q, K)[i]
                        act.wait_ge(s["proj"], it * n_proj + n + 1)
                        if rms is None:
                            for e in range(2):
                                r = slice(64 * e, 64 * e + 64)
                                ins = nc.scalar.activation(dst[2 * hp + e][0:64, 0:S], s2[hp][r, :], ACT.Copy, scale=0.125 if i == 0 else 1.0)
                                if i == 1:
                                    ins = nc.scalar.activation(dst[2 * hp + e][0:64, S:n_keys], out_ps[r, 2 + hp, 0:SC], ACT.Copy)
                            ins.then_inc(s["evacuated"], 1)
                        else:
                            first = n + 1 if i == 0 else 2 * hp + 3
                            if n >= 1:
                                act.wait_ge(s["sumsq"], it * 6 + first - 1)
                            nc.scalar.activation(sq[:], s2[hp], ACT.Square).then_inc(s["sq_ready"], 1)
                            act.wait_ge(s["sumsq"], it * 6 + first)
                            if n >= 1:
                                act.wait_ge(s["norm_ready"], it * 6 + first - 1)
                            nc.scalar.activation(rsum[:], o2[0], ACT.Sqrt).then_inc(s["root_ready"], 1)
                            if i == 1:
                                nc.scalar.activation(sq[:, 0:SC], out_ps[:, 2 + hp, 0:SC], ACT.Square).then_inc(s["sq_ready"], 1)
                                act.wait_ge(s["sumsq"], it * 6 + first + 1)
                                act.wait_ge(s["norm_ready"], it * 6 + first)
                                nc.scalar.activation(rsum[:, 0:SC], o2[0][:, 0:SC], ACT.Sqrt).then_inc(s["root_ready"], 1)
                    act.wait_ge(s["proj"], it * n_proj + 5)
                    v5 = V[:].rearrange("p t (a e) n -> p t a e n", e=2)
                    p4 = sall.rearrange("p (t a e n) -> p t a e n", t=NT, a=2, e=2)
                    c4 = out_ps[0:SC, 2, 0:D].rearrange("p (a e n) -> p a e n", a=2, e=2)
                    for e in range(2):
                        cols = slice(64 * e, 64 * e + 64)
                        nc.scalar.activation(v5[0:SC, NT, :, e, cols], c4[:, :, e, :], ACT.Copy)
                        ins = nc.scalar.activation(v5[:, 0:NT, :, e, cols], p4[:, :, :, e, :], ACT.Copy)
                    ins.then_inc(s["evacuated" if rms is None else "v_ready"], 1)
                    for h in range(HG):
                        act.wait_ge(s["evacuated"], it * 5 + 3 + h // 2)
                        if h == 0:
                            act.wait_ge(s["mask_placed"], b * 16 * HG + 16 * HG)
                        nc.scalar.activation(Kb[h][:], K[h][0:65, :], ACT.Copy).then_inc(s["kb_ready"], 1)
                    for m in range(M):
                        kw = P if m % n_kt < NT else SC
                        act.wait_ge(s["s_ready"], it * M + m + 1)
                        if m >= 2:
                            act.wait_ge(s["pv_done"], it * M + m - 1)
                        nc.scalar.activation(probs[0:kw, m % 2, :], s2[m % 2][0:kw, :], ACT.Exp).then_inc(s["exp_done"], 1)
                if out_ln is not None:
                    act.wait_ge(s["tail_var"], b + 1)
                    nc.scalar.activation(std[:], mv[:, :, 1], ACT.Sqrt, bias=c.eps[:, 0:1]).then_inc(s["tail_std"], 1)

        @block.vector
        def _(dve):
            dve.memset(mx[:], 0.0).then_inc(s["acc_added"], 1)
            dve.wait_ge(s["cst_loaded"], 16 * n_cst)
            dve.wait_ge(s["pool_step"], 2 + 2 * HG + 1)
            with dve.Fori(0, B) as b:
                def norm(src, dst, n, parts, r, step):
                    for t in range(n):
                        step.add(nc.vector.bn_stats(stats[0:parts, t, :], src[0:parts, t, :]))
                    step.wait(s["dve_passed"])
                    for t in range(n):
                        ins = nc.vector.bn_aggr(mv[0:parts, t, :], stats[0:parts, t, :])
                        if t < n - 1:
                            step.add(ins)
                    ins.then_inc(s["var_ready"], 1)
                    dve.wait_ge(s["std_ready"], b * 3 + r + 1)
                    step.add(nc.vector.reciprocal(rstd[0:parts, 0:n], std[0:parts, 0:n]))
                    step.wait()
                    for t in range(n):
                        ins = nc.vector.tensor_scalar(dst[0:parts, t, :], src[0:parts, t, :], mv[0:parts, t, 0:1],
                                                      rstd[0:parts, t:t + 1], ALU.subtract, ALU.mult)
                        if t < n - 1:
                            step.add(ins)
                    ins.then_inc(s["xn_ready"], 1)
                    if r == 1:
                        dve.wait_ge(s["xn_ready"], b * 3 + r + 1)

                per = 1 + 2 + 2 * (3 * NT - 1)
                step = Tally(dve, s["dve_step"], per, b)
                dve.wait_ge(s["mask_loaded"], b * 16 + 16)
                nc.vector.tensor_scalar(mrow[:, S:n_keys], mask_in[:], -1.0, 1.0, ALU.mult, ALU.add).then_inc(s["mrow_ready"], 1)
                dve.wait_ge(s["x_loaded"], b * 16 + 16)
                step.add(nc.vector.memset(accf, 0.0))
                dve.wait_ge(s["c_loaded"], b * 16 + 16)
                norm(cx, cx, 1, SC, 0, step)
                norm(x, xn, NT, P, 1, step)
                norm(xn, xn, NT, P, 2, step)
                step.close()
                with dve.Fori(0, G) as g:
                    it = dve.snap(b * G + g)
                    if rms is not None:
                        turn = Tally(dve, s["dve_tail"], 12, it)
                        for n in range(4):
                            i, hp = divmod(n, 2)
                            first = n + 1 if i == 0 else 2 * hp + 3
                            parts = [(0, S, s2[hp])] if i == 0 else [(0, S, s2[hp]), (S, SC, out_ps[:, 2 + hp, 0:SC])]
                            for j, (lo, w, ps) in enumerate(parts):
                                dve.wait_ge(s["root_ready"], it * 6 + first + j)
                                turn.add(nc.vector.tensor_scalar(rsum[:, 0:w], rsum[:, 0:w], 0.125 if i else 1.0, 1e-8 if i else 8e-8,
                                                                 ALU.mult, ALU.max))
                                turn.wait()
                                turn.add(nc.vector.reciprocal(rsum[:, 0:w], rsum[:, 0:w]))
                                turn.wait()
                                for e in range(2):
                                    r = slice(64 * e, 64 * e + 64)
                                    ins = nc.vector.scalar_tensor_tensor((Q, K)[i][2 * hp + e][0:64, lo:lo + w], ps[r, :], gam[r, i:i + 1],
                                                                         rsum[r, 0:w], ALU.mult, ALU.mult)
                                ins.then_inc(s["norm_ready"], 1)
                            dve.wait_ge(s["norm_ready"], it * 6 + first + len(parts) - 1)
                            dve.sem_inc(s["evacuated"], 1)
                        turn.close()
                        pause(dve, s["v_ready"], it + 1, s["evacuated"])
                    for h in range(HG):
                        dve.wait_ge(s["evacuated"], it * 5 + 1 + h // 2)
                        nc.vector.tensor_copy(Qb[h][:], Q[h][0:65, :]).then_inc(s["qb_ready"], 1)
                    for n in range(n_max):
                        dve.wait_ge(s["smax_ready"], it * n_max + n + 1)
                        nc.vector.tensor_reduce(mxc[:, n:n + 1], out_ps[:, n % 2, 0:SC], AX.X, ALU.max)
                        nc.vector.tensor_reduce(mx[:, n:n + 1], s2[n % 2], AX.X, ALU.max).then_inc(s["max_done"], 1)
                        if n == n_max - 1:
                            dve.wait_ge(s["max_done"], it * n_max + n + 1)
                    nc.vector.tensor_tensor(mx[:, 0:n_max], mx[:, 0:n_max], mxc[:, 0:n_max], ALU.max).then_inc(s["rec_done"], 1)
                    dve.wait_ge(s["mxt_ready"], it + 1)
                    nc.vector.tensor_scalar(neg[:], out_ps[0:n_max, 2, 0:P], -1.0, None, ALU.mult).then_inc(s["neg_ready"], 1)
                    for h in range(HG):
                        out_r, sum_r = slice(64 * (h % 2), 64 * (h % 2) + 64), slice(64 - 64 * (h % 2), 128 - 64 * (h % 2))
                        dve.wait_ge(s["pv_done"], it * M + n_kt * (h + 1))
                        nc.vector.reciprocal(rsum[out_r, :], o2[h % 2][sum_r, :]).then_inc(s["rec_done"], 1)
                        dve.wait_ge(s["rec_done"], it * (HG + 1) + h + 2)
                        nc.vector.tensor_tensor(OT[h // 2][out_r, :], o2[h % 2][out_r, :], rsum[out_r, :], ALU.mult).then_inc(s["head_ready"], 1)
                    dve.wait_ge(s["wo_done"], it + 1)
                    dve.wait_ge(s["acc_added"], it + 1)
                    nc.vector.tensor_tensor(accf, accf, sall, ALU.add).then_inc(s["acc_added"], 1)
                gate_col = c.gates[:, gate:gate + 1]
                dve.wait_ge(s["acc_added"], b * G + G + 1)
                tail = Tally(dve, s["root_ready"] if rms is None else s["tail_var"], (5 * NT) if out_ln is not None else NT, b)
                if out_ln is not None:
                    for t in range(NT):
                        tail.add(nc.vector.bn_stats(stats[:, t, :], acc[:, t, :]))
                    tail.wait(s["dve_passed"])
                    for t in range(NT):
                        ins = nc.vector.bn_aggr(mv[:, t, :], stats[:, t, :])
                        if t < NT - 1:
                            tail.add(ins)
                    ins.then_inc(s["tail_var"], 1)
                    dve.wait_ge(s["tail_std"], b + 1)
                    tail.add(nc.vector.reciprocal(rstd[:], std[:]))
                    tail.wait()
                    for t in range(NT):
                        tail.add(nc.vector.tensor_scalar(acc[:, t, :], acc[:, t, :], mv[:, t, 0:1], rstd[:, t:t + 1],
                                                         ALU.subtract, ALU.mult))
                    tail.wait()
                    for t in range(NT):
                        tail.add(nc.vector.tensor_tensor(acc[:, t, :], acc[:, t, :], og[:], ALU.mult))
                    tail.wait()
                for t in range(NT):
                    tail.add(nc.vector.tensor_tensor(acc[:, t, :], acc[:, t, :], ob[:], ALU.add))
                tail.wait()
                tail.close()
                nc.vector.scalar_tensor_tensor(x[:].rearrange("p t d -> p (t d)"), accf, gate_col,
                                               x[:].rearrange("p t d -> p (t d)"), ALU.mult, ALU.add).then_inc(s["out_ready"], 1)


def normed(nc, ctx, c, name, x_in, mode="plain", ln=None, outs=(), token=None, keep_xn=False):
    keep = Kept()

    def sb(n, shape, dt=F32):
        return ctx.enter_context(nc.sbuf_tensor(f"{name}_{n}", shape, dt))

    keep.x = x = sb("x", [P, TT, D])
    with ExitStack() as inner:
        def tmp(n, shape, dt=F32):
            return inner.enter_context(nc.sbuf_tensor(f"{name}_{n}", shape, dt))

        def sem(n):
            return c.semaphore(f"{name}_{n}")

        if mode == "rms":
            keep.route = sb("route", [P, TT])
        if mode == "quant":
            keep.step_size = sb("step_size", [P, TT])
        xn = keep.xn = (sb if keep_xn else tmp)("xn", [P, TT, D])
        work = tmp("work", [P, CT, D])
        stats, mv = tmp("stats", [P, TT, 6]), tmp("mv", [P, TT, 2])
        std, rstd = tmp("std", [P, TT]), tmp("rstd", [P, TT])
        size, scale = tmp("size", [P, TT]), tmp("scale", [P, TT])
        if token is not None:
            tok = tmp("tok", [P, D])
        if ln is not None:
            lnw = tmp("lnw", list(ln.shape))
        turned = inner.enter_context(nc.psum_tensor(f"{name}_turned", [P, NC, KD, 512], F32))
        s = {n: sem(n) for n in ("cst_loaded var_ready std_ready sq_ready len_ready xn_ready turned_ready "
                                 "step evacuated").split()}
        x_loaded = [sem(f"x_loaded{n}") for n in range(NC)]
        n_cst = (token is not None) + (ln is not None)
        block = inner.enter_context(nc.Block())

        @block.sync
        def _(sp):
            for n in range(NC):
                sp.dma_start(x[:, n * CT:(n + 1) * CT, :], tiles_of(x_in, n * CH, CT)).then_inc(x_loaded[n], 16)
                if n == 0:
                    if token is not None:
                        sp.dma_start(tok[:], row_tile(token, P)).then_inc(s["cst_loaded"], 16)
                    if ln is not None:
                        sp.dma_start(lnw[:], ln).then_inc(s["cst_loaded"], 16)

        @block.vector
        def _(dve):
            step = Tally(dve, s["step"])
            for n in range(NC):
                ts = range(n * CT, (n + 1) * CT)
                cols = slice(n * CT, (n + 1) * CT)
                dve.wait_ge(x_loaded[n], 16)
                for t in ts:
                    step.add(nc.vector.bn_stats(stats[:, t, :], x[:, t, :]))
                step.wait()
                for t in ts:
                    ins = nc.vector.bn_aggr(mv[:, t, :], stats[:, t, :])
                ins.then_inc(s["var_ready"], 1)
                dve.wait_ge(s["std_ready"], n + 1)
                step.add(nc.vector.reciprocal(rstd[:, cols], std[:, cols]))
                step.wait()
                for t in ts:
                    ins = nc.vector.tensor_scalar(xn[:, t, :], x[:, t, :], mv[:, t, 0:1], rstd[:, t:t + 1],
                                                  ALU.subtract, ALU.mult)
                    if t < ts[-1] or mode != "plain":
                        step.add(ins)
                if mode == "plain":
                    ins.then_inc(s["xn_ready"], 1)
                    continue
                step.wait()
                if mode == "rms":
                    if n == 0:
                        dve.wait_ge(s["cst_loaded"], 16 * n_cst)
                    for t in ts:
                        step.add(nc.vector.tensor_tensor_reduce(work[:, t % CT, :], xn[:, t, :], tok[:], 1.0, 0.0,
                                                                ALU.mult, ALU.add, keep.route[:, t:t + 1]))
                    step.wait()
                    for t in ts:
                        ins = nc.vector.tensor_tensor_reduce(work[:, t % CT, :], xn[:, t, :], xn[:, t, :], 1.0, 0.0,
                                                             ALU.mult, ALU.add, size[:, t:t + 1])
                    ins.then_inc(s["sq_ready"], 1)
                    dve.wait_ge(s["len_ready"], n + 1)
                    step.add(nc.vector.tensor_scalar(scale[:, cols], scale[:, cols], 1e-12, None, ALU.max))
                    step.wait()
                    step.add(nc.vector.reciprocal(scale[:, cols], scale[:, cols]))
                    step.wait()
                    for t in ts:
                        ins = nc.vector.tensor_scalar(xn[:, t, :], xn[:, t, :], scale[:, t:t + 1], float(D) ** 0.5,
                                                      ALU.mult, ALU.mult)
                    ins.then_inc(s["xn_ready"], 1)
                else:
                    step.add(nc.vector.tensor_reduce(size[:, cols], xn[:, cols, :], AX.X, ALU.max, apply_absolute_value=True))
                    step.wait()
                    step.add(nc.vector.tensor_scalar(size[:, cols], size[:, cols], 1e-5, None, ALU.max))
                    step.wait()
                    step.add(nc.vector.tensor_scalar(keep.step_size[:, cols], size[:, cols], 1.0 / 127.0, None, ALU.mult))
                    step.add(nc.vector.reciprocal(scale[:, cols], size[:, cols]))
                    step.wait()
                    step.add(nc.vector.tensor_scalar(scale[:, cols], scale[:, cols], 127.0, None, ALU.mult))
                    step.wait()
                    for t in ts:
                        step.add(nc.vector.tensor_scalar(xn[:, t, :], xn[:, t, :], scale[:, t:t + 1], ROUND, ALU.mult, ALU.add))
                    step.wait()
                    step.add(nc.vector.tensor_scalar(xn[:, cols, :], xn[:, cols, :], -ROUND, -128.0, ALU.add, ALU.max))
                    step.wait()
                    nc.vector.tensor_scalar(xn[:, cols, :], xn[:, cols, :], 127.0, None, ALU.min).then_inc(s["xn_ready"], 1)

        @block.tensor
        def _(pe):
            for n in range(NC):
                pe.wait_ge(s["xn_ready"], n + 1)
                for k in range(KD):
                    for t in range(CT):
                        last = nc.tensor.transpose(turned[:, n, k, t * P:(t + 1) * P], xn[:, n * CT + t, k * P:(k + 1) * P], c.ident[:])
                last.then_inc(s["turned_ready"], 1)

        @block.scalar
        def _(act):
            if n_cst:
                act.wait_ge(s["cst_loaded"], 16 * n_cst)

            def root(n):
                cols = slice(n * CT, (n + 1) * CT)
                act.wait_ge(s["var_ready"], n + 1)
                nc.scalar.activation(std[:, cols], mv[:, cols, 1], ACT.Sqrt, bias=c.eps[:, 0:1]).then_inc(s["std_ready"], 1)
                if mode == "rms":
                    act.wait_ge(s["sq_ready"], n + 1)
                    nc.scalar.activation(scale[:, cols], size[:, cols], ACT.Sqrt).then_inc(s["len_ready"], 1)

            root(0)
            for n in range(NC):
                if n + 1 < NC:
                    root(n + 1)
                act.wait_ge(s["turned_ready"], n + 1)
                for i, (dst, off) in enumerate(outs):
                    for k in range(KD):
                        d = dst[:, k, n * CH:(n + 1) * CH]
                        if ln is None:
                            nc.scalar.activation(d, turned[:, n, k, :], ACT.Copy)
                        elif off:
                            nc.scalar.activation(d, turned[:, n, k, :], ACT.Identity, scale=lnw[:, k, 0:1], bias=lnw[:, k, 1:2])
                        else:
                            nc.scalar.activation(d, turned[:, n, k, :], ACT.Copy, scale=lnw[:, k, i:i + 1])
    return keep


def route_tokens(nc, ctx, c, name, route, scratch, weight):
    n_iter, k_eff, heavy = 50, min(256 * 9.0 / 8.0, S), 256
    log_k = float(np.log(np.float32(k_eff)))
    with ExitStack() as inner:
        def tmp(n, shape, dt=F32):
            return inner.enter_context(nc.sbuf_tensor(f"{name}_{n}", shape, dt))

        def sem(n):
            return c.semaphore(f"{name}_{n}")

        r3 = route[:].rearrange("p (b t) -> p b t", b=B)
        best, best_all = tmp("best", [P, B]), tmp("best_all", [P, B])
        na, top = tmp("na", [P, B]), tmp("top", [P, B])
        part, total_ln = tmp("part", [P, B]), tmp("total_ln", [P, B])
        sbm, ex = tmp("sbm", [P, B, NT]), tmp("ex", [P, B, NT])
        t_col = tmp("t_col", [P, P])
        t_row = tmp("t_row", [TT, P])
        t_all = tmp("t_all", [P, TOK])
        e_col, g_col = tmp("e_col", [P, TT]), tmp("g_col", [P, TT])
        before = tmp("before", [P, 2 * S])
        junk = tmp("junk", [P, 2, S])
        above, equal = tmp("above", [P, TT]), tmp("equal", [P, TT])
        ps = inner.enter_context(nc.psum_tensor(f"{name}_ps", [P, 512], F32))
        pt = inner.enter_context(nc.psum_tensor(f"{name}_pt", [P, 512], F32))
        s = {n: sem(n) for n in ("best_ready best_done ex_ready sbm_ready part_ready sum_ready ln_ready na_ready tcol_ready trow_ps "
                                 "trow_ready stored t_loaded e_ready before_ready step loop_step tail_step").split()}
        block = inner.enter_context(nc.Block())

        def wide(v):
            return v[:].unsqueeze(2).broadcast_to([P, B, NT])

        @block.gpsimd
        def _(pool):
            pool.wait_ge(s["best_ready"], 1)
            pool.partition_all_reduce(best_all[:], best[:], P, bass.bass_isa.ReduceOp.max).then_inc(s["best_done"], 1)
            pool.wait_ge(s["best_done"], 1)
            pool.memset(before[:], 1.0).then_inc(s["before_ready"], 1)
            pool.wait_ge(s["before_ready"], 1)
            pool.affine_select(out=before[:], in_=before[:], compare_op=ALU.is_gt, fill=0.0, base=S, pattern=[[-1, 2 * S]],
                               channel_multiplier=1).then_inc(s["before_ready"], 1)

        @block.tensor
        def _(pe):
            with pe.Fori(0, n_iter - 1) as i:
                pe.wait_ge(s["part_ready"], i + 1)
                nc.tensor.matmul(ps[:, 0:B], c.ones[:], part[:], start=True, stop=True).then_inc(s["sum_ready"], 1)
            pe.wait_ge(s["tcol_ready"], 1)
            nc.tensor.transpose(pt[:, 0:P], t_col[:], c.ident[:]).then_inc(s["trow_ps"], 1)

        @block.scalar
        def _(act):
            with act.Fori(0, n_iter - 1) as i:
                act.wait_ge(s["sbm_ready"], i + 1)
                nc.scalar.activation(ex[:], sbm[:], ACT.Exp).then_inc(s["ex_ready"], 1)
                act.wait_ge(s["sum_ready"], i + 1)
                nc.scalar.activation(total_ln[:], ps[:, 0:B], ACT.Ln).then_inc(s["ln_ready"], 1)
            act.wait_ge(s["tcol_ready"], 1)
            nc.scalar.activation(e_col[:], t_col[:, 0:TT], ACT.Exp).then_inc(s["e_ready"], 1)

        @block.sync
        def _(sp):
            sp.wait_ge(s["trow_ready"], 1)
            sp.dma_start(scratch, t_row[:]).then_inc(s["stored"], 16)
            sp.wait_ge(s["stored"], 16)
            sp.dma_start(t_all[:], row_tile(scratch.rearrange("t p -> (t p)"), P)).then_inc(s["t_loaded"], 16)
            sp.wait_ge(s["t_loaded"], 16)

        @block.vector
        def _(dve):
            step = Tally(dve, s["step"])
            step.add(nc.vector.memset(t_col[:], 0.0))
            step.add(nc.vector.memset(na[:], float(np.log(np.float32(S))) - log_k))
            nc.vector.tensor_reduce(best[:], r3, AX.X, ALU.max).then_inc(s["best_ready"], 1)
            dve.wait_ge(s["best_done"], 1)
            step.wait()
            dve.sem_inc(s["na_ready"], 1)
            with dve.Fori(0, n_iter - 1) as i:
                dve.wait_ge(s["na_ready"], i + 1)
                nc.vector.tensor_tensor(sbm[:], r3, wide(na), ALU.min).then_inc(s["loop_step"], 1)
                nc.vector.tensor_tensor(top[:], best_all[:], na[:], ALU.min).then_inc(s["loop_step"], 1)
                dve.wait_ge(s["loop_step"], i * 2 + 2)
                nc.vector.tensor_tensor(sbm[:], sbm[:], wide(top), ALU.subtract).then_inc(s["sbm_ready"], 1)
                dve.wait_ge(s["ex_ready"], i + 1)
                nc.vector.tensor_reduce(part[:], ex[:], AX.X, ALU.add).then_inc(s["part_ready"], 1)
                dve.wait_ge(s["ln_ready"], i + 1)
                nc.vector.scalar_tensor_tensor(na[:], top[:], -log_k, total_ln[:], ALU.add, ALU.add).then_inc(s["na_ready"], 1)
            tail = Tally(dve, s["tail_step"])
            dve.wait_ge(s["na_ready"], n_iter)
            t3 = t_col[:, 0:TT].rearrange("p (b t) -> p b t", b=B)
            tail.add(nc.vector.tensor_tensor(t3, r3, wide(na), ALU.subtract))
            tail.wait()
            nc.vector.tensor_scalar(t_col[:, 0:TT], t_col[:, 0:TT], 0.0, None, ALU.min).then_inc(s["tcol_ready"], 1)
            dve.wait_ge(s["trow_ps"], 1)
            nc.vector.tensor_copy(t_row[:], pt[0:TT, 0:P]).then_inc(s["trow_ready"], 1)
            dve.wait_ge(s["e_ready"], 1)
            tail.add(nc.vector.tensor_scalar(g_col[:], e_col[:], -1.0, 1.0, ALU.mult, ALU.add))
            tail.wait()
            tail.add(nc.vector.tensor_tensor(g_col[:], g_col[:], e_col[:], ALU.add))
            dve.wait_ge(s["before_ready"], 2)
            dve.wait_ge(s["t_loaded"], 16)
            dve.wait_ge(s["tcol_ready"], 1)
            for t in range(TT):
                b, own = divmod(t, NT)
                row = t_all[:, b * S:(b + 1) * S]
                if t:
                    tail.wait()
                tail.add(nc.vector.scalar_tensor_tensor(junk[:, 0, :], row, t_col[:, t:t + 1], before[:, 0:S],
                                                        ALU.is_gt, ALU.mult, accum_out=above[:, t:t + 1]))
                tail.add(nc.vector.scalar_tensor_tensor(junk[:, 1, :], row, t_col[:, t:t + 1], before[:, S - P * own:2 * S - P * own],
                                                        ALU.is_equal, ALU.mult, accum_out=equal[:, t:t + 1]))
            tail.wait()
            tail.add(nc.vector.tensor_tensor(above[:], above[:], equal[:], ALU.add))
            tail.wait()
            nc.vector.scalar_tensor_tensor(weight[:], above[:], heavy - 0.5, g_col[:], ALU.is_lt, ALU.mult)


def ffn0(nc, c, name, x_in, x_out, gate, io):
    DH = io["l0_w1h"].shape[1]
    MH = DH // P
    with ExitStack() as ctx:
        def sb(n, shape, dt=F32):
            return ctx.enter_context(nc.sbuf_tensor(f"{name}_{n}", shape, dt))

        light_in, heavy_in = sb("light_in", [P, KD, TOK]), sb("heavy_in", [P, KD, TOK])
        weight = sb("weight", [P, TT])
        keep = normed(nc, ctx, c, f"{name}n", x_in, "rms", io["l0_gammas"], ((light_in, 0), (heavy_in, 0)), io["l0_token"])
        x = keep.x
        route_tokens(nc, ctx, c, f"{name}r", keep.route, io["scratch"], weight)

        w1l, w2l = sb("w1l", [P, KD, P]), sb("w2l", [P, D])
        w1h, w2h = sb("w1h", [P, KD, DH]), sb("w2h", [P, MH, D])
        b1 = sb("b1", [P, 1 + MH])
        b2l, b2h = sb("b2l", [P, D]), sb("b2h", [P, D])
        hl, hh = sb("hl", [P, CH]), sb("hh", [P, MH, CH])
        yl, yh = sb("yl", [P, CT, D]), sb("yh", [P, CT, D])
        hid = ctx.enter_context(nc.psum_tensor(f"{name}_hid", [P, 3, 512], F32))
        out_l = ctx.enter_context(nc.psum_tensor(f"{name}_out_l", [P, CT, D], F32))
        out_h = ctx.enter_context(nc.psum_tensor(f"{name}_out_h", [P, CT, D], F32))
        s = {n: c.semaphore(f"{name}_{n}") for n in
             "w_loaded hid_ready act_done light_done heavy_done out_free step x_ready stored dve_passed".split()}
        H = 1 + MH
        block = ctx.enter_context(nc.Block())

        @block.sync
        def _(sp):
            for dst, src in ((w1l, io["l0_w1l"].rearrange("(k p) m -> p k m", p=P)), (b1, io["l0_b1"]),
                             (w1h, io["l0_w1h"].rearrange("(k p) m -> p k m", p=P)), (w2l, io["l0_w2l"]),
                             (w2h, io["l0_w2h"].rearrange("(k p) m -> p k m", p=P)),
                             (b2l, row_tile(io["l0_b2l"], P)), (b2h, row_tile(io["l0_b2h"], P))):
                sp.dma_start(dst[:], src).then_inc(s["w_loaded"], 16)
            with sp.Fori(0, NC) as n:
                tile, tok = sp.snap(n * CT), sp.snap(n * CH)
                sp.wait_ge(s["x_ready"], n + 1)
                sp.dma_start(tiles_of(x_out, tok, CT), x[:, bass.ds(tile, CT), :]).then_inc(s["stored"], 16)
            sp.wait_ge(s["stored"], 16 * NC)

        @block.tensor
        def _(pe):
            pe.wait_ge(s["w_loaded"], 16 * 7)
            with pe.Fori(0, NC) as n:
                for i in range(H):
                    if i >= 3:
                        pe.wait_ge(s["act_done"], n * H + i - 2)
                    src = light_in if i == 0 else heavy_in
                    for k in range(KD):
                        w = w1l[:, k, :] if i == 0 else w1h[:, k, (i - 1) * P:i * P]
                        last = nc.tensor.matmul(hid[:, i % 3, :], w, src[:, k, bass.ds(n * CH, CH)], start=k == 0, stop=k == KD - 1)
                    last.then_inc(s["hid_ready"], 1)
                pe.wait_ge(s["out_free"], n + 1)
                pe.wait_ge(s["act_done"], n * H + 1)
                for t in range(CT):
                    last = nc.tensor.matmul(out_l[:, t, :], hl[:, t * P:(t + 1) * P], w2l[:], start=True, stop=True)
                last.then_inc(s["light_done"], 1)
                for t in range(CT):
                    for k in range(MH):
                        if t == 0:
                            pe.wait_ge(s["act_done"], n * H + k + 2)
                        last = nc.tensor.matmul(out_h[:, t, :], hh[:, k, t * P:(t + 1) * P], w2h[:, k, :], start=k == 0, stop=k == MH - 1)
                last.then_inc(s["heavy_done"], 1)

        @block.scalar
        def _(act):
            act.wait_ge(s["w_loaded"], 16 * 7)
            with act.Fori(0, NC) as n:
                for i in range(H):
                    act.wait_ge(s["hid_ready"], n * H + i + 1)
                    dst = hl[:] if i == 0 else hh[:, i - 1, :]
                    nc.scalar.activation(dst, hid[:, i % 3, :], ACT.Gelu, bias=b1[:, i:i + 1]).then_inc(s["act_done"], 1)

        @block.vector
        def _(dve):
            dve.wait_ge(s["w_loaded"], 16 * 7)
            dve.sem_inc(s["out_free"], 1)
            with dve.Fori(0, NC) as n:
                tile = dve.snap(n * CT)
                step = Tally(dve, s["step"], 1 + CT, n)
                dve.wait_ge(s["light_done"], n + 1)
                step.add(nc.vector.tensor_tensor(yl[:], out_l[:], b2l[:].unsqueeze(1).broadcast_to([P, CT, D]), ALU.add))
                dve.wait_ge(s["heavy_done"], n + 1)
                nc.vector.tensor_tensor(yh[:], out_h[:], b2h[:].unsqueeze(1).broadcast_to([P, CT, D]), ALU.add).then_inc(s["out_free"], 1)
                dve.wait_ge(s["out_free"], n + 2)
                step.wait()
                for t in range(CT):
                    step.add(nc.vector.scalar_tensor_tensor(yl[:, t, :], yh[:, t, :], weight[:, bass.ds(tile + t, 1)], yl[:, t, :],
                                                            ALU.mult, ALU.add))
                step.wait()
                step.close()
                xs = x[:, bass.ds(tile, CT), :]
                nc.vector.scalar_tensor_tensor(xs, yl[:], c.gates[:, gate:gate + 1], xs, ALU.mult, ALU.add).then_inc(s["x_ready"], 1)
                pause(dve, s["x_ready"], n + 1, s["dve_passed"])


def ffn1(nc, c, name, x_in, x_out, gate, io):
    DH = io["l1_w1"].shape[1]
    MH = DH // P
    with ExitStack() as ctx:
        def sb(n, shape, dt=F32):
            return ctx.enter_context(nc.sbuf_tensor(f"{name}_{n}", shape, dt))

        xq = sb("xq", [P, KD, TOK], BF16)
        keep = normed(nc, ctx, c, f"{name}n", x_in, "quant", None, ((xq, 0),))
        x, step_size = keep.x, keep.step_size

        w1, w2 = sb("w1", [P, KD, DH]), sb("w2", [P, MH, D])
        w1t, w2t = sb("w1t", [P, KD, DH], BF16), sb("w2t", [P, MH, D], BF16)
        part, mean, scale = sb("part", [P, 2]), sb("mean", [P, 2]), sb("scale", [P, 2])
        conv = sb("conv", [P, MH, 4])
        diag = sb("diag", [P, P * TT])
        row = sb("row", [P, B, S])
        h = sb("h", [P, S + 2])
        y = sb("y", [P, S])
        act_out = sb("act_out", [P, MH, S])
        big = sb("big", [P, S])
        mag = sb("mag", [P, 2, S])
        size, back, inv = sb("size", [P, NT]), sb("back", [P, NT]), sb("inv", [P, NT])
        diag2 = sb("diag2", [P, P * NT])
        hq = sb("hq", [P, MH, S], BF16)
        ps = [ctx.enter_context(nc.psum_tensor(f"{name}_ps{i}", [P, 2, 512], F32)) for i in range(2)]
        out_ps = ctx.enter_context(nc.psum_tensor(f"{name}_out_ps", [P, NT, D], F32))
        psf = [p[:].rearrange("p a n -> p (a n)") for p in ps]
        outf = out_ps[:].rearrange("p t d -> p (t d)")
        s = {n: c.semaphore(f"{name}_{n}") for n in
             "w1_loaded w2_loaded conv_loaded part_ready total_ready tern_ready diag_ready row_ps row_ready hid_ready h_ready conv_ready silu_done mag_ready big_done "
             "big_ready big_turned diag2_ready row2_ps hq_ready out_ready x_ready stored step body_step sp_passed dve_passed".split()}
        block = ctx.enter_context(nc.Block())

        @block.sync
        def _(sp):
            sp.dma_start(w1[:], io["l1_w1"].rearrange("(k p) m -> p k m", p=P)).then_inc(s["w1_loaded"], 16)
            sp.dma_start(w2[:], io["l1_w2"].rearrange("(k p) m -> p k m", p=P)).then_inc(s["w2_loaded"], 16)
            sp.dma_start(conv[:], io["l1_conv"]).then_inc(s["conv_loaded"], 16)
            with sp.Fori(0, B) as b:
                tile, tok = sp.snap(b * NT), sp.snap(b * S)
                sp.wait_ge(s["x_ready"], b + 1)
                sp.dma_start(tiles_of(x_out, tok, NT), x[:, bass.ds(tile, NT), :]).then_inc(s["stored"], 16)
            sp.wait_ge(s["stored"], 16 * B)

        @block.tensor
        def _(pe):
            pe.wait_ge(s["part_ready"], 2)
            nc.tensor.matmul(ps[0][:, 0, 0:2], c.ones[:], part[:], start=True, stop=True).then_inc(s["total_ready"], 1)
            pe.wait_ge(s["diag_ready"], TT)
            for b in range(B):
                for t in range(NT):
                    n = b * NT + t
                    last = nc.tensor.matmul(outf[:, n * P:(n + 1) * P], c.ones[:], diag[:, n * P:(n + 1) * P], start=True, stop=True)
            last.then_inc(s["row_ps"], 1)
            pe.wait_ge(s["tern_ready"], 2)
            pe.wait_ge(s["row_ready"], 1)
            with pe.Fori(0, B) as b:
                for m in range(MH):
                    if m >= 2:
                        pe.wait_ge(s["h_ready"], b * MH + m - 1)
                    for j in range(2):
                        for k in range(KD):
                            last = nc.tensor.matmul(ps[m % 2][:, j, :], w1t[:, k, m * P:(m + 1) * P],
                                                    xq[:, k, bass.ds(b * S + j * CH, CH)], start=k == 0, stop=k == KD - 1)
                    last.then_inc(s["hid_ready"], 1)
                pe.wait_ge(s["big_ready"], b + 1)
                for t in range(NT):
                    last = nc.tensor.transpose(psf[0][:, t * P:(t + 1) * P], big[:, t * P:(t + 1) * P], c.ident[:])
                last.then_inc(s["big_turned"], 1)
                pe.wait_ge(s["diag2_ready"], b + 1)
                for t in range(NT):
                    last = nc.tensor.matmul(psf[1][:, t * P:(t + 1) * P], c.ones[:], diag2[:, t * P:(t + 1) * P], start=True, stop=True)
                last.then_inc(s["row2_ps"], 1)
                for t in range(NT):
                    for k in range(MH):
                        if t == 0:
                            pe.wait_ge(s["hq_ready"], b * MH + k + 1)
                        last = nc.tensor.matmul(out_ps[:, t, :], hq[:, k, t * P:(t + 1) * P], w2t[:, k, :], start=k == 0, stop=k == MH - 1)
                last.then_inc(s["out_ready"], 1)

        @block.scalar
        def _(act):
            act.wait_ge(s["row_ps"], 1)
            act.wait_ge(s["tern_ready"], 2)
            nc.scalar.activation(row[:].rearrange("p b n -> p (b n)"), outf, ACT.Copy, scale=mean[:, 0:1]).then_inc(s["row_ready"], 1)
            with act.Fori(0, B) as b:
                for m in range(MH):
                    act.wait_ge(s["conv_ready"], b * MH + m + 1)
                    nc.scalar.activation(act_out[:, m, :], y[:], ACT.Silu).then_inc(s["silu_done"], 1)
                    act.wait_ge(s["silu_done"], b * MH + m + 1)
                    if m >= 2:
                        act.wait_ge(s["big_done"], b * MH + m - 1)
                    nc.scalar.activation(mag[:, m % 2, :], act_out[:, m, :], ACT.Abs).then_inc(s["mag_ready"], 1)

        @block.vector
        def _(dve):
            step = Tally(dve, s["step"])
            step.add(nc.vector.memset(h[:], 0.0))
            for t in range(TT):
                nc.vector.tensor_scalar(diag[:, t * P:(t + 1) * P], c.ident[:], step_size[:, t:t + 1], None, ALU.mult).then_inc(s["diag_ready"], 1)
            for i, (w, loaded) in enumerate(((w1, "w1_loaded"), (w2, "w2_loaded"))):
                dve.wait_ge(s[loaded], 16)
                nc.vector.tensor_reduce(part[:, i:i + 1], w[:], AX.XY, ALU.add, apply_absolute_value=True).then_inc(s["part_ready"], 1)
            dve.wait_ge(s["total_ready"], 1)
            step.add(nc.vector.tensor_scalar(mean[:], ps[0][:, 0, 0:2], 1.0 / (D * DH), 1e-5, ALU.mult, ALU.max))
            step.wait()
            step.add(nc.vector.reciprocal(scale[:], mean[:]))
            step.wait()
            for i, w in enumerate((w1, w2)):
                step.add(nc.vector.tensor_scalar(w[:], w[:], scale[:, i:i + 1], ROUND, ALU.mult, ALU.add))
            step.wait()
            for w in (w1, w2):
                step.add(nc.vector.tensor_scalar(w[:], w[:], -ROUND, -1.0, ALU.add, ALU.max))
            step.wait()
            for w, wt in ((w1, w1t), (w2, w2t)):
                nc.vector.tensor_scalar(wt[:], w[:], 1.0, None, ALU.min).then_inc(s["tern_ready"], 1)
            dve.wait_ge(s["conv_loaded"], 16)
            dve.wait_ge(s["row_ready"], 1)
            with dve.Fori(0, B) as b:
                body = Tally(dve, s["body_step"], 1 + 2 * MH + 4 + NT - 1 + 2 + 2 * MH + NT - 1, b)
                body.add(nc.vector.memset(big[:], 0.0))
                body.wait()

                def largest(m):
                    dve.wait_ge(s["mag_ready"], b * MH + m + 1)
                    if m >= 1:
                        dve.wait_ge(s["big_done"], b * MH + m)
                    nc.vector.tensor_tensor(big[:], mag[:, m % 2, :], big[:], ALU.max).then_inc(s["big_done"], 1)

                for m in range(MH):
                    dve.wait_ge(s["hid_ready"], b * MH + m + 1)
                    if m >= 1:
                        dve.wait_ge(s["conv_ready"], b * MH + m)
                    rowb = row[:, bass.ds(b, 1), :].rearrange("p o n -> p (o n)")
                    nc.vector.tensor_tensor(h[:, 1:S + 1], psf[m % 2], rowb, ALU.mult).then_inc(s["h_ready"], 1)
                    dve.wait_ge(s["h_ready"], b * MH + m + 1)
                    if m >= 1:
                        dve.wait_ge(s["silu_done"], b * MH + m)
                        largest(m - 1)
                    body.add(nc.vector.tensor_scalar(y[:], h[:, 1:S + 1], conv[:, m, 1:2], conv[:, m, 3:4], ALU.mult, ALU.add))
                    body.wait()
                    body.add(nc.vector.scalar_tensor_tensor(y[:], h[:, 0:S], conv[:, m, 0:1], y[:], ALU.mult, ALU.add))
                    body.wait()
                    nc.vector.scalar_tensor_tensor(y[:], h[:, 2:S + 2], conv[:, m, 2:3], y[:], ALU.mult, ALU.add).then_inc(s["conv_ready"], 1)
                largest(MH - 1)
                dve.wait_ge(s["big_done"], b * MH + MH)
                dve.sem_inc(s["big_ready"], 1)
                dve.wait_ge(s["big_turned"], b + 1)
                body.add(nc.vector.tensor_reduce(size[:], psf[0].rearrange("p (t n) -> p t n", t=NT), AX.X, ALU.max))
                body.wait()
                body.add(nc.vector.tensor_scalar(size[:], size[:], 1e-5, None, ALU.max))
                body.wait()
                body.add(nc.vector.reciprocal(inv[:], size[:]))
                body.wait()
                body.add(nc.vector.tensor_scalar(inv[:], inv[:], 127.0, None, ALU.mult))
                body.wait()
                for t in range(NT):
                    ins = nc.vector.tensor_scalar(diag2[:, t * P:(t + 1) * P], c.ident[:], inv[:, t:t + 1], None, ALU.mult)
                    if t < NT - 1:
                        body.add(ins)
                ins.then_inc(s["diag2_ready"], 1)
                body.add(nc.vector.tensor_scalar(back[:], size[:], mean[:, 1:2], 1.0 / 127.0, ALU.mult, ALU.mult))
                body.wait()
                body.add(nc.vector.tensor_scalar(back[:], back[:], c.gates[:, gate:gate + 1], None, ALU.mult))
                dve.wait_ge(s["row2_ps"], b + 1)
                for m in range(MH):
                    body.add(nc.vector.tensor_tensor(act_out[:, m, :], act_out[:, m, :], psf[1], ALU.mult))
                    body.wait()
                    body.add(nc.vector.tensor_scalar(act_out[:, m, :], act_out[:, m, :], ROUND, -ROUND, ALU.add, ALU.add))
                    body.wait()
                    nc.vector.tensor_scalar(hq[:, m, :], act_out[:, m, :], 127.0, -128.0, ALU.min, ALU.max).then_inc(s["hq_ready"], 1)
                dve.wait_ge(s["out_ready"], b + 1)
                for t in range(NT):
                    xs = x[:, bass.ds(b * NT + t, 1), :].rearrange("p o d -> p (o d)")
                    ins = nc.vector.scalar_tensor_tensor(xs, out_ps[:, t, :], back[:, t:t + 1], xs, ALU.mult, ALU.add)
                    if t < NT - 1:
                        body.add(ins)
                ins.then_inc(s["x_ready"], 1)
                body.close()
                pause(dve, s["x_ready"], b + 1, s["dve_passed"])




def moe(nc, c, name, x_in, x_out, gate, top, io, w, ln=None, base=None):
    E = EXPERTS
    DH = w["gate"].shape[1] // KD
    MH = DH // P
    ST = SLOTS // P
    TILES = slot_tiles(top)
    assert TILES % 2 == 1
    up = "up" in w
    n_w = 3 if up else 2
    HID = 4
    FAR = float(2 * TILES * SLOTS)
    slots_in, slots_out = io["slots_in"][0:TILES * SLOTS, :], io["slots_out"][0:TILES * SLOTS, :]
    with ExitStack() as ctx:
        def sb(n, shape, dt=F32):
            return ctx.enter_context(nc.sbuf_tensor(f"{name}_{n}", shape, dt))

        def ps(n, shape):
            return ctx.enter_context(nc.psum_tensor(f"{name}_{n}", shape, F32))

        xT = sb("xT", [P, KD, TOK])
        keep = normed(nc, ctx, c, f"{name}n", x_in, "plain", ln, ((xT, ln is not None),), keep_xn=True)
        x, xn = keep.x, keep.xn

        wr, br = sb("wr", [P, KD, E]), sb("br", [P, E])
        tile_no, part_no = sb("tile_no", [P, TILES]), sb("part_no", [P, 1])
        lg, rank = sb("lg", [P, TT, E]), sb("rank", [P, TT, E])
        cmp_ = sb("cmp", [P, E, TT, E])
        sel, slot, wt = sb("sel", [P, TT, E]), sb("slot", [P, TT, E]), sb("wt", [P, TT, E])
        lead, total = sb("lead", [P, TT]), sb("total", [P, TT])
        tiles_of_e, ends = sb("tiles_of_e", [P, E]), sb("ends", [P, E])
        passed_e = sb("passed_e", [P, TILES, E])
        expert = sb("expert", [P, TILES])
        expert_row = sb("expert_row", [P, TILES], U32)
        row_now = [sb(f"row_now{i}", [P, 1], U32) for i in range(2)]
        at, at_row = sb("at", [P, top, TT]), sb("at_row", [P, top, TT], U32)
        share = sb("share", [P, top, TT])
        weight_names = ("gate", "up", "down") if up else ("gate", "down")
        wb = [{n: sb(f"{n}{i}", [P, w[n].shape[1]]) for n in weight_names} for i in range(2)]
        xg = [sb(f"xg{i}", [P, ST, D]) for i in range(2)]
        xgT = [sb(f"xgT{i}", [P, KD, SLOTS]) for i in range(2)]
        hh = sb("hh", [P, MH, SLOTS])
        sg = sb("sg", [P, 2, SLOTS])
        y = [sb(f"y{i}", [P, ST, D]) for i in range(2)]
        yg = sb("yg", [P, TT, top, D])
        if base is not None:
            base_sb = sb("base", [P, TT, D])
        if ln is not None:
            lnw = sb("lnw", [P, KD, 2])
        hid = ps("hid", [P, HID, 2, SLOTS])
        turn = ps("turn", [P, KD, SLOTS])
        out_ps = [ps(f"out{i}", [P, ST, D]) for i in range(2)]
        routed = ps("routed", [P, 3, TT * E])

        names = ("r_loaded base_loaded lg_ps step shift_ready ex_ready sel_ready count_ready rows_ready row_taken slots_ready scattered "
                 "w_loaded0 w_loaded1 xg_loaded0 xg_loaded1 turned xgt_ready hid_ready silu_done h_ready down_done y_ready "
                 "y_stored0 y_stored1 share_ready added out_ready stored pe_passed pool_passed").split()
        s = {n: c.semaphore(f"{name}_{n}") for n in names}
        gathered = [c.semaphore(f"{name}_gathered{n}") for n in range(NC)]
        consts = [(wr, io[f"{name}_wr"].rearrange("(k p) e -> p k e", p=P)), (br, row_tile(io[f"{name}_br"], P)),
                  (tile_no, row_tile(io["tile_numbers"][0:TILES], P)), (part_no, io["part_numbers"])]
        if ln is not None:
            consts.append((lnw, ln))
        n_cst = 16 * len(consts)
        block = ctx.enter_context(nc.Block())

        @block.sync
        def _(sp):
            for dst, src in consts:
                sp.dma_start(dst[:], src).then_inc(s["r_loaded"], 16)
            if base is not None:
                sp.dma_start(base_sb[:], tiles_of(base, 0, TT)).then_inc(s["base_loaded"], 16)

            def load(first, i):
                sp.dma_start(xg[i][:], slots_in[bass.ds(first, SLOTS), :].rearrange("(t p) d -> p t d", p=P)).then_inc(s[f"xg_loaded{i}"], 16)

            def store(first, i):
                sp.dma_start(slots_out[bass.ds(first, SLOTS), :].rearrange("(t p) d -> p t d", p=P), y[i][:]).then_inc(s[f"y_stored{i}"], 16)

            sp.wait_ge(s["scattered"], 16 * TT * top)
            load(0, 0)
            load(SLOTS, 1)
            with sp.Fori(0, (TILES - 3) // 2) as r:
                for i in range(2):
                    v = r * 2 + i
                    ahead, here = sp.snap(v * SLOTS + 2 * SLOTS), sp.snap(v * SLOTS)
                    sp.wait_ge(s["turned"], v + 1)
                    load(ahead, i)
                    sp.wait_ge(s["y_ready"], v + 3)
                    store(here, i)
            for v in range(TILES - 3, TILES):
                if v + 2 < TILES:
                    sp.wait_ge(s["turned"], v + 1)
                    load((v + 2) * SLOTS, v % 2)
                sp.wait_ge(s["y_ready"], v + 3)
                store(v * SLOTS, v % 2)
            for n in range(NC):
                sp.wait_ge(s["out_ready"], n + 1)
                sp.dma_start(tiles_of(x_out, n * CH, CT), x[:, n * CT:(n + 1) * CT, :]).then_inc(s["stored"], 16)
            sp.wait_ge(s["stored"], 16 * NC)

        @block.gpsimd
        def _(pool):
            def fetch(v, i):
                nc.gpsimd.tensor_copy(row_now[i][:], expert_row[:, bass.ds(v, 1)]).then_inc(s["row_taken"], 1)
                pause(pool, s["row_taken"], v + 1, s["pool_passed"])
                for n in weight_names:
                    pool.indirect_dma_start(wb[i][n][:], None, w[n],
                                            bass.IndirectOffsetOnAxis(row_now[i][:], 0)).then_inc(s[f"w_loaded{i}"], 16)

            pool.wait_ge(s["rows_ready"], 1)
            for v in range(2):
                fetch(v, v)
            pool.wait_ge(c.cleared, 16)
            pool.wait_ge(s["slots_ready"], 1)
            for t in range(TT):
                for j in range(top):
                    pool.indirect_dma_start(slots_in, bass.IndirectOffsetOnAxis(at_row[:, j, t:t + 1], 0), xn[:, t, :],
                                            None).then_inc(s["scattered"], 16)
            with pool.Fori(0, (TILES - 3) // 2) as r:
                for i in range(2):
                    v = r * 2 + i
                    pause(pool, s["down_done"], v + 1, s["pool_passed"])
                    fetch(v + 2, i)
            pool.wait_ge(s["down_done"], TILES - 2)
            fetch(TILES - 1, 0)
            pool.wait_ge(s["y_stored0"], 16 * (TILES // 2 + 2))
            pool.wait_ge(s["y_stored1"], 16 * (TILES // 2 + 1))
            for t in range(TT):
                for j in range(top):
                    pool.indirect_dma_start(yg[:, t, j, :], None, slots_out,
                                            bass.IndirectOffsetOnAxis(at_row[:, j, t:t + 1], 0)).then_inc(gathered[t // CT], 16)

        @block.tensor
        def _(pe):
            pe.wait_ge(s["r_loaded"], n_cst)
            for t in range(TT):
                for k in range(KD):
                    last = nc.tensor.matmul(routed[:, 0, t * E:(t + 1) * E], xT[:, k, t * P:(t + 1) * P], wr[:, k, :],
                                            start=k == 0, stop=k == KD - 1)
            last.then_inc(s["lg_ps"], 1)
            pe.wait_ge(s["sel_ready"], 1)
            flat = sel[:].rearrange("p t e -> p (t e)")
            nc.tensor.matmul(routed[:, 1, :], c.earlier[:], flat, start=True, stop=False)
            for d in range(1, TT):
                nc.tensor.matmul(routed[:, 1, d * E:], c.ones[:], flat[:, 0:(TT - d) * E], start=False, stop=d == TT - 1)
            for t in range(TT):
                last = nc.tensor.matmul(routed[:, 2, 0:E], c.ones[:], sel[:, t, :], start=t == 0, stop=t == TT - 1)
            last.then_inc(s["count_ready"], 1)

            def turn_tile(i):
                for k in range(KD):
                    for t in range(ST):
                        last = nc.tensor.transpose(turn[:, k, t * P:(t + 1) * P], xg[i][:, t, k * P:(k + 1) * P], c.ident[:])
                last.then_inc(s["turned"], 1)

            def tile(v, i, r, more):
                pe.wait_ge(s["xgt_ready"], v * KD + KD)
                pause(pe, s[f"w_loaded{i}"], r * 16 * n_w + 16 * n_w, s["pe_passed"])
                for m in range(MH):
                    pe.wait_ge(s["h_ready"], v * MH + m + 1)
                    for j in range(n_w - 1):
                        for k in range(KD):
                            col = k * DH + m * P
                            last = nc.tensor.matmul(hid[:, m % HID, j, :], wb[i][weight_names[j]][:, col:col + P], xgT[i][:, k, :],
                                                    start=k == 0, stop=k == KD - 1)
                    last.then_inc(s["hid_ready"], 1)
                if more:
                    pause(pe, s[f"xg_loaded{1 - i}"], (r + i) * 16 + 16, s["pe_passed"])
                    turn_tile(1 - i)
                pe.wait_ge(s["y_ready"], v + 1)
                for t in range(ST):
                    for k in range(MH):
                        if t == 0:
                            pe.wait_ge(s["h_ready"], v * MH + HID + k + 1)
                        last = nc.tensor.matmul(out_ps[i][:, t, :], hh[:, k, t * P:(t + 1) * P], wb[i]["down"][:, k * D:(k + 1) * D],
                                                start=k == 0, stop=k == MH - 1)
                last.then_inc(s["down_done"], 1)

            pe.wait_ge(s["xg_loaded0"], 16)
            turn_tile(0)
            with pe.Fori(0, TILES // 2) as r:
                for i in range(2):
                    tile(r * 2 + i, i, r, True)
            tile(TILES - 1, 0, TILES // 2, False)

        @block.scalar
        def _(act):
            act.wait_ge(s["r_loaded"], n_cst)
            if top > 1:
                act.wait_ge(s["shift_ready"], 1)
                nc.scalar.activation(wt[:], wt[:], ACT.Exp).then_inc(s["ex_ready"], 1)

            def spread(v, i):
                act.wait_ge(s["turned"], v + 1)
                for k in range(KD):
                    if ln is None:
                        ins = nc.scalar.activation(xgT[i][:, k, :], turn[:, k, :], ACT.Copy)
                    else:
                        ins = nc.scalar.activation(xgT[i][:, k, :], turn[:, k, :], ACT.Identity, scale=lnw[:, k, 0:1], bias=lnw[:, k, 1:2])
                    ins.then_inc(s["xgt_ready"], 1)

            def tile(v, i, more):
                for m in range(MH):
                    act.wait_ge(s["hid_ready"], v * MH + m + 1)
                    if up:
                        if m >= 2:
                            act.wait_ge(s["h_ready"], v * MH + HID + m - 1)
                        nc.scalar.activation(sg[:, m % 2, :], hid[:, m % HID, 0, :], ACT.Silu).then_inc(s["silu_done"], 1)
                    else:
                        nc.scalar.activation(hh[:, m, :], hid[:, m % HID, 0, :], ACT.Gelu_apprx_tanh).then_inc(s["h_ready"], 1)
                if more:
                    spread(v + 1, 1 - i)

            spread(0, 0)
            with act.Fori(0, TILES // 2) as r:
                for i in range(2):
                    tile(r * 2 + i, i, True)
            tile(TILES - 1, 0, False)

        @block.vector
        def _(dve):
            step = Tally(dve, s["step"])
            dve.sem_inc(s["h_ready"], HID)
            dve.sem_inc(s["y_ready"], 2)
            for i in range(2):
                dve.sem_inc(s[f"y_stored{i}"], 16)
            dve.wait_ge(s["r_loaded"], n_cst)
            dve.wait_ge(s["lg_ps"], 1)
            step.add(nc.vector.tensor_tensor(lg[:], routed[:, 0, :].rearrange("p (t e) -> p t e", e=E),
                                             br[:].unsqueeze(1).broadcast_to([P, TT, E]), ALU.add))
            step.wait()
            for f in range(E):
                n = f + 1
                step.add(nc.vector.tensor_tensor(cmp_[:, f, :, 0:n], lg[:, :, f:n].broadcast_to([P, TT, n]), lg[:, :, 0:n], ALU.is_gt))
                if n < E:
                    step.add(nc.vector.tensor_tensor(cmp_[:, f, :, n:E], lg[:, :, f:n].broadcast_to([P, TT, E - n]), lg[:, :, n:E], ALU.is_ge))
            if top > 1:
                step.add(nc.vector.tensor_reduce(lead[:], lg[:], AX.X, ALU.max))
            step.wait()
            step.add(nc.vector.tensor_reduce(rank[:], cmp_[:].rearrange("p f t e -> p t e f"), AX.X, ALU.add))
            step.wait()
            nc.vector.tensor_scalar(sel[:], rank[:], top - 0.5, None, ALU.is_lt).then_inc(s["sel_ready"], 1)
            dve.wait_ge(s["sel_ready"], 1)
            if top > 1:
                nc.vector.tensor_tensor(wt[:], lg[:], lead[:].unsqueeze(2).broadcast_to([P, TT, E]), ALU.subtract).then_inc(s["shift_ready"], 1)
            dve.wait_ge(s["count_ready"], 1)
            step.add(nc.vector.tensor_scalar(tiles_of_e[:], routed[:, 2, 0:E], 1.0 / SLOTS, (SLOTS - 0.5) / SLOTS - 0.5, ALU.mult, ALU.add))
            step.wait()
            step.add(nc.vector.tensor_scalar(tiles_of_e[:], tiles_of_e[:], ROUND, -ROUND, ALU.add, ALU.add))
            step.wait()
            step.add(nc.vector.tensor_copy(ends[:, 0:1], tiles_of_e[:, 0:1]))
            for e in range(1, E):
                step.wait()
                step.add(nc.vector.tensor_tensor(ends[:, e:e + 1], ends[:, e - 1:e], tiles_of_e[:, e:e + 1], ALU.add))
            step.wait()
            step.add(nc.vector.tensor_tensor(passed_e[:, :, 0:E - 1], tile_no[:].unsqueeze(2).broadcast_to([P, TILES, E - 1]),
                                             ends[:, 0:E - 1].unsqueeze(1).broadcast_to([P, TILES, E - 1]), ALU.is_ge))
            step.wait()
            step.add(nc.vector.tensor_reduce(expert[:], passed_e[:, :, 0:E - 1], AX.X, ALU.add))
            step.wait()
            step.add(nc.vector.tensor_scalar(expert[:], expert[:], float(P), part_no[:, 0:1], ALU.mult, ALU.add))
            step.wait()
            nc.vector.tensor_copy(expert_row[:], expert[:]).then_inc(s["rows_ready"], 1)
            step.add(nc.vector.tensor_tensor(ends[:], ends[:], tiles_of_e[:], ALU.subtract))
            step.wait()
            step.add(nc.vector.tensor_scalar(ends[:], ends[:], float(SLOTS), None, ALU.mult))
            step.wait()
            step.add(nc.vector.tensor_tensor(slot[:], routed[:, 1, :].rearrange("p (t e) -> p t e", e=E),
                                             ends[:].unsqueeze(1).broadcast_to([P, TT, E]), ALU.add))
            step.add(nc.vector.tensor_scalar(rank[:], sel[:], -FAR, FAR, ALU.mult, ALU.add))
            step.wait()
            step.add(nc.vector.tensor_tensor(rank[:], rank[:], slot[:], ALU.add))
            step.wait()
            step.add(nc.vector.tensor_reduce(at[:, 0, :], rank[:], AX.X, ALU.min))
            if top > 1:
                dve.wait_ge(s["shift_ready"], 1)
                step.add(nc.vector.tensor_tensor(lg[:], slot[:], sel[:], ALU.mult))
                step.wait()
                step.add(nc.vector.tensor_reduce(at[:, 1, :], lg[:], AX.X, ALU.max))
            step.wait()
            nc.vector.tensor_copy(at_row[:], at[:]).then_inc(s["slots_ready"], 1)
            if top > 1:
                dve.wait_ge(s["ex_ready"], 1)
                step.add(nc.vector.tensor_tensor(wt[:], wt[:], sel[:], ALU.mult))
                step.wait()
                step.add(nc.vector.tensor_reduce(total[:], wt[:], AX.X, ALU.add))
                step.wait()
                step.add(nc.vector.reciprocal(total[:], total[:]))
                step.wait()
                step.add(nc.vector.tensor_scalar(total[:], total[:], c.gates[:, gate:gate + 1], None, ALU.mult))
                step.wait()
                step.add(nc.vector.tensor_tensor(wt[:], wt[:], total[:].unsqueeze(2).broadcast_to([P, TT, E]), ALU.mult))
                for j in range(top):
                    step.wait()
                    step.add(nc.vector.tensor_tensor(lg[:], slot[:], at[:, j, :].unsqueeze(2).broadcast_to([P, TT, E]), ALU.is_equal))
                    step.wait()
                    step.add(nc.vector.tensor_tensor(lg[:], lg[:], wt[:], ALU.mult))
                    step.wait()
                    step.add(nc.vector.tensor_reduce(share[:, j, :], lg[:], AX.X, ALU.add))

            def tile(v, i, r):
                if up:
                    for m in range(MH):
                        dve.wait_ge(s["silu_done"], v * MH + m + 1)
                        nc.vector.tensor_tensor(hh[:, m, :], sg[:, m % 2, :], hid[:, m % HID, 1, :], ALU.mult).then_inc(s["h_ready"], 1)
                dve.wait_ge(s["down_done"], v + 1)
                dve.wait_ge(s[f"y_stored{i}"], r * 16 + 16)
                nc.vector.tensor_copy(y[i][:], out_ps[i][:]).then_inc(s["y_ready"], 1)

            with dve.Fori(0, TILES // 2) as r:
                for i in range(2):
                    tile(r * 2 + i, i, r)
            tile(TILES - 1, 0, TILES // 2)
            g = c.gates[:, gate:gate + 1]
            if base is not None:
                dve.wait_ge(s["base_loaded"], 16)
                step.add(nc.vector.scalar_tensor_tensor(x[:], x[:], g, base_sb[:], ALU.mult, ALU.add))
            for n in range(NC):
                dve.wait_ge(gathered[n], 16 * CT * top)
                for t in range(n * CT, (n + 1) * CT):
                    for j in range(top):
                        if t == n * CT:
                            step.wait()
                        scale = share[:, j, t:t + 1] if top > 1 else g
                        ins = nc.vector.scalar_tensor_tensor(x[:, t, :], yg[:, t, j, :], scale, x[:, t, :], ALU.mult, ALU.add)
                        if j < top - 1 or t < (n + 1) * CT - 1:
                            step.add(ins)
                        if j < top - 1 and t > n * CT:
                            step.wait()
                ins.then_inc(s["out_ready"], 1)


def pack64(wq, wk, wv, wo):
    groups = wq.shape[1] // D
    qkv = np.stack([np.stack([by_partition(w[:, g * D:(g + 1) * D]) for w in (wq, wk, wv)], 1) for g in range(groups)])
    out = np.stack([by_partition(wo[g * D:(g + 1) * D]) for g in range(groups)])
    return np.concatenate([qkv, qkv]), np.concatenate([out, out])


def columns(*vectors):
    return np.stack([v.reshape(-1, P).T for v in vectors], 2)


def pack16(wq, bq, wk, bk, wv, bv, wo, bo):
    def dims_first(m):
        return m.reshape(m.shape[0], 2, 8, 16).transpose(0, 1, 3, 2).reshape(m.shape[0], D)

    zero = np.zeros(D, np.float32)
    bias = [dims_first((zero if v is None else v).reshape(1, D)).reshape(2, P).T for v in (bq, bk)]
    values = np.zeros((D, 16, 32), np.float32)
    values[:, :, 0:16] = wv.reshape(D, 16, 16)
    row = np.zeros((16, 32), np.float32)
    row[:, 0:16] = (zero if bv is None else bv).reshape(16, 16)
    row[:, 16] = 1.0
    out = np.zeros((16, 32, D), np.float32)
    out[:, 0:16] = wo.reshape(16, 16, D)
    if bo is not None:
        out[0, 16] = bo
    return {"q": by_partition(dims_first(wq)), "k": by_partition(dims_first(wk)), "v": by_partition(values.reshape(D, 2 * D)),
            "o": by_partition(out.reshape(2 * D, D)), "bqk": np.concatenate(bias, 1), "bv": row.reshape(2 * D)}


def pack_experts(w):
    e, rows, n = w.shape
    return w.reshape(e, rows // P, P, n).transpose(0, 2, 1, 3).reshape(e * P, rows // P * n)


def numbers():
    return {"tile_numbers": np.arange(slot_tiles(2), dtype=np.float32), "part_numbers": np.arange(P, dtype=np.float32).reshape(P, 1)}


def by_partition(w):
    return w.reshape(-1, P, w.shape[1]).transpose(1, 0, 2)


def kernel(**inputs):
    import concourse.bacc as _bacc
    from concourse.bass_utils import run_bass_kernel_spmd as _run

    a = {k: np.ascontiguousarray(v) for k, v in inputs.items()}
    arrays = lay_out(a)
    nc = _bacc.Bacc("TRN2", target_bir_lowering=False, num_devices=1)
    io = {}
    feed = {}
    for n, v in arrays.items():
        v = np.ascontiguousarray(v)
        feed[f"in_{n}"] = v
        io[n] = nc.dram_tensor(f"in_{n}", v.shape, mybir.dt.from_np(v.dtype), kind="ExternalInput").ap()
    io["out"] = nc.dram_tensor("out_0", (TOK, D), F32, kind="ExternalOutput").ap()
    for i in range(8):
        io[f"x{i}"] = nc.dram_tensor(f"x_{i}", (TOK, D), F32, kind="Internal").ap()
    program(nc, io)
    r = _run(nc, [feed], core_ids=[0])
    return r.results[0]["out_0"].reshape(B, S, D)


def weights(io, name):
    return {k[len(name) + 1:]: v for k, v in io.items() if k.startswith(name + "_")}


def program(nc, io):
    with ExitStack() as ctx:
        c = setup(nc, ctx, io)
        io["scratch"] = nc.dram_tensor("scratch", (TT, P), F32, kind="Internal").ap()
        attention16(nc, c, "l0x", io["x"], io["x0"], weights(io, "l0x"), 0, ctx_t=io["ctx_t"], mask=io["mask0"],
                    slots=io["slots_in"])
        c.end_stage()
        ffn0(nc, c, "l0f", io["x0"], io["x1"], 4, io)
        c.end_stage()
        attention64(nc, c, "l1x", io["x1"], io["x2"], io["l1_qkv"], io["l1_wo"], 1, io["ctx"], io["mask1"], io["l1_ln"],
                    out_ln=(io["l1_go"], io["l1_bo"]))
        c.end_stage()
        ffn1(nc, c, "l1f", io["x2"], io["x3"], 5, io)
        c.end_stage()
        attention16(nc, c, "l2x", io["x3"], io["x4"], weights(io, "l2x"), 2, ctx_t=io["ctx_t"])
        c.end_stage()
        moe(nc, c, "l2f", io["x4"], io["x5"], 6, 2, io, weights(io, "l2e"))
        c.end_stage()
        attention64(nc, c, "l3x", io["x5"], io["x6"], io["l3_qkv"], io["l3_wo"], 3, io["ctx"], io["mask3"], io["l3_ln"],
                    rms=io["l3_gam"], out_b=io["l3_bo"])
        c.end_stage()
        attention16(nc, c, "l3a", io["x6"], io["x7"], weights(io, "l3a"), None, ln=io["l3_ln1"], twice=True)
        c.end_stage()
        moe(nc, c, "l3f", io["x7"], io["out"], 7, 1, io, weights(io, "l3e"), io["l3_ln2"], io["x6"])
        c.end_stage()


def lay_out(a):
    arrays = {"x": a["x"].reshape(TOK, D), "ctx": a["ctx_1024"].reshape(B * SC, D), "ctx_t": a["ctx_1024"].reshape(B * SC, D).T,
              "g_xattn": a["g_xattn"], "g_ffn": a["g_ffn"], "mask0": a["mask_Bx1x1xS2_fk0"].reshape(B, SC),
              "mask1": a["mask_BxS2_bf1"], "mask3": a["mask_BxS2_bk0"]}
    n = "L0_xattn_"
    for k, v in pack16(*[a[n + k] for k in ("Wq", "bq", "Wk", "bk", "Wv", "bv", "Wo", "bo")]).items():
        arrays["l0x_" + k] = v
    n = "L0_ffn_"
    arrays["l0_gammas"] = columns(a[n + "light_gamma"], a[n + "heavy_gamma"])
    arrays["l0_token"] = a[n + "routing_token"]
    for k, m in (("w1l", "light_w1"), ("w2l", "light_w2"), ("w1h", "heavy_w1"), ("w2h", "heavy_w2"), ("b2l", "light_b2"), ("b2h", "heavy_b2")):
        arrays["l0_" + k] = a[n + m]
    arrays["l0_b1"] = np.concatenate([a[n + "light_b1"], a[n + "heavy_b1"]]).reshape(-1, P).T
    n = "L1_xattn_"
    wkv = a[n + "Wkv"]
    half = wkv.shape[1] // 2
    arrays["l1_qkv"], arrays["l1_wo"] = pack64(a[n + "Wq"], wkv[:, :half], wkv[:, half:], a[n + "Wout"])
    arrays["l1_ln"] = columns(a[n + "g_l"], a[n + "b_l"], a[n + "g_x"], a[n + "b_x"])
    arrays["l1_go"], arrays["l1_bo"] = a[n + "g_o"], a[n + "b_o"]
    n = "L1_ffn_"
    arrays["l1_w1"], arrays["l1_w2"] = a[n + "w1"].T, a[n + "w2"].T
    cw = a[n + "conv_w"]
    arrays["l1_conv"] = columns(cw[:, 0, 0], cw[:, 0, 1], cw[:, 0, 2], a[n + "conv_b"])
    n = "L2_xattn_"
    for k, v in pack16(*[a[n + k].T for k in ("Wq", "bq", "Wk", "bk", "Wv", "bv", "Wo", "bo")]).items():
        arrays["l2x_" + k] = v
    n = "L2_ffn_"
    for k, m in (("gate", "Wgate"), ("up", "Wup"), ("down", "Wdown")):
        arrays["l2e_" + k] = pack_experts(a[n + m].transpose(0, 2, 1))
    arrays["l2f_wr"], arrays["l2f_br"] = a[n + "wg"].T, a[n + "bg"]
    n = "L3_xattn_"
    wkv = a[n + "W_kv"]
    half = wkv.shape[1] // 2
    arrays["l3_qkv"], arrays["l3_wo"] = pack64(a[n + "W_q"], wkv[:, :half], wkv[:, half:], a[n + "W_out"])
    arrays["l3_ln"] = columns(a[n + "ln_l_g"], a[n + "ln_l_b"], a[n + "ln_x_g"], a[n + "ln_x_b"])
    arrays["l3_gam"] = np.stack([np.concatenate([a[n + "q_gamma"]] * 2), np.concatenate([a[n + "k_gamma"]] * 2)], 1)
    arrays["l3_bo"] = a[n + "b_out"]
    n = "L3_ffn_"
    w = a[n + "w_qkv"]
    for k, v in pack16(w[:, :D], None, w[:, D:2 * D], None, w[:, 2 * D:], None, a[n + "w_proj"], None).items():
        arrays["l3a_" + k] = v
    arrays["l3_ln1"] = columns(a[n + "ln1_w"], a[n + "ln1_b"])
    arrays["l3_ln2"] = columns(a[n + "ln2_w"], a[n + "ln2_b"])
    arrays["l3e_gate"], arrays["l3e_down"] = pack_experts(a[n + "w1"]), pack_experts(a[n + "w2"])
    arrays["l3f_wr"], arrays["l3f_br"] = a[n + "gate_w"], a[n + "gate_b"]
    arrays.update(numbers())
    return arrays
```

```python
from contextlib import ExitStack

import concourse.bass as bass
from concourse import mybir
import numpy as np

P = 128
B, S, D = 2, 1024, 256
TOK = B * S
KD = D // P
NT = S // P
TT = TOK // P
CH = 512
NC = TOK // CH
CT = CH // P
SC = 77
F32 = mybir.dt.float32
BF16 = mybir.dt.bfloat16
U32 = mybir.dt.uint32
U8 = mybir.dt.uint8
ALU = mybir.AluOpType
ACT = mybir.ActivationFunctionType
AX = mybir.AxisListType
EPS = 1e-5
EXPERTS = 8
SLOTS = 256
ROUND = 1.5 * 2.0 ** 23


class Tally:

    def __init__(self, eng, sem, per_pass=0, turn=0):
        self.eng, self.sem, self.per_pass, self.n = eng, sem, per_pass, 0
        self.base = turn * per_pass if per_pass else 0

    def add(self, ins):
        self.n += 1
        ins.then_inc(self.sem, 1)

    def wait(self, passed=None):
        if passed is None:
            self.eng.wait_ge(self.sem, self.base + self.n)
        else:
            pause(self.eng, self.sem, self.base + self.n, passed)

    def close(self):
        assert self.n == self.per_pass, f"{self.n} steps, {self.per_pass} declared"


def pause(eng, sem, value, passed):
    eng.wait_ge(sem, value)
    eng.sem_inc(passed, 1)


def tiles_of(dram, first, n):
    return dram[bass.ds(first, n * P), :].rearrange("(t p) d -> p t d", p=P)


def row_tile(dram, parts):
    return dram.partition_broadcast(parts)


class Consts:

    def __init__(self, nc):
        self.nc, self.taken = nc, []

    def semaphore(self, name):
        self.taken.append(self.nc.alloc_semaphore(name))
        return self.taken[-1]

    def end_stage(self):
        self.nc.clear_and_free_semaphores(self.taken)
        self.nc.all_engine_barrier()
        self.taken = []


def slot_tiles(top):
    return (TOK * top + EXPERTS * (SLOTS - 1)) // SLOTS


class Kept:
    pass


def setup(nc, ctx, io):
    c = Consts(nc)

    def sb(name, shape, dt=F32):
        return ctx.enter_context(nc.sbuf_tensor(name, shape, dt))

    c.ident = sb("ident", [P, P])
    c.ones = sb("ones", [P, P])
    c.earlier = sb("earlier", [P, P])
    c.zeros = sb("zeros", [P, D])
    c.eps = sb("eps", [P, 1])
    c.gates = sb("gates", [P, 8])
    c.half64 = sb("half64", [P, P])
    gates_loaded = c.semaphore("gates_loaded")
    consts_step = c.semaphore("consts_step")
    gates_done = c.semaphore("gates_done")
    c.cleared = nc.alloc_semaphore("cleared")
    io["slots_in"] = nc.dram_tensor("slots_in", (slot_tiles(2) * SLOTS, D), F32, kind="Internal").ap()
    io["slots_out"] = nc.dram_tensor("slots_out", (slot_tiles(2) * SLOTS, D), F32, kind="Internal").ap()
    with nc.Block() as block:
        @block.sync
        def _(sp):
            sp.dma_start(c.gates[:, 0:4], row_tile(io["g_xattn"], P)).then_inc(gates_loaded, 16)
            sp.dma_start(c.gates[:, 4:8], row_tile(io["g_ffn"], P)).then_inc(gates_loaded, 16)

        @block.gpsimd
        def _(pool):
            step = Tally(pool, consts_step)
            step.add(pool.memset(c.ident[:], 0.0))
            step.add(pool.memset(c.ones[:], 1.0))
            step.add(pool.memset(c.zeros[:], 0.0))
            step.add(pool.memset(c.earlier[:], 1.0))
            step.add(pool.memset(c.eps[:], EPS))
            step.add(pool.memset(c.half64[:], 0.0))
            step.wait()
            step.add(pool.memset(c.half64[0:64, 0:64], 1.0))
            step.add(pool.memset(c.half64[64:128, 64:128], 1.0))
            step.wait()
            step.add(pool.affine_select(out=c.ident[:], in_=c.ident[:], compare_op=ALU.not_equal, fill=1.0,
                                        base=0, pattern=[[-1, P]], channel_multiplier=1))
            step.add(pool.affine_select(out=c.earlier[:], in_=c.earlier[:], compare_op=ALU.is_gt, fill=0.0,
                                        base=0, pattern=[[1, P]], channel_multiplier=-1))
            step.wait()

        @block.scalar
        def _(act):
            act.wait_ge(gates_loaded, 32)
            nc.scalar.activation(c.gates[:], c.gates[:], ACT.Tanh).then_inc(gates_done, 1)
            act.wait_ge(gates_done, 1)
    c.end_stage()
    return c


def norm_stats(nc, dve, step, x, stats, mv, n, parts=P):
    for t in range(n):
        step.add(nc.vector.bn_stats(stats[0:parts, t, :], x[0:parts, t, :]))
    step.wait()
    for t in range(n):
        step.add(nc.vector.bn_aggr(mv[0:parts, t, :], stats[0:parts, t, :]))


def norm_apply(nc, dve, step, out, x, mv, rstd, std, n, parts=P):
    step.add(nc.vector.reciprocal(rstd[0:parts, 0:n], std[0:parts, 0:n]))
    step.wait()
    for t in range(n):
        step.add(nc.vector.tensor_scalar(out[0:parts, t, :], x[0:parts, t, :], mv[0:parts, t, 0:1],
                                         rstd[0:parts, t:t + 1], ALU.subtract, ALU.mult))


Q_TERMS = (0, 1, 2, 0, 1, 0)
K_TERMS = (0, 0, 0, 1, 1, 2)
TERM_ROWS = 16 * len(Q_TERMS)
FAR_PARTS = (-998244352.0, -1753088.0, -2560.0)


def attention16(nc, c, name, x_in, x_out, w, gate, ctx_t=None, mask=None, ln=None, twice=False, slots=None):
    H, QUADS = 16, 4
    cross = ctx_t is not None
    nk = SC if cross else S
    n_kt = 1 if cross else NT
    kw = nk if cross else P
    mask_at = TERM_ROWS + 3
    ITEMS = 4 * n_kt
    BURSTS = ITEMS // 2
    HALVES = 2 * ITEMS
    IB, HB = QUADS * ITEMS, QUADS * HALVES
    MG = 1 if cross else QUADS
    GQ, GH = QUADS // MG, 16 // MG
    rounds = 2 if twice else 1
    with ExitStack() as ctx:
        def sb(n, shape, dt=F32):
            return ctx.enter_context(nc.sbuf_tensor(f"{name}_{n}", shape, dt))

        def sem(n):
            return c.semaphore(f"{name}_{n}")

        scores = ctx.enter_context(nc.psum_tensor(f"{name}_scores", [P, 4, 512], F32))
        for_max = ctx.enter_context(nc.psum_tensor(f"{name}_for_max", [P, 2, 512], F32))
        pv = ctx.enter_context(nc.psum_tensor(f"{name}_pv", [P, 2, 512], F32))
        s2 = [scores[:, 2 * i:2 * i + 2, :].rearrange("p a n -> p (a n)") for i in range(2)]
        sall = scores[:].rearrange("p a n -> p (a n)")

        x, xn = sb("x", [P, NT, D]), sb("xn", [P, NT, D])
        stats, mv = sb("stats", [P, NT, 6]), sb("mv", [P, NT, 2])
        std, rstd = sb("std", [P, NT]), sb("rstd", [P, NT])
        xT = sb("xT", [P, KD, S])
        wq, wk = sb("wq", [P, KD, D]), sb("wk", [P, KD, D])
        wv, wo = sb("wv", [P, KD, 2 * D]), sb("wo", [P, QUADS, D])
        bqk, bv = sb("bqk", [P, 4]), sb("bv", [P, 2 * D])
        full = [sb(f"full{i}", [P, S]) for i in range(2)]
        rest = [sb(f"rest{i}", [P, S]) for i in range(2)]
        parts = [sb(f"parts{i}", [P, 3, S], BF16) for i in range(2)]
        QS, KS = sb("QS", [P, H, S], BF16), sb("KS", [P, H, nk], BF16)
        V = sb("V", [P, n_kt, 2 * D])
        halves = sb("halves", [P, 2, P])
        mx = sb("mx", [P, P])
        neg, neg_parts = sb("neg", [GH * NT, 2, P]), sb("neg_parts", [GH * NT, 3, P], BF16)
        probs = sb("probs", [P, 4, S])
        raw, rsum = sb("raw", [P, CH]), sb("rsum", [P, CH])
        OT = sb("OT", [P, QUADS, S])
        if cross:
            cT, cb = sb("cT", [P, KD, B * SC]), sb("cb", [P, KD, SC])
        if mask is not None:
            mask_in, mask_b = sb("mask_in", [1, B * SC]), sb("mask_b", [1, SC], BF16)
            far = sb("far", [1, 3, S], BF16)
        if ln is not None:
            lnw = sb("lnw", [P, KD, 2])

        names = ("x_loaded cst_loaded rows_set far_placed var_ready std_ready xn_ready xt_psum xt_ready c_ready proj full_ready high_ready rest_ready "
                 "mid_ready low_ready stacked mask_ready mask_placed v_ready max_psum max_done mxt_ready mx_ready rsum_ready neg_ready max_placed s_ready "
                 "exp_done pv_done raw_ready ot_ready wo_done out_ready stored step quad_step zeroed sp_passed dve_passed pool_passed").split()
        s = {n: sem(n) for n in names}
        consts = [(wq, w["q"]), (wk, w["k"]), (wv, w["v"]), (wo, w["o"]), (bqk, w["bqk"]), (bv, row_tile(w["bv"], P))]
        if cross:
            consts.append((cT, ctx_t.rearrange("(k p) n -> p k n", p=P)))
        if mask is not None:
            consts.append((mask_in, mask.rearrange("b n -> (b n)").unsqueeze(0)))
        if ln is not None:
            consts.append((lnw, ln))
        n_cst = 16 * len(consts)
        STACKS = 4
        block = ctx.enter_context(nc.Block())

        def quad_items(q):
            for h in range(2):
                for kt in range(n_kt):
                    for pair in range(2):
                        yield (h * n_kt + kt) * 2 + pair, 4 * q + 2 * pair, h, kt

        @block.sync
        def _(sp):
            for dst, src in consts:
                sp.dma_start(dst[:], src).then_inc(s["cst_loaded"], 16)
            if mask is not None:
                sp.wait_ge(s["rows_set"], 2 + 3)
                for i in range(3):
                    sp.dma_start(QS[mask_at + i:mask_at + i + 1, :, :],
                                 far[:, i, :].unsqueeze(1).broadcast_to([1, H, S])).then_inc(s["far_placed"], 16)
            with sp.Fori(0, B) as b:
                first = sp.snap(b * S)
                sp.dma_start(x[:], tiles_of(x_in, first, NT)).then_inc(s["x_loaded"], 16)
                if mask is not None:
                    sp.wait_ge(s["mask_ready"], b + 1)
                    for i in range(3):
                        sp.dma_start(KS[mask_at + i:mask_at + i + 1, :, :],
                                     mask_b[:].unsqueeze(1).broadcast_to([1, H, SC])).then_inc(s["mask_placed"], 16)
                for i in range(STACKS):
                    half, key = divmod(i, 2)
                    heads = slice(8 * half, 8 * half + 8)
                    sp.wait_ge(s["low_ready"], b * STACKS + i + 1)
                    for r, term in enumerate(K_TERMS if key else Q_TERMS):
                        n = nk if key else S
                        sp.dma_start((KS if key else QS)[16 * r:16 * r + 16, heads, :], parts[key][:, term, 0:n]).then_inc(s["stacked"], 16)
                for g in range(MG):
                    sp.wait_ge(s["neg_ready"], b * MG + g + 1)
                    for i in range(3):
                        sp.dma_start(QS[TERM_ROWS + i:TERM_ROWS + i + 1, GH * g:GH * g + GH, :], neg_parts[:, i, :]).then_inc(s["max_placed"], 16)
                sp.wait_ge(s["out_ready"], b + 2)
                sp.dma_start(tiles_of(x_out, first, NT), x[:]).then_inc(s["stored"], 16)
                pause(sp, s["stored"], b * 16 + 16, s["sp_passed"])

        @block.gpsimd
        def _(pool):
            pool.memset(KS[TERM_ROWS:P, :, :], 1.0).then_inc(s["rows_set"], 1)
            pool.memset(QS[TERM_ROWS:P, :, :], 0.0).then_inc(s["rows_set"], 1)
            if mask is not None:
                for i in range(3):
                    pool.memset(far[:, i, :], FAR_PARTS[i]).then_inc(s["rows_set"], 1)
            if slots is not None:
                pool.dma_start(slots.rearrange("(n p) d -> p n d", p=P),
                               c.zeros[:].unsqueeze(1).broadcast_to([P, slots.shape[0] // P, D])).then_inc(c.cleared, 16)
            with pool.Fori(0, B - 1) as b:
                pause(pool, s["out_ready"], b + 2, s["pool_passed"])
                pool.memset(QS[TERM_ROWS:TERM_ROWS + 3, :, :], 0.0).then_inc(s["zeroed"], 1)

        @block.tensor
        def _(pe):
            pe.wait_ge(s["cst_loaded"], n_cst)
            with pe.Fori(0, B) as b:
                pe.wait_ge(s["xn_ready"], (b + 1) * rounds)
                pe.wait_ge(s["out_ready"], b + 1)
                for k in range(KD):
                    for t in range(NT):
                        last = nc.tensor.transpose(s2[k][:, t * P:(t + 1) * P], xn[:, t, k * P:(k + 1) * P] if not twice else x[:, t, k * P:(k + 1) * P],
                                                   c.ident[:])
                last.then_inc(s["xt_psum"], 1)
                pe.wait_ge(s["xt_ready"], b * KD + KD)
                if cross:
                    pe.wait_ge(s["c_ready"], b + 1)
                for i in range(STACKS):
                    half, key = divmod(i, 2)
                    if i >= 2:
                        pe.wait_ge(s["full_ready"], b * STACKS + i - 1)
                    src, n = (cb, SC) if key and cross else (xT, S)
                    for lo in range(0, n, CH):
                        wide = min(CH, n - lo)
                        for k in range(KD):
                            last = nc.tensor.matmul(s2[key][:, lo:lo + wide], (wk if key else wq)[:, k, half * P:(half + 1) * P],
                                                    src[:, k, lo:lo + wide], start=k == 0, stop=k == KD - 1)
                    last.then_inc(s["proj"], 1)
                for t in range(n_kt):
                    if t >= 2:
                        pe.wait_ge(s["v_ready"], b * n_kt + t - 1)
                    for k in range(KD):
                        last = nc.tensor.matmul(pv[0:kw, t % 2, :], (cb if cross else xT)[:, k, t * P:t * P + kw], wv[:, k, :],
                                                start=k == 0, stop=k == KD - 1)
                    last.then_inc(s["proj"], 1)

                def half_step(q, i):
                    n = q * HALVES + i
                    if n >= 2:
                        pe.wait_ge(s["max_done"], b * HB + n - 1)
                    if n == 0 or n == 2 * HALVES:
                        pe.wait_ge(s["stacked"], b * STACKS * 96 + (192 if n == 0 else 384))
                        if n == 0 and mask is not None:
                            pe.wait_ge(s["mask_placed"], b * 48 + 48)
                            pe.wait_ge(s["far_placed"], 32)
                        if n == 0:
                            pe.wait_ge(s["rows_set"], 2)
                            pe.wait_ge(s["zeroed"], b + 1)
                    if cross:
                        h = 4 * q + i // 2
                        for t in range(4):
                            at = (i % 2 * 4 + t) * P
                            last = nc.tensor.matmul(for_max[:, i % 2, t * P:t * P + SC], QS[:, h, at:at + P], KS[:, h, :],
                                                    start=True, stop=True)
                    else:
                        h, at = 4 * q + i // 16, i % 16 // 2 * P
                        last = nc.tensor.matmul(for_max[:, i % 2, :], QS[:, h, at:at + P], KS[:, h, i % 2 * CH:i % 2 * CH + CH],
                                                start=True, stop=True)
                    last.then_inc(s["max_psum"], 1)

                def turn_max(g):
                    pe.wait_ge(s["mx_ready"], b * MG + g + 1)
                    nc.tensor.transpose(for_max[:, 0, 0:P], mx[:], c.ident[:]).then_inc(s["mxt_ready"], 1)

                def values(q, burst):
                    h, kt = divmod(burst, n_kt)
                    chunk = 2 * q + h
                    if kt == 0 and chunk >= 2:
                        pe.wait_ge(s["raw_ready"], b * 2 * QUADS + chunk - 1)
                    pe.wait_ge(s["exp_done"], b * IB + q * ITEMS + 2 * burst + 2)
                    for j in range(4):
                        col = 32 * (4 * q + j)
                        last = nc.tensor.matmul(pv[32 * j:32 * j + 32, h, :], V[0:kw, kt, col:col + 32],
                                                probs[0:kw, (2 * burst + j // 2) % 4, j % 2 * CH:j % 2 * CH + CH],
                                                start=kt == 0, stop=kt == n_kt - 1, tile_position=(0, 32 * j))
                    last.then_inc(s["pv_done"], 1)

                for q in range(GQ):
                    for i in range(HALVES):
                        half_step(q, i)
                turn_max(0)
                pe.wait_ge(s["v_ready"], b * n_kt + n_kt)
                for q in range(QUADS):
                    more = MG > 1 and q + 1 < QUADS
                    if q % GQ == 0:
                        pe.wait_ge(s["max_placed"], b * MG * 48 + q // GQ * 48 + 48)
                    for i, h0, h, kt in quad_items(q):
                        n = q * ITEMS + i
                        if more:
                            half_step(q + 1, 2 * i)
                        if n >= 2:
                            pe.wait_ge(s["exp_done"], b * IB + n - 1)
                        for j in range(2):
                            last = nc.tensor.matmul(s2[i % 2][0:kw, j * CH:(j + 1) * CH], KS[:, h0 + j, kt * P:kt * P + kw],
                                                    QS[:, h0 + j, h * CH:(h + 1) * CH], start=True, stop=True)
                        last.then_inc(s["s_ready"], 1)
                        if more:
                            half_step(q + 1, 2 * i + 1)
                        if i >= 2 and i % 2 == 0:
                            values(q, i // 2 - 1)
                    if more:
                        turn_max(q + 1)
                    values(q, BURSTS - 1)
                pe.wait_ge(s["ot_ready"], b * 2 * QUADS + 2 * QUADS)
                for t in range(NT):
                    for q in range(QUADS):
                        last = nc.tensor.matmul(sall[:, t * D:(t + 1) * D], OT[:, q, t * P:(t + 1) * P], wo[:, q, :],
                                                start=q == 0, stop=q == QUADS - 1)
                last.then_inc(s["wo_done"], 1)

        @block.scalar
        def _(act):
            act.wait_ge(s["cst_loaded"], n_cst)
            with act.Fori(0, B) as b:
                if cross:
                    nc.scalar.activation(cb[:], cT[:, :, bass.ds(b * SC, SC)], ACT.Copy).then_inc(s["c_ready"], 1)
                for r in range(rounds):
                    act.wait_ge(s["var_ready"], b * rounds + r + 1)
                    nc.scalar.activation(std[:], mv[:, :, 1], ACT.Sqrt, bias=c.eps[:, 0:1]).then_inc(s["std_ready"], 1)
                act.wait_ge(s["xt_psum"], b + 1)
                for k in range(KD):
                    if ln is not None:
                        ins = nc.scalar.activation(xT[:, k, :], s2[k], ACT.Identity, bias=lnw[:, k, 1:2], scale=lnw[:, k, 0:1])
                    else:
                        ins = nc.scalar.activation(xT[:, k, :], s2[k], ACT.Copy)
                    ins.then_inc(s["xt_ready"], 1)
                for i in range(STACKS):
                    n = nk if i % 2 else S
                    u = b * STACKS + i
                    act.wait_ge(s["full_ready"], u + 1)
                    if i >= 2:
                        act.wait_ge(s["stacked"], b * STACKS * 96 + 96 * 2)
                    nc.scalar.activation(parts[i % 2][:, 0, 0:n], full[i % 2][:, 0:n], ACT.Copy).then_inc(s["high_ready"], 1)
                    act.wait_ge(s["rest_ready"], u + 1)
                    nc.scalar.activation(parts[i % 2][:, 1, 0:n], rest[i % 2][:, 0:n], ACT.Copy).then_inc(s["mid_ready"], 1)
                for n in range(IB):
                    i = n % ITEMS
                    act.wait_ge(s["s_ready"], b * IB + n + 1)
                    if n >= 4:
                        act.wait_ge(s["pv_done"], b * QUADS * BURSTS + n // 2 - 1)
                    nc.scalar.activation(probs[0:kw, i % 4, :], s2[i % 2][0:kw, :], ACT.Exp).then_inc(s["exp_done"], 1)

        @block.vector
        def _(dve):
            dve.sem_inc(s["zeroed"], 1)
            dve.memset(mx[:], 0.0).then_inc(s["out_ready"], 1)
            dve.wait_ge(s["cst_loaded"], n_cst)
            with dve.Fori(0, B) as b:
                step = Tally(dve, s["step"], rounds * (3 * NT - 1), b)
                if mask is not None:
                    nc.vector.tensor_copy(mask_b[:], mask_in[:, bass.ds(b * SC, SC)]).then_inc(s["mask_ready"], 1)
                dve.wait_ge(s["x_loaded"], b * 16 + 16)
                for r in range(rounds):
                    src, dst = ((x, xn), (xn, x))[r]
                    for t in range(NT):
                        step.add(nc.vector.bn_stats(stats[:, t, :], src[:, t, :]))
                    step.wait(s["dve_passed"])
                    for t in range(NT):
                        ins = nc.vector.bn_aggr(mv[:, t, :], stats[:, t, :])
                        if t < NT - 1:
                            step.add(ins)
                    ins.then_inc(s["var_ready"], 1)
                    dve.wait_ge(s["std_ready"], b * rounds + r + 1)
                    step.add(nc.vector.reciprocal(rstd[:], std[:]))
                    step.wait()
                    for t in range(NT):
                        ins = nc.vector.tensor_scalar(dst[:, t, :], src[:, t, :], mv[:, t, 0:1], rstd[:, t:t + 1],
                                                      ALU.subtract, ALU.mult)
                        if t < NT - 1:
                            step.add(ins)
                    ins.then_inc(s["xn_ready"], 1)
                    if r < rounds - 1:
                        dve.wait_ge(s["xn_ready"], b * rounds + r + 1)
                step.close()
                for i in range(STACKS):
                    half, key = divmod(i, 2)
                    n = nk if key else S
                    u = b * STACKS + i
                    dve.wait_ge(s["proj"], b * (STACKS + n_kt) + i + 1)
                    if i >= 2:
                        dve.wait_ge(s["low_ready"], u - 1)
                    bias = bqk[:, 2 * key + half:2 * key + half + 1]
                    nc.vector.tensor_scalar(full[key][:, 0:n], s2[key][:, 0:n], bias, 1.0 if key else 0.25, ALU.add, ALU.mult).then_inc(s["full_ready"], 1)
                    dve.wait_ge(s["full_ready"], u + 1)
                    dve.wait_ge(s["high_ready"], u + 1)
                    nc.vector.tensor_tensor(rest[key][:, 0:n], full[key][:, 0:n], parts[key][:, 0, 0:n], ALU.subtract).then_inc(s["rest_ready"], 1)
                    dve.wait_ge(s["mid_ready"], u + 1)
                    dve.wait_ge(s["rest_ready"], u + 1)
                    nc.vector.tensor_tensor(parts[key][:, 2, 0:n], rest[key][:, 0:n], parts[key][:, 1, 0:n], ALU.subtract).then_inc(s["low_ready"], 1)
                for t in range(n_kt):
                    dve.wait_ge(s["proj"], b * (STACKS + n_kt) + STACKS + t + 1)
                    nc.vector.tensor_tensor(V[0:kw, t, :], pv[0:kw, t % 2, :], bv[0:kw, :], ALU.add).then_inc(s["v_ready"], 1)

                turn = Tally(dve, s["quad_step"], 4 * MG + 2 * QUADS, b)

                def half_step(q, i):
                    dve.wait_ge(s["max_psum"], b * HB + q * HALVES + i + 1)
                    if cross:
                        col = 32 * q + 4 * i
                        ins = nc.vector.tensor_reduce(mx[:, col:col + 4], for_max[:, i % 2, :].rearrange("p (t n) -> p t n", t=4)[:, :, 0:SC],
                                                      AX.X, ALU.max)
                    else:
                        ins = nc.vector.tensor_reduce(halves[:, i % 2, i // 2:i // 2 + 1], for_max[:, i % 2, :], AX.X, ALU.max)
                    ins.then_inc(s["max_done"], 1)

                def negate(g):
                    dve.wait_ge(s["max_done"], b * HB + (g + 1) * GQ * HALVES)
                    if cross:
                        dve.sem_inc(s["mx_ready"], 1)
                    else:
                        nc.vector.tensor_tensor(mx[:, 0:32], halves[:, 0, 0:32], halves[:, 1, 0:32], ALU.max).then_inc(s["mx_ready"], 1)
                    dve.wait_ge(s["mxt_ready"], b * MG + g + 1)
                    if g >= 1:
                        dve.wait_ge(s["max_placed"], b * MG * 48 + g * 48)
                    turn.add(nc.vector.tensor_scalar(neg[:, 0, :], for_max[0:GH * NT, 0, 0:P], -1.0, None, ALU.mult))
                    turn.wait()
                    turn.add(nc.vector.tensor_copy(neg_parts[:, 0, :], neg[:, 0, :]))
                    turn.wait()
                    turn.add(nc.vector.tensor_tensor(neg[:, 1, :], neg[:, 0, :], neg_parts[:, 0, :], ALU.subtract))
                    turn.wait()
                    turn.add(nc.vector.tensor_copy(neg_parts[:, 1, :], neg[:, 1, :]))
                    turn.wait()
                    nc.vector.tensor_tensor(neg_parts[:, 2, :], neg[:, 1, :], neg_parts[:, 1, :], ALU.subtract).then_inc(s["neg_ready"], 1)

                def norm_heads(q, h):
                    chunk = 2 * q + h
                    dve.wait_ge(s["pv_done"], b * QUADS * BURSTS + q * BURSTS + (h + 1) * n_kt)
                    if chunk >= 1:
                        dve.wait_ge(s["ot_ready"], b * 2 * QUADS + chunk)
                    nc.vector.tensor_copy(raw[:], pv[:, h, :]).then_inc(s["raw_ready"], 1)
                    pause(dve, s["raw_ready"], b * 2 * QUADS + chunk + 1, s["dve_passed"])
                    turn.add(nc.vector.stream_shuffle(rsum[:], raw[:], [16] * 32))
                    turn.wait()
                    nc.vector.reciprocal(rsum[:], rsum[:]).then_inc(s["rsum_ready"], 1)
                    dve.wait_ge(s["rsum_ready"], b * 2 * QUADS + chunk + 1)
                    nc.vector.tensor_tensor(OT[:, q, h * CH:(h + 1) * CH], raw[:], rsum[:], ALU.mult).then_inc(s["ot_ready"], 1)

                for q in range(GQ):
                    for i in range(HALVES):
                        half_step(q, i)
                negate(0)
                for q in range(QUADS):
                    if MG > 1 and q + 1 < QUADS:
                        behind = ITEMS + 4
                        for i in range(behind):
                            half_step(q + 1, i)
                        norm_heads(q, 0)
                        for i in range(behind, HALVES):
                            half_step(q + 1, i)
                        negate(q + 1)
                    else:
                        norm_heads(q, 0)
                    norm_heads(q, 1)
                turn.close()
                dve.wait_ge(s["wo_done"], b + 1)
                base = xn if twice else x
                xf, bf = x[:].rearrange("p t d -> p (t d)"), base[:].rearrange("p t d -> p (t d)")
                if gate is None:
                    ins = nc.vector.tensor_tensor(xf, sall, bf, ALU.add)
                else:
                    ins = nc.vector.scalar_tensor_tensor(xf, sall, c.gates[:, gate:gate + 1], bf, ALU.mult, ALU.add)
                ins.then_inc(s["out_ready"], 1)




def attention64(nc, c, name, x_in, x_out, w_qkv, w_o, gate, ctx_in, mask, ln, rms=None, out_ln=None, out_b=None):
    PAIRS = w_qkv.shape[0]
    U = B * PAIRS
    n_keys = S + SC
    KT = NT + 1
    HALF = S // 2
    HT = HALF // P
    ITEMS = 2 * KT
    STEPS = 2 * (2 * NT + 2)
    KINDS = "q k c v".split() if rms is None else "q qs k ks c cs v".split()
    NPROJ = len(KINDS)
    PROJ_AT = (1, 2, 3, 4) if rms is None else (1, 3, 4, 6, 7, 8, 9)
    PROBS = 4
    with ExitStack() as ctx:
        def sb(n, shape, dt=F32):
            return ctx.enter_context(nc.sbuf_tensor(f"{name}_{n}", shape, dt))

        lT_all = sb("lT_all", [P, KD, TOK])
        keep = normed(nc, ctx, c, f"{name}n", x_in, "twice", ln, ((lT_all, True),))
        x = keep.x
        slots = ctx.enter_context(nc.psum_tensor(f"{name}_slots", [P, 4, 512], F32))
        for_max = ctx.enter_context(nc.psum_tensor(f"{name}_for_max", [P, 2, 512], F32))
        pv = ctx.enter_context(nc.psum_tensor(f"{name}_pv", [P, HALF], F32))
        rs = ctx.enter_context(nc.psum_tensor(f"{name}_rs", [P, HALF], F32))
        s2 = [slots[:, 2 * i:2 * i + 2, :].rearrange("p a n -> p (a n)") for i in range(2)]

        acc = sb("acc", [P, TT, D])
        cx = sb("cx", [SC, B, D])
        stats, mv = sb("stats", [P, CT, 6]), sb("mv", [P, CT, 2])
        std, rstd = sb("std", [P, CT]), sb("rstd", [P, CT])
        cT_all = sb("cT_all", [P, KD, B * SC])
        lT, cT = sb("lT", [P, KD, S]), sb("cT", [P, KD, SC])
        lnw = sb("lnw", [P, KD, 4])
        w = [sb(f"w{i}", [P, 3, KD, P]) for i in range(2)]
        wo = sb("wo", [P, PAIRS, D])
        Q = [[sb(f"Q{i}{e}", [P, S]) for e in range(2)] for i in range(2)]
        K = [[sb(f"K{i}{e}", [P, KT * P]) for e in range(2)] for i in range(2)]
        Qb = [[sb(f"Qb{i}{e}", [P, S], BF16) for e in range(2)] for i in range(2)]
        Kb = [[sb(f"Kb{i}{e}", [P, n_keys], BF16) for e in range(2)] for i in range(2)]
        V = [sb(f"V{i}", [P, KT, P]) for i in range(2)]
        mx_half, mx_c, mx = sb("mx_half", [P, 2, 2 * NT]), sb("mx_c", [P, 2 * NT]), sb("mx", [P, P])
        neg = sb("neg", [2 * NT, P])
        probs = sb("probs", [P, PROBS, 2, HALF])
        added = [sb(f"added{h}", [P, 2, HALF]) for h in range(2)]
        raw = [sb(f"raw{h}", [P, HALF]) for h in range(2)]
        rsum = sb("rsum", [P, HALF])
        OT = [sb(f"OT{h}", [P, HALF]) for h in range(2)]
        mask_in = sb("mask_in", [1, B * SC], U8)
        mrow, mrow_b = sb("mrow", [1, B * SC]), sb("mrow_b", [1, B * SC], BF16)
        ob = sb("ob", [P, D])
        consts = [(lnw, ln), (wo, w_o)]
        if rms is not None:
            gam, sq = sb("gam", [P, 2]), sb("sq", [P, S])
            roots, raws = [[sb(f"{n}{j}", [P, wide]) for j, wide in enumerate((S, S, SC))] for n in ("root", "qk_raw")]
            consts.append((gam, rms))
        if out_ln is not None:
            og = sb("og", [P, D])
            consts += [(og, row_tile(out_ln[0], P)), (ob, row_tile(out_ln[1], P))]
        if out_b is not None:
            consts.append((ob, row_tile(out_b, P)))
        n_cst = 16 * len(consts)

        names = ("c_loaded cst_loaded mask_loaded mask_placed0 mask_placed1 rows_set mrow_ready w_loaded0 w_loaded1 var_ready std_ready xn_ready lt_ready "
                 "xt_psum xt_ready free0 free1 proj sq_ready root_ready norm_step full_ready q_ready k_ready kc_ready v_ready vc_ready "
                 "max_psum max_done mx_half_ready mx_ready mxt_ready neg_ready max_placed s_ready exp_done pv_done pool_added raw_ready sums_ready rsum_ready "
                 "ot_ready wo_done out_ready stored dve_step dve_tail tail_var tail_std sp_passed pe_passed dve_passed pool_passed")
        s = {n: c.semaphore(f"{name}_{n}") for n in names.split()}
        free = [s["free0"], s["free1"]]
        AHEAD = 2

        def projections(m):
            return [("proj", kind, m + j) for j, kind in enumerate(KINDS)]

        def phase_plan(m, first, more):
            events = []
            start = PROJ_AT[-1] + 2
            per = -(-STEPS // (16 - start))
            step = 0
            for n in range(ITEMS):
                if n == 1 and not first:
                    events.append(("sums", -1, None))
                if n in PROJ_AT and more:
                    events.append(("proj", KINDS[PROJ_AT.index(n)], m))
                    m += 1
                if n == 4 and not first:
                    events.append(("wo", -1, m))
                    m += 1
                if n == KT + 2:
                    events.append(("sums", 0, None))
                if n == KT + 5:
                    events.append(("wo", 0, m))
                    m += 1
                steps = range(step, min(STEPS, step + per)) if more and n >= start else range(0)
                step += len(steps)
                events += [("max", k, None) for k in steps[:per // 2]]
                events.append(("item", n, m))
                m += 1
                events += [("max", k, None) for k in steps[per // 2:]]
                if n >= 1:
                    events.append(("values", n - 1, None))
                if more and n == 16:
                    assert step == STEPS
                    events.append(("turn", None, None))
            events.append(("values", ITEMS - 1, None))
            if not more:
                events += [("sums", 1, None), ("wo", 1, m)]
                m += 1
            return events, m

        first_plan, m1 = phase_plan(NPROJ, True, True)
        plan_a, m2 = phase_plan(m1, False, True)
        plan_b, m3 = phase_plan(m2, False, True)
        LOOPS = (U - 2) // 2
        last_plan, m_end = phase_plan(m3, False, False)
        BODY = m3 - m1
        USES = m_end + BODY * (LOOPS - 1)
        assert BODY % 2 == 0 and U % 2 == 0 and LOOPS >= 1

        def phases(eng, run):
            run(first_plan, 0, 0, 0)
            with eng.Fori(0, LOOPS) as r:
                run(plan_a, r * 2 + 1, 1, r)
                run(plan_b, r * 2 + 2, 0, r)
            run(last_plan, U - 1, 1, LOOPS - 1)

        block = ctx.enter_context(nc.Block())

        @block.sync
        def _(sp):
            for dst, src in consts:
                sp.dma_start(dst[:], src).then_inc(s["cst_loaded"], 16)

            def load_w(pair, i):
                sp.dma_start(w[i][:], w_qkv[bass.ds(pair, 1)].rearrange("o p a k d -> (o p) a k d")).then_inc(s[f"w_loaded{i}"], 16)

            def place(n, i):
                sp.wait_ge(s["neg_ready"], n + 1)
                for e in range(2):
                    sp.dma_start(Q[i][e][65:66, :], neg[NT * e:NT * e + NT, :]).then_inc(s["max_placed"], 16)

            sp.dma_start(cx[:], ctx_in.rearrange("(b p) d -> p b d", p=SC)).then_inc(s["c_loaded"], 16)
            sp.dma_start(mask_in[:], mask.rearrange("b n -> (b n)").unsqueeze(0)).then_inc(s["mask_loaded"], 16)
            for i in range(2):
                load_w(i, i)
            sp.wait_ge(s["rows_set"], 38)
            sp.wait_ge(s["mrow_ready"], 2)

            def place_mask(first, i):
                for e in range(2):
                    sp.dma_start(K[i][e][64:65, S:n_keys], mrow[:, bass.ds(first, SC)]).then_inc(s[f"mask_placed{i}"], 16)
                    sp.dma_start(Kb[i][e][64:65, S:n_keys], mrow_b[:, bass.ds(first, SC)]).then_inc(s[f"mask_placed{i}"], 16)

            def latents(first, first_c):
                sp.dma_start(lT[:], lT_all[:, :, bass.ds(first, S)]).then_inc(s["lt_ready"], 16)
                sp.dma_start(cT[:], cT_all[:, :, bass.ds(first_c, SC)]).then_inc(s["lt_ready"], 16)

            for i in range(2):
                place_mask(0, i)
            sp.wait_ge(s["xt_ready"], KD * B)
            latents(0, 0)
            place(0, 0)
            with sp.Fori(0, LOOPS) as r:
                for i in range(2):
                    n = r * 2 + i
                    ahead, row = sp.snap((n + 2) % PAIRS), sp.snap((n + 2) // PAIRS * SC)
                    tok = sp.snap((n + 2) // PAIRS * S)
                    load_w(ahead, i)
                    pause(sp, s["proj"], n * NPROJ + 2 * NPROJ, s["sp_passed"])
                    latents(tok, row)
                    place(n + 1, 1 - i)
                    pause(sp, s["s_ready"], n * ITEMS + ITEMS, s["sp_passed"])
                    place_mask(row, i)
            place(U - 1, 1)
            for n in range(NC):
                sp.wait_ge(s["out_ready"], n + 1)
                sp.dma_start(tiles_of(x_out, n * CH, CT), x[:, n * CT:(n + 1) * CT, :]).then_inc(s["stored"], 16)
            sp.wait_ge(s["stored"], 16 * NC)

        @block.gpsimd
        def _(pool):
            pairs = [(i, e) for i in range(2) for e in range(2)]
            for i in range(2):
                pool.memset(V[i][:, NT, :], 0.0).then_inc(s["rows_set"], 1)
            pool.wait_ge(s["rows_set"], 2)
            for i, e in pairs:
                for t in (Q, Qb, K, Kb):
                    pool.memset(t[i][e][64:P, :], 0.0).then_inc(s["rows_set"], 1)
                pool.memset(K[i][e][0:64, n_keys:], 0.0).then_inc(s["rows_set"], 1)
            pool.wait_ge(s["rows_set"], 22)
            for i, e in pairs:
                pool.memset(Q[i][e][64:66, :], -1e30).then_inc(s["rows_set"], 1)
                pool.memset(Qb[i][e][64:65, :], -1e30).then_inc(s["rows_set"], 1)
                pool.memset(K[i][e][64:66, :], 1.0).then_inc(s["rows_set"], 1)
            pool.wait_ge(s["rows_set"], 34)
            for i, e in pairs:
                pool.memset(K[i][e][64:65, 0:n_keys], 0.0).then_inc(s["rows_set"], 1)
            pool.sem_inc(s["pool_added"], PROBS)

            def run(plan, at, i, r):
                for n in range(ITEMS):
                    h, kt = divmod(n, KT)
                    p = probs[:, (2 * i + n) % PROBS, :, :]
                    if kt == 0:
                        pool.wait_ge(s["sums_ready"], at * 2 + h + 1)
                    pause(pool, s["exp_done"], at * ITEMS + n + 1, s["pool_passed"])
                    if kt == 0:
                        ins = nc.gpsimd.tensor_copy(added[h][:], p)
                    else:
                        pause(pool, s["pool_added"], at * ITEMS + n + PROBS, s["pool_passed"])
                        ins = nc.gpsimd.tensor_tensor(added[h][:], added[h][:], p, ALU.add)
                    ins.then_inc(s["pool_added"], 1)

            phases(pool, run)

        @block.tensor
        def _(pe):
            pe.wait_ge(s["cst_loaded"], n_cst)
            def slot(m, r):
                pe.wait_ge(free[m % 2], r * (BODY // 2) + m // 2 + 1)
                return s2[m % 2]

            def project(kind, i, at, m, r, more=True):
                out = slot(m, r)
                halves = [slice(h * HALF, (h + 1) * HALF) for h in range(2)]
                if kind == "q":
                    pe.wait_ge(s["lt_ready"], at * 32 if more else 32)
                    pause(pe, s[f"w_loaded{i}"], (at - i) * 8 + 16, s["pe_passed"])
                if kind in ("q", "k"):
                    for h in halves:
                        for k in range(KD):
                            last = nc.tensor.matmul(out[:, h], w[i][:, 0 if kind == "q" else 1, k, :], lT[:, k, h], start=k == 0, stop=k == KD - 1)
                elif kind == "c":
                    for k in range(KD):
                        nc.tensor.matmul(out[:, 0:SC], w[i][:, 1, k, :], cT[:, k, :], start=k == 0, stop=k == KD - 1)
                    for k in range(KD):
                        last = nc.tensor.matmul(out[0:SC, CH:CH + P], cT[:, k, :], w[i][:, 2, k, :], start=k == 0, stop=k == KD - 1)
                elif kind == "v":
                    for t in range(NT):
                        for k in range(KD):
                            last = nc.tensor.matmul(out[:, t * P:(t + 1) * P], lT[:, k, t * P:(t + 1) * P], w[i][:, 2, k, :],
                                                    start=k == 0, stop=k == KD - 1)
                else:
                    pe.wait_ge(s["sq_ready"], at * 3 + "qkc".index(kind[0]) + 1)
                    for h in halves if kind != "cs" else [slice(0, SC)]:
                        last = nc.tensor.matmul(out[:, h], c.half64[:], sq[:, h], start=True, stop=True)
                last.then_inc(s["proj"], 1)

            def max_step(k, i, at):
                e, j = divmod(k, STEPS // 2)
                if k == 0:
                    for n in ("q_ready", "k_ready", "kc_ready"):
                        pe.wait_ge(s[n], at + 1)
                    pe.wait_ge(s[f"mask_placed{i}"], (at - i) * 32 + 64)
                if k >= 2:
                    pe.wait_ge(s["max_done"], at * STEPS + k - 1)
                if j < 2 * NT:
                    t, h = divmod(j, 2)
                    last = nc.tensor.matmul(for_max[:, k % 2, :], Qb[i][e][:, t * P:(t + 1) * P], Kb[i][e][:, h * CH:(h + 1) * CH],
                                            start=True, stop=True)
                else:
                    for n in range(4):
                        t = (j - 2 * NT) * 4 + n
                        last = nc.tensor.matmul(for_max[:, k % 2, n * P:n * P + SC], Qb[i][e][:, t * P:(t + 1) * P], Kb[i][e][:, S:n_keys],
                                                start=True, stop=True)
                last.then_inc(s["max_psum"], 1)

            def turn(at):
                pe.wait_ge(s["mx_ready"], at + 1)
                nc.tensor.transpose(for_max[:, 0, 0:P], mx[:], c.ident[:]).then_inc(s["mxt_ready"], 1)

            def run(plan, at, i, r):
                for event, n, m in plan:
                    if event == "proj":
                        project(n, 1 - i, at + 1, m, r)
                    elif event == "max":
                        max_step(n, 1 - i, at + 1)
                    elif event == "turn":
                        turn(at + 1)
                    elif event == "item":
                        h, kt = divmod(n, KT)
                        out = slot(m, r)
                        if n == 0:
                            pe.wait_ge(s["max_placed"], at * 32 + 32)
                        for e in range(2):
                            last = nc.tensor.matmul(out[:, e * HALF:(e + 1) * HALF], K[i][e][:, kt * P:(kt + 1) * P],
                                                    Q[i][e][:, h * HALF:(h + 1) * HALF], start=True, stop=True)
                        last.then_inc(s["s_ready"], 1)
                    elif event == "values":
                        h, kt = divmod(n, KT)
                        if n == 0:
                            pe.wait_ge(s["v_ready"], at + 1)
                            pe.wait_ge(s["vc_ready"], at + 1)
                        if kt == 0:
                            pe.wait_ge(s["raw_ready"], at * 2 + h + 1)
                        pe.wait_ge(s["exp_done"], at * ITEMS + n + 1)
                        for e in range(2):
                            last = nc.tensor.matmul(pv[64 * e:64 * e + 64, :], V[i][:, kt, 64 * e:64 * e + 64],
                                                    probs[:, (2 * i + n) % PROBS, e, :], start=kt == 0, stop=kt == KT - 1,
                                                    tile_position=(0, 64 * e))
                        last.then_inc(s["pv_done"], 1)
                    elif event == "sums":
                        h = n % 2
                        g = at * 2 + n
                        pe.wait_ge(s["ot_ready"], g + AHEAD)
                        pe.wait_ge(s["pool_added"], at * ITEMS + PROBS + (n + 1) * KT)
                        for e in range(2):
                            last = nc.tensor.matmul(rs[64 * e:64 * e + 64, :], c.ones[:, 0:64], added[h][:, e, :], start=True, stop=True,
                                                    tile_position=(0, 64 * e))
                        last.then_inc(s["sums_ready"], 1)
                    elif event == "wo":
                        h = n % 2
                        out = slot(m, r)
                        pe.wait_ge(s["ot_ready"], at * 2 + n + 1 + AHEAD)
                        rows = wo[:, bass.ds((at if n >= 0 else at - 1) % PAIRS, 1), :].rearrange("p o d -> p (o d)")
                        for t in range(HT):
                            last = nc.tensor.matmul(out[:, t * D:(t + 1) * D], OT[h][:, t * P:(t + 1) * P], rows, start=True, stop=True)
                        last.then_inc(s["wo_done"], 1)

            pe.wait_ge(s["xn_ready"], 1)
            for k in range(KD):
                for b in range(B):
                    last = nc.tensor.transpose(for_max[:, k, b * P:b * P + SC], cx[:, b, k * P:(k + 1) * P], c.ident[0:SC, 0:SC])
            last.then_inc(s["xt_psum"], 1)
            for _, kind, m in projections(0):
                project(kind, 0, 0, m, 0, False)
            pe.wait_ge(s["rows_set"], 38)
            for k in range(STEPS):
                max_step(k, 0, 0)
            turn(0)
            phases(pe, run)

        @block.scalar
        def _(act):
            act.wait_ge(s["cst_loaded"], n_cst)
            act.wait_ge(s["rows_set"], 2)
            def evacuate(kind, i, at, m, later):
                ps = s2[m % 2]
                act.wait_ge(s["proj"], at * NPROJ + KINDS.index(kind) + 1)
                if kind in ("q", "k", "c") and rms is None:
                    lo, n = (S, SC) if kind == "c" else (0, S)
                    for e in range(2):
                        r = slice(64 * e, 64 * e + 64)
                        ins = nc.scalar.activation((Q if kind == "q" else K)[i][e][0:64, lo:lo + n], ps[r, 0:n], ACT.Copy,
                                                   scale=0.125 if kind == "q" else 1.0)
                    ins.then_inc(s["full_ready"], 1)
                elif kind in ("q", "k", "c"):
                    n = SC if kind == "c" else S
                    j = "qkc".index(kind)
                    if later:
                        act.wait_ge(s[("q_ready", "k_ready", "kc_ready")[j]], at)
                    nc.scalar.activation(raws[j][:], ps[:, 0:n], ACT.Copy)
                    nc.scalar.activation(sq[:, 0:n], ps[:, 0:n], ACT.Square).then_inc(s["sq_ready"], 1)
                elif kind in ("qs", "ks", "cs"):
                    root = roots["qkc".index(kind[0])]
                    nc.scalar.activation(root[:], ps[:, 0:root.shape[1]], ACT.Sqrt).then_inc(s["root_ready"], 1)
                if kind == "c":
                    nc.scalar.activation(V[i][0:SC, NT, :], ps[0:SC, CH:CH + P], ACT.Copy).then_inc(s["vc_ready"], 1)
                if kind == "v":
                    nc.scalar.activation(V[i][:, 0:NT, :].rearrange("p t d -> p (t d)"), ps, ACT.Copy).then_inc(s["v_ready"], 1)
                j = "qkc".find(kind[0])
                if kind in ("c", "v"):
                    act.wait_ge(s["vc_ready" if kind == "c" else "v_ready"], at + 1)
                elif rms is None:
                    act.wait_ge(s["full_ready"], at * 3 + j + 1)
                else:
                    act.wait_ge(s["sq_ready" if len(kind) == 1 else "root_ready"], at * 3 + j + 1)
                act.sem_inc(free[m % 2], 1)

            def run(plan, at, i, r):
                for event, n, m in plan:
                    if event == "proj":
                        evacuate(n, 1 - i, at + 1, m, True)
                    elif event == "item":
                        act.wait_ge(s["s_ready"], at * ITEMS + n + 1)
                        act.wait_ge(s["pv_done"], at * ITEMS + n + 1)
                        act.wait_ge(s["pool_added"], at * ITEMS + n + 1)
                        nc.scalar.activation(probs[:, (2 * i + n) % PROBS, :, :].rearrange("p e n -> p (e n)"), s2[m % 2],
                                             ACT.Exp).then_inc(s["exp_done"], 1)
                        act.wait_ge(s["exp_done"], at * ITEMS + n + 1)
                        act.sem_inc(free[m % 2], 1)

            act.wait_ge(s["var_ready"], 1)
            nc.scalar.activation(std[0:SC, 0:B], mv[0:SC, 0:B, 1], ACT.Sqrt, bias=c.eps[0:SC, 0:1]).then_inc(s["std_ready"], 1)
            act.wait_ge(s["xt_psum"], 1)
            for k in range(KD):
                for b in range(B):
                    nc.scalar.activation(cT_all[:, k, b * SC:(b + 1) * SC], for_max[:, k, b * P:b * P + SC], ACT.Identity, bias=lnw[:, k, 3:4],
                                         scale=lnw[:, k, 2:3]).then_inc(s["xt_ready"], 1)
            act.wait_ge(s["xt_ready"], KD * B)
            for _, kind, m in projections(0):
                evacuate(kind, 0, 0, m, False)
            phases(act, run)
            if out_ln is not None:
                for n in range(NC):
                    act.wait_ge(s["tail_var"], n + 1)
                    nc.scalar.activation(std[:], mv[:, :, 1], ACT.Sqrt, bias=c.eps[:, 0:1]).then_inc(s["tail_std"], 1)

        @block.vector
        def _(dve):
            for n, ahead in (("free0", 1), ("free1", 1), ("raw_ready", 1), ("pv_done", PROBS), ("ot_ready", AHEAD), ("sums_ready", AHEAD),
                             ("wo_done", AHEAD)):
                dve.sem_inc(s[n], ahead)
            dve.memset(mx[:], 0.0).then_inc(s["mx_half_ready"], 1)
            dve.wait_ge(s["mx_half_ready"], 1)
            dve.wait_ge(s["cst_loaded"], n_cst)
            def low_head(kind, i, at):
                j = "qkc".index(kind)
                lo, n = (S, SC) if kind == "c" else (0, S)
                full, low = (Q, Qb) if kind == "q" else (K, Kb)
                if rms is None:
                    dve.wait_ge(s["full_ready"], at * 3 + j + 1)
                for e in range(2):
                    ins = nc.vector.tensor_copy(low[i][e][0:64, lo:lo + n], full[i][e][0:64, lo:lo + n])
                ins.then_inc(s[("q_ready", "k_ready", "kc_ready")[j]], 1)

            def normed_head(kind, i, at):
                j = "qkc".index(kind)
                lo, n = (S, SC) if kind == "c" else (0, S)
                root = roots[j]
                full = Q if kind == "q" else K
                step = Tally(dve, s["norm_step"], 12, at)
                step.n = 4 * j
                dve.wait_ge(s["root_ready"], at * 3 + j + 1)
                step.add(nc.vector.tensor_scalar(root[:], root[:], 0.125 if j else 1.0, 1e-8 if j else 8e-8, ALU.mult, ALU.max))
                step.wait()
                step.add(nc.vector.reciprocal(root[:], root[:]))
                step.wait()
                for e in range(2):
                    r = slice(64 * e, 64 * e + 64)
                    step.add(nc.vector.scalar_tensor_tensor(full[i][e][0:64, lo:lo + n], raws[j][r, :], gam[r, min(j, 1):min(j, 1) + 1],
                                                            root[r, :], ALU.mult, ALU.mult))
                step.wait()
                low_head(kind, i, at)

            def max_step(k, at):
                e, j = divmod(k, STEPS // 2)
                dve.wait_ge(s["max_psum"], at * STEPS + k + 1)
                if j < 2 * NT:
                    col = e * NT + j // 2
                    ins = nc.vector.tensor_reduce(mx_half[:, j % 2, col:col + 1], for_max[:, k % 2, :], AX.X, ALU.max)
                else:
                    col = e * NT + (j - 2 * NT) * 4
                    ins = nc.vector.tensor_reduce(mx_c[:, col:col + 4], for_max[:, k % 2, :].rearrange("p (t n) -> p t n", t=4)[:, :, 0:SC],
                                                  AX.X, ALU.max)
                ins.then_inc(s["max_done"], 1)

            def turn(at):
                dve.wait_ge(s["max_done"], at * STEPS + STEPS)
                nc.vector.tensor_tensor(mx_c[:], mx_c[:], mx_half[:, 0, :], ALU.max).then_inc(s["mx_half_ready"], 1)
                dve.wait_ge(s["mx_half_ready"], at + 2)
                nc.vector.tensor_tensor(mx[:, 0:2 * NT], mx_c[:], mx_half[:, 1, :], ALU.max).then_inc(s["mx_ready"], 1)
                dve.wait_ge(s["mxt_ready"], at + 1)
                nc.vector.tensor_scalar(neg[:], for_max[0:2 * NT, 0, 0:P], -1.0, None, ALU.mult).then_inc(s["neg_ready"], 1)

            def run(plan, at, i, r):
                for event, n, m in plan:
                    if event == "proj" and rms is not None and n in ("qs", "ks", "cs"):
                        normed_head(n[0], 1 - i, at + 1)
                    elif event == "proj" and rms is None and n in ("q", "k", "c"):
                        low_head(n, 1 - i, at + 1)
                    elif event == "max":
                        max_step(n, at + 1)
                    elif event == "turn":
                        turn(at + 1)
                    elif event == "values" and n % KT == KT - 1:
                        h = n // KT
                        g = at * 2 + h
                        dve.wait_ge(s["pv_done"], at * ITEMS + n + 1 + PROBS)
                        dve.wait_ge(s["ot_ready"], g + 1)
                        nc.vector.tensor_copy(raw[h][:], pv[:]).then_inc(s["raw_ready"], 1)
                    elif event == "sums":
                        h = n % 2
                        g = at * 2 + n
                        dve.wait_ge(s["sums_ready"], g + 1 + AHEAD)
                        dve.wait_ge(s["ot_ready"], g + AHEAD)
                        nc.vector.reciprocal(rsum[:], rs[:]).then_inc(s["rsum_ready"], 1)
                        dve.wait_ge(s["rsum_ready"], g + 1)
                        dve.wait_ge(s["raw_ready"], g + 2)
                        dve.wait_ge(s["wo_done"], g + 1)
                        nc.vector.tensor_tensor(OT[h][:], raw[h][:], rsum[:], ALU.mult).then_inc(s["ot_ready"], 1)
                    elif event == "wo":
                        a = acc[:, bass.ds((at if n >= 0 else at - 1) // PAIRS * NT + n % 2 * HT, HT), :].rearrange("p t d -> p (t d)")
                        dve.wait_ge(s["wo_done"], at * 2 + n + 1 + AHEAD)
                        nc.vector.tensor_tensor(a, a, s2[m % 2], ALU.add).then_inc(free[m % 2], 1)

            step = Tally(dve, s["dve_step"])
            dve.wait_ge(s["mask_loaded"], 16)
            for row in (mrow, mrow_b):
                nc.vector.tensor_scalar(row[:], mask_in[:], -1.0, 1.0, ALU.mult, ALU.add).then_inc(s["mrow_ready"], 1)
            step.add(nc.vector.memset(acc[:], 0.0))
            dve.wait_ge(s["c_loaded"], 16)
            for b in range(B):
                step.add(nc.vector.bn_stats(stats[0:SC, b, :], cx[:, b, :]))
            step.wait()
            for b in range(B):
                ins = nc.vector.bn_aggr(mv[0:SC, b, :], stats[0:SC, b, :])
            ins.then_inc(s["var_ready"], 1)
            dve.wait_ge(s["std_ready"], 1)
            step.add(nc.vector.reciprocal(rstd[0:SC, 0:B], std[0:SC, 0:B]))
            step.wait()
            for b in range(B):
                ins = nc.vector.tensor_scalar(cx[:, b, :], cx[:, b, :], mv[0:SC, b, 0:1], rstd[0:SC, b:b + 1], ALU.subtract, ALU.mult)
            ins.then_inc(s["xn_ready"], 1)
            for kind in "qkc":
                (low_head if rms is None else normed_head)(kind, 0, 0)
            for k in range(STEPS):
                max_step(k, 0)
            turn(0)
            phases(dve, run)
            gate_col = c.gates[:, gate:gate + 1]
            for i in range(2):
                pause(dve, free[i], (USES + 1 - i) // 2 + 1, s["dve_passed"])
            tail = Tally(dve, s["dve_tail"])
            for n in range(NC):
                ts = range(n * CT, (n + 1) * CT)
                if out_ln is not None:
                    for t in ts:
                        tail.add(nc.vector.bn_stats(stats[:, t % CT, :], acc[:, t, :]))
                    tail.wait()
                    for t in range(CT):
                        ins = nc.vector.bn_aggr(mv[:, t, :], stats[:, t, :])
                    ins.then_inc(s["tail_var"], 1)
                    dve.wait_ge(s["tail_std"], n + 1)
                    tail.add(nc.vector.reciprocal(rstd[:], std[:]))
                    tail.wait()
                    for t in ts:
                        tail.add(nc.vector.tensor_scalar(acc[:, t, :], acc[:, t, :], mv[:, t % CT, 0:1], rstd[:, t % CT:t % CT + 1],
                                                         ALU.subtract, ALU.mult))
                    tail.wait()
                    for t in ts:
                        tail.add(nc.vector.tensor_tensor(acc[:, t, :], acc[:, t, :], og[:], ALU.mult))
                    tail.wait()
                for t in ts:
                    tail.add(nc.vector.tensor_tensor(acc[:, t, :], acc[:, t, :], ob[:], ALU.add))
                tail.wait()
                cols = slice(n * CT, (n + 1) * CT)
                nc.vector.scalar_tensor_tensor(x[:, cols, :], acc[:, cols, :], gate_col, x[:, cols, :], ALU.mult, ALU.add).then_inc(s["out_ready"], 1)


def normed(nc, ctx, c, name, x_in, mode="plain", ln=None, outs=(), token=None, keep_xn=False):
    keep = Kept()

    def sb(n, shape, dt=F32):
        return ctx.enter_context(nc.sbuf_tensor(f"{name}_{n}", shape, dt))

    keep.x = x = sb("x", [P, TT, D])
    with ExitStack() as inner:
        def tmp(n, shape, dt=F32):
            return inner.enter_context(nc.sbuf_tensor(f"{name}_{n}", shape, dt))

        def sem(n):
            return c.semaphore(f"{name}_{n}")

        if mode == "rms":
            keep.route = sb("route", [P, TT])
        if mode == "quant":
            keep.step_size = sb("step_size", [P, TT])
        xn = keep.xn = (sb if keep_xn else tmp)("xn", [P, TT, D])
        work = tmp("work", [P, CT, D])
        stats, mv = tmp("stats", [P, TT, 6]), tmp("mv", [P, TT, 2])
        std, rstd = tmp("std", [P, TT]), tmp("rstd", [P, TT])
        size, scale = tmp("size", [P, TT]), tmp("scale", [P, TT])
        if token is not None:
            tok = tmp("tok", [P, D])
        if ln is not None:
            lnw = tmp("lnw", list(ln.shape))
        turned = inner.enter_context(nc.psum_tensor(f"{name}_turned", [P, NC, KD, 512], F32))
        s = {n: sem(n) for n in ("cst_loaded var_ready std_ready sq_ready len_ready xn_ready turned_ready "
                                 "step evacuated").split()}
        x_loaded = [sem(f"x_loaded{n}") for n in range(NC)]
        n_cst = (token is not None) + (ln is not None)
        block = inner.enter_context(nc.Block())

        @block.sync
        def _(sp):
            for n in range(NC):
                sp.dma_start(x[:, n * CT:(n + 1) * CT, :], tiles_of(x_in, n * CH, CT)).then_inc(x_loaded[n], 16)
                if n == 0:
                    if token is not None:
                        sp.dma_start(tok[:], row_tile(token, P)).then_inc(s["cst_loaded"], 16)
                    if ln is not None:
                        sp.dma_start(lnw[:], ln).then_inc(s["cst_loaded"], 16)

        @block.vector
        def _(dve):
            step = Tally(dve, s["step"])
            for n in range(NC):
                ts = range(n * CT, (n + 1) * CT)
                cols = slice(n * CT, (n + 1) * CT)
                dve.wait_ge(x_loaded[n], 16)
                for t in ts:
                    step.add(nc.vector.bn_stats(stats[:, t, :], x[:, t, :]))
                step.wait()
                for t in ts:
                    ins = nc.vector.bn_aggr(mv[:, t, :], stats[:, t, :])
                ins.then_inc(s["var_ready"], 1)
                dve.wait_ge(s["std_ready"], n + 1)
                step.add(nc.vector.reciprocal(rstd[:, cols], std[:, cols]))
                step.wait()
                for t in ts:
                    ins = nc.vector.tensor_scalar(xn[:, t, :], x[:, t, :], mv[:, t, 0:1], rstd[:, t:t + 1],
                                                  ALU.subtract, ALU.mult)
                    if t < ts[-1] or mode != "plain":
                        step.add(ins)
                if mode == "plain":
                    ins.then_inc(s["xn_ready"], 1)
                    continue
                step.wait()
                if mode == "twice":
                    for t in ts:
                        step.add(nc.vector.bn_stats(stats[:, t, :], xn[:, t, :]))
                    step.wait()
                    for t in ts:
                        ins = nc.vector.bn_aggr(mv[:, t, :], stats[:, t, :])
                    ins.then_inc(s["sq_ready"], 1)
                    dve.wait_ge(s["len_ready"], n + 1)
                    step.add(nc.vector.reciprocal(rstd[:, cols], scale[:, cols]))
                    step.wait()
                    for t in ts:
                        ins = nc.vector.tensor_scalar(xn[:, t, :], xn[:, t, :], mv[:, t, 0:1], rstd[:, t:t + 1], ALU.subtract, ALU.mult)
                    ins.then_inc(s["xn_ready"], 1)
                    continue
                if mode == "rms":
                    if n == 0:
                        dve.wait_ge(s["cst_loaded"], 16 * n_cst)
                    for t in ts:
                        step.add(nc.vector.tensor_tensor_reduce(work[:, t % CT, :], xn[:, t, :], tok[:], 1.0, 0.0,
                                                                ALU.mult, ALU.add, keep.route[:, t:t + 1]))
                    step.wait()
                    for t in ts:
                        ins = nc.vector.tensor_tensor_reduce(work[:, t % CT, :], xn[:, t, :], xn[:, t, :], 1.0, 0.0,
                                                             ALU.mult, ALU.add, size[:, t:t + 1])
                    ins.then_inc(s["sq_ready"], 1)
                    dve.wait_ge(s["len_ready"], n + 1)
                    step.add(nc.vector.tensor_scalar(scale[:, cols], scale[:, cols], 1e-12, None, ALU.max))
                    step.wait()
                    step.add(nc.vector.reciprocal(scale[:, cols], scale[:, cols]))
                    step.wait()
                    for t in ts:
                        ins = nc.vector.tensor_scalar(xn[:, t, :], xn[:, t, :], scale[:, t:t + 1], float(D) ** 0.5,
                                                      ALU.mult, ALU.mult)
                    ins.then_inc(s["xn_ready"], 1)
                else:
                    step.add(nc.vector.tensor_reduce(size[:, cols], xn[:, cols, :], AX.X, ALU.max, apply_absolute_value=True))
                    step.wait()
                    step.add(nc.vector.tensor_scalar(size[:, cols], size[:, cols], 1e-5, None, ALU.max))
                    step.wait()
                    step.add(nc.vector.tensor_scalar(keep.step_size[:, cols], size[:, cols], 1.0 / 127.0, None, ALU.mult))
                    step.add(nc.vector.reciprocal(scale[:, cols], size[:, cols]))
                    step.wait()
                    step.add(nc.vector.tensor_scalar(scale[:, cols], scale[:, cols], 127.0, None, ALU.mult))
                    step.wait()
                    for t in ts:
                        step.add(nc.vector.tensor_scalar(xn[:, t, :], xn[:, t, :], scale[:, t:t + 1], ROUND, ALU.mult, ALU.add))
                    step.wait()
                    step.add(nc.vector.tensor_scalar(xn[:, cols, :], xn[:, cols, :], -ROUND, -128.0, ALU.add, ALU.max))
                    step.wait()
                    nc.vector.tensor_scalar(xn[:, cols, :], xn[:, cols, :], 127.0, None, ALU.min).then_inc(s["xn_ready"], 1)

        @block.tensor
        def _(pe):
            for n in range(NC):
                pe.wait_ge(s["xn_ready"], n + 1)
                for k in range(KD):
                    for t in range(CT):
                        last = nc.tensor.transpose(turned[:, n, k, t * P:(t + 1) * P], xn[:, n * CT + t, k * P:(k + 1) * P], c.ident[:])
                last.then_inc(s["turned_ready"], 1)

        @block.scalar
        def _(act):
            if n_cst:
                act.wait_ge(s["cst_loaded"], 16 * n_cst)

            def root(n):
                cols = slice(n * CT, (n + 1) * CT)
                act.wait_ge(s["var_ready"], n + 1)
                nc.scalar.activation(std[:, cols], mv[:, cols, 1], ACT.Sqrt, bias=c.eps[:, 0:1]).then_inc(s["std_ready"], 1)
                if mode == "twice":
                    act.wait_ge(s["sq_ready"], n + 1)
                    nc.scalar.activation(scale[:, cols], mv[:, cols, 1], ACT.Sqrt, bias=c.eps[:, 0:1]).then_inc(s["len_ready"], 1)
                if mode == "rms":
                    act.wait_ge(s["sq_ready"], n + 1)
                    nc.scalar.activation(scale[:, cols], size[:, cols], ACT.Sqrt).then_inc(s["len_ready"], 1)

            root(0)
            for n in range(NC):
                if n + 1 < NC:
                    root(n + 1)
                act.wait_ge(s["turned_ready"], n + 1)
                for i, (dst, off) in enumerate(outs):
                    for k in range(KD):
                        d = dst[:, k, n * CH:(n + 1) * CH]
                        if ln is None:
                            nc.scalar.activation(d, turned[:, n, k, :], ACT.Copy)
                        elif off:
                            nc.scalar.activation(d, turned[:, n, k, :], ACT.Identity, scale=lnw[:, k, 0:1], bias=lnw[:, k, 1:2])
                        else:
                            nc.scalar.activation(d, turned[:, n, k, :], ACT.Copy, scale=lnw[:, k, i:i + 1])
    return keep


def route_tokens(nc, ctx, c, name, route, scratch):
    n_iter, k_eff = 50, min(256 * 9.0 / 8.0, S)
    log_k = float(np.log(np.float32(k_eff)))
    def keep(n, shape, dt=F32):
        return ctx.enter_context(nc.sbuf_tensor(f"{name}_{n}", shape, dt))

    t_col, t_all = keep("t_col", [P, P]), keep("t_all", [P, TOK])
    e_col, before = keep("e_col", [P, TT]), keep("before", [P, 2 * S])
    with ExitStack() as inner:
        def tmp(n, shape, dt=F32):
            return inner.enter_context(nc.sbuf_tensor(f"{name}_{n}", shape, dt))

        def sem(n):
            return c.semaphore(f"{name}_{n}")

        r3 = route[:].rearrange("p (b t) -> p b t", b=B)
        best, best_all = tmp("best", [P, B]), tmp("best_all", [P, B])
        na, top = tmp("na", [P, B]), tmp("top", [P, B])
        part, total_ln = tmp("part", [P, B]), tmp("total_ln", [P, B])
        sbm, ex = tmp("sbm", [P, B, NT]), tmp("ex", [P, B, NT])
        t_row = tmp("t_row", [TT, P])
        ps = inner.enter_context(nc.psum_tensor(f"{name}_ps", [P, 512], F32))
        pt = inner.enter_context(nc.psum_tensor(f"{name}_pt", [P, 512], F32))
        s = {n: sem(n) for n in ("best_ready best_done ex_ready sbm_ready part_ready sum_ready ln_ready na_ready tcol_ready trow_ps "
                                 "trow_ready stored t_loaded e_ready before_ready step loop_step tail_step").split()}
        block = inner.enter_context(nc.Block())

        def wide(v):
            return v[:].unsqueeze(2).broadcast_to([P, B, NT])

        @block.gpsimd
        def _(pool):
            pool.wait_ge(s["best_ready"], 1)
            pool.partition_all_reduce(best_all[:], best[:], P, bass.bass_isa.ReduceOp.max).then_inc(s["best_done"], 1)
            pool.wait_ge(s["best_done"], 1)
            pool.memset(before[:], 1.0).then_inc(s["before_ready"], 1)
            pool.wait_ge(s["before_ready"], 1)
            pool.affine_select(out=before[:], in_=before[:], compare_op=ALU.is_gt, fill=0.0, base=S, pattern=[[-1, 2 * S]],
                               channel_multiplier=1).then_inc(s["before_ready"], 1)

        @block.tensor
        def _(pe):
            with pe.Fori(0, n_iter - 1) as i:
                pe.wait_ge(s["part_ready"], i + 1)
                nc.tensor.matmul(ps[:, 0:B], c.ones[:], part[:], start=True, stop=True).then_inc(s["sum_ready"], 1)
            pe.wait_ge(s["tcol_ready"], 1)
            nc.tensor.transpose(pt[:, 0:P], t_col[:], c.ident[:]).then_inc(s["trow_ps"], 1)

        @block.scalar
        def _(act):
            nc.scalar.preload_act_table_set("natural_log_exp_and_others")
            with act.Fori(0, n_iter - 1) as i:
                act.wait_ge(s["sbm_ready"], i + 1)
                nc.scalar.activation(ex[:], sbm[:], ACT.Exp).then_inc(s["ex_ready"], 1)
                act.wait_ge(s["sum_ready"], i + 1)
                nc.scalar.activation(total_ln[:], ps[:, 0:B], ACT.Ln).then_inc(s["ln_ready"], 1)
            act.wait_ge(s["tcol_ready"], 1)
            nc.scalar.activation(e_col[:], t_col[:, 0:TT], ACT.Exp).then_inc(s["e_ready"], 1)

        @block.sync
        def _(sp):
            sp.wait_ge(s["trow_ready"], 1)
            sp.dma_start(scratch, t_row[:]).then_inc(s["stored"], 16)
            sp.wait_ge(s["stored"], 16)
            sp.dma_start(t_all[:], row_tile(scratch.rearrange("t p -> (t p)"), P)).then_inc(s["t_loaded"], 16)
            sp.wait_ge(s["t_loaded"], 16)

        @block.vector
        def _(dve):
            step = Tally(dve, s["step"])
            step.add(nc.vector.memset(t_col[:], 0.0))
            step.add(nc.vector.memset(na[:], float(np.log(np.float32(S))) - log_k))
            nc.vector.tensor_reduce(best[:], r3, AX.X, ALU.max).then_inc(s["best_ready"], 1)
            dve.wait_ge(s["best_done"], 1)
            step.wait()
            dve.sem_inc(s["na_ready"], 1)
            with dve.Fori(0, n_iter - 1) as i:
                dve.wait_ge(s["na_ready"], i + 1)
                nc.vector.tensor_tensor(sbm[:], r3, wide(na), ALU.min).then_inc(s["loop_step"], 1)
                nc.vector.tensor_tensor(top[:], best_all[:], na[:], ALU.min).then_inc(s["loop_step"], 1)
                dve.wait_ge(s["loop_step"], i * 2 + 2)
                nc.vector.tensor_tensor(sbm[:], sbm[:], wide(top), ALU.subtract).then_inc(s["sbm_ready"], 1)
                dve.wait_ge(s["ex_ready"], i + 1)
                nc.vector.tensor_reduce(part[:], ex[:], AX.X, ALU.add).then_inc(s["part_ready"], 1)
                dve.wait_ge(s["ln_ready"], i + 1)
                nc.vector.scalar_tensor_tensor(na[:], top[:], -log_k, total_ln[:], ALU.add, ALU.add).then_inc(s["na_ready"], 1)
            tail = Tally(dve, s["tail_step"])
            dve.wait_ge(s["na_ready"], n_iter)
            t3 = t_col[:, 0:TT].rearrange("p (b t) -> p b t", b=B)
            tail.add(nc.vector.tensor_tensor(t3, r3, wide(na), ALU.subtract))
            tail.wait()
            nc.vector.tensor_scalar(t_col[:, 0:TT], t_col[:, 0:TT], 0.0, None, ALU.min).then_inc(s["tcol_ready"], 1)
            dve.wait_ge(s["trow_ps"], 1)
            nc.vector.tensor_copy(t_row[:], pt[0:TT, 0:P]).then_inc(s["trow_ready"], 1)
    return t_col, t_all, e_col, before


def rank_tokens(nc, step, scores, buf, weight):
    heavy = 256
    t_col, t_all, e_col, before = scores
    step.add(nc.vector.tensor_scalar(buf.score[:], e_col[:], -1.0, 1.0, ALU.mult, ALU.add))
    step.wait()
    step.add(nc.vector.tensor_tensor(buf.score[:], buf.score[:], e_col[:], ALU.add))
    for t in range(TT):
        b, own = divmod(t, NT)
        row = t_all[:, b * S:(b + 1) * S]
        if t:
            step.wait()
        step.add(nc.vector.scalar_tensor_tensor(buf.junk[:, 0, :], row, t_col[:, t:t + 1], before[:, 0:S],
                                                ALU.is_gt, ALU.mult, accum_out=buf.above[:, t:t + 1]))
        step.add(nc.vector.scalar_tensor_tensor(buf.junk[:, 1, :], row, t_col[:, t:t + 1], before[:, S - P * own:2 * S - P * own],
                                                ALU.is_equal, ALU.mult, accum_out=buf.equal[:, t:t + 1]))
    step.wait()
    step.add(nc.vector.tensor_tensor(buf.above[:], buf.above[:], buf.equal[:], ALU.add))
    step.wait()
    step.add(nc.vector.scalar_tensor_tensor(weight[:], buf.above[:], heavy - 0.5, buf.score[:], ALU.is_lt, ALU.mult))
    step.wait()


def ffn0(nc, c, name, x_in, x_out, gate, io):
    DH = io["l0_w1h"].shape[1]
    MH = DH // P
    with ExitStack() as ctx:
        def sb(n, shape, dt=F32):
            return ctx.enter_context(nc.sbuf_tensor(f"{name}_{n}", shape, dt))

        light_in, heavy_in = sb("light_in", [P, KD, TOK]), sb("heavy_in", [P, KD, TOK])
        weight = sb("weight", [P, TT])
        keep = normed(nc, ctx, c, f"{name}n", x_in, "rms", io["l0_gammas"], ((light_in, 0), (heavy_in, 0)), io["l0_token"])
        x = keep.x
        scores = route_tokens(nc, ctx, c, f"{name}r", keep.route, io["scratch"])
        buf = Kept()
        buf.score, buf.above, buf.equal, buf.junk = sb("score", [P, TT]), sb("above", [P, TT]), sb("equal", [P, TT]), sb("junk", [P, 2, S])

        w1l, w2l = sb("w1l", [P, KD, P]), sb("w2l", [P, D])
        w1h, w2h = sb("w1h", [P, KD, DH]), sb("w2h", [P, MH, D])
        b1 = sb("b1", [P, 1 + MH])
        b2l, b2h = sb("b2l", [P, D]), sb("b2h", [P, D])
        hl, hh = sb("hl", [P, CH]), sb("hh", [P, MH, CH])
        yl, yh = sb("yl", [P, CT, D]), sb("yh", [P, CT, D])
        hid = ctx.enter_context(nc.psum_tensor(f"{name}_hid", [P, 3, 512], F32))
        out_l = ctx.enter_context(nc.psum_tensor(f"{name}_out_l", [P, CT, D], F32))
        out_h = ctx.enter_context(nc.psum_tensor(f"{name}_out_h", [P, CT, D], F32))
        s = {n: c.semaphore(f"{name}_{n}") for n in
             "w_loaded hid_ready act_done light_done heavy_done out_free step rank_step x_ready stored dve_passed".split()}
        H = 1 + MH
        block = ctx.enter_context(nc.Block())

        @block.sync
        def _(sp):
            for dst, src in ((w1l, io["l0_w1l"].rearrange("(k p) m -> p k m", p=P)), (b1, io["l0_b1"]),
                             (w1h, io["l0_w1h"].rearrange("(k p) m -> p k m", p=P)), (w2l, io["l0_w2l"]),
                             (w2h, io["l0_w2h"].rearrange("(k p) m -> p k m", p=P)),
                             (b2l, row_tile(io["l0_b2l"], P)), (b2h, row_tile(io["l0_b2h"], P))):
                sp.dma_start(dst[:], src).then_inc(s["w_loaded"], 16)
            with sp.Fori(0, NC) as n:
                tile, tok = sp.snap(n * CT), sp.snap(n * CH)
                sp.wait_ge(s["x_ready"], n + 1)
                sp.dma_start(tiles_of(x_out, tok, CT), x[:, bass.ds(tile, CT), :]).then_inc(s["stored"], 16)
            sp.wait_ge(s["stored"], 16 * NC)

        @block.tensor
        def _(pe):
            pe.wait_ge(s["w_loaded"], 16 * 7)
            with pe.Fori(0, NC) as n:
                for i in range(H):
                    if i >= 3:
                        pe.wait_ge(s["act_done"], n * H + i - 2)
                    src = light_in if i == 0 else heavy_in
                    for k in range(KD):
                        w = w1l[:, k, :] if i == 0 else w1h[:, k, (i - 1) * P:i * P]
                        last = nc.tensor.matmul(hid[:, i % 3, :], w, src[:, k, bass.ds(n * CH, CH)], start=k == 0, stop=k == KD - 1)
                    last.then_inc(s["hid_ready"], 1)
                pe.wait_ge(s["out_free"], n + 1)
                pe.wait_ge(s["act_done"], n * H + 1)
                for t in range(CT):
                    last = nc.tensor.matmul(out_l[:, t, :], hl[:, t * P:(t + 1) * P], w2l[:], start=True, stop=True)
                last.then_inc(s["light_done"], 1)
                for t in range(CT):
                    for k in range(MH):
                        if t == 0:
                            pe.wait_ge(s["act_done"], n * H + k + 2)
                        last = nc.tensor.matmul(out_h[:, t, :], hh[:, k, t * P:(t + 1) * P], w2h[:, k, :], start=k == 0, stop=k == MH - 1)
                last.then_inc(s["heavy_done"], 1)

        @block.scalar
        def _(act):
            act.wait_ge(s["w_loaded"], 16 * 7)
            with act.Fori(0, NC) as n:
                for i in range(H):
                    act.wait_ge(s["hid_ready"], n * H + i + 1)
                    dst = hl[:] if i == 0 else hh[:, i - 1, :]
                    nc.scalar.activation(dst, hid[:, i % 3, :], ACT.Gelu, bias=b1[:, i:i + 1]).then_inc(s["act_done"], 1)

        @block.vector
        def _(dve):
            rank_tokens(nc, Tally(dve, s["rank_step"]), scores, buf, weight)
            dve.wait_ge(s["w_loaded"], 16 * 7)
            dve.sem_inc(s["out_free"], 1)
            with dve.Fori(0, NC) as n:
                tile = dve.snap(n * CT)
                step = Tally(dve, s["step"], 1 + CT, n)
                dve.wait_ge(s["light_done"], n + 1)
                step.add(nc.vector.tensor_tensor(yl[:], out_l[:], b2l[:].unsqueeze(1).broadcast_to([P, CT, D]), ALU.add))
                dve.wait_ge(s["heavy_done"], n + 1)
                nc.vector.tensor_tensor(yh[:], out_h[:], b2h[:].unsqueeze(1).broadcast_to([P, CT, D]), ALU.add).then_inc(s["out_free"], 1)
                dve.wait_ge(s["out_free"], n + 2)
                step.wait()
                for t in range(CT):
                    step.add(nc.vector.scalar_tensor_tensor(yl[:, t, :], yh[:, t, :], weight[:, bass.ds(tile + t, 1)], yl[:, t, :],
                                                            ALU.mult, ALU.add))
                step.wait()
                step.close()
                xs = x[:, bass.ds(tile, CT), :]
                nc.vector.scalar_tensor_tensor(xs, yl[:], c.gates[:, gate:gate + 1], xs, ALU.mult, ALU.add).then_inc(s["x_ready"], 1)
                pause(dve, s["x_ready"], n + 1, s["dve_passed"])


def ffn1(nc, c, name, x_in, x_out, gate, io):
    DH = io["l1_w1"].shape[1]
    MH = DH // P
    with ExitStack() as ctx:
        def sb(n, shape, dt=F32):
            return ctx.enter_context(nc.sbuf_tensor(f"{name}_{n}", shape, dt))

        xq = sb("xq", [P, KD, TOK], BF16)
        keep = normed(nc, ctx, c, f"{name}n", x_in, "quant", None, ((xq, 0),))
        x, step_size = keep.x, keep.step_size

        w1, w2 = sb("w1", [P, KD, DH]), sb("w2", [P, MH, D])
        w1t, w2t = sb("w1t", [P, KD, DH], BF16), sb("w2t", [P, MH, D], BF16)
        part, mean, scale = sb("part", [P, 2]), sb("mean", [P, 2]), sb("scale", [P, 2])
        conv = sb("conv", [P, MH, 4])
        diag = sb("diag", [P, P * TT])
        row = sb("row", [P, B, S])
        h = sb("h", [P, S + 2])
        y = sb("y", [P, S])
        act_out = sb("act_out", [P, MH, S])
        big = sb("big", [P, S])
        mag = sb("mag", [P, 2, S])
        size, back, inv = sb("size", [P, NT]), sb("back", [P, NT]), sb("inv", [P, NT])
        diag2 = sb("diag2", [P, P * NT])
        hq = sb("hq", [P, MH, S], BF16)
        ps = [ctx.enter_context(nc.psum_tensor(f"{name}_ps{i}", [P, 2, 512], F32)) for i in range(2)]
        out_ps = ctx.enter_context(nc.psum_tensor(f"{name}_out_ps", [P, NT, D], F32))
        psf = [p[:].rearrange("p a n -> p (a n)") for p in ps]
        outf = out_ps[:].rearrange("p t d -> p (t d)")
        s = {n: c.semaphore(f"{name}_{n}") for n in
             "w1_loaded w2_loaded conv_loaded part_ready total_ready tern_ready diag_ready row_ps row_ready hid_ready h_ready conv_ready silu_done mag_ready big_done "
             "big_ready big_turned diag2_ready row2_ps hq_ready out_ready x_ready stored step body_step sp_passed dve_passed".split()}
        block = ctx.enter_context(nc.Block())

        @block.sync
        def _(sp):
            sp.dma_start(w1[:], io["l1_w1"].rearrange("(k p) m -> p k m", p=P)).then_inc(s["w1_loaded"], 16)
            sp.dma_start(w2[:], io["l1_w2"].rearrange("(k p) m -> p k m", p=P)).then_inc(s["w2_loaded"], 16)
            sp.dma_start(conv[:], io["l1_conv"]).then_inc(s["conv_loaded"], 16)
            with sp.Fori(0, B) as b:
                tile, tok = sp.snap(b * NT), sp.snap(b * S)
                sp.wait_ge(s["x_ready"], b + 1)
                sp.dma_start(tiles_of(x_out, tok, NT), x[:, bass.ds(tile, NT), :]).then_inc(s["stored"], 16)
            sp.wait_ge(s["stored"], 16 * B)

        @block.tensor
        def _(pe):
            pe.wait_ge(s["part_ready"], 2)
            nc.tensor.matmul(ps[0][:, 0, 0:2], c.ones[:], part[:], start=True, stop=True).then_inc(s["total_ready"], 1)
            pe.wait_ge(s["diag_ready"], TT)
            for b in range(B):
                for t in range(NT):
                    n = b * NT + t
                    last = nc.tensor.matmul(outf[:, n * P:(n + 1) * P], c.ones[:], diag[:, n * P:(n + 1) * P], start=True, stop=True)
            last.then_inc(s["row_ps"], 1)
            pe.wait_ge(s["tern_ready"], 2)
            pe.wait_ge(s["row_ready"], 1)
            with pe.Fori(0, B) as b:
                for m in range(MH):
                    if m >= 2:
                        pe.wait_ge(s["h_ready"], b * MH + m - 1)
                    for j in range(2):
                        for k in range(KD):
                            last = nc.tensor.matmul(ps[m % 2][:, j, :], w1t[:, k, m * P:(m + 1) * P],
                                                    xq[:, k, bass.ds(b * S + j * CH, CH)], start=k == 0, stop=k == KD - 1)
                    last.then_inc(s["hid_ready"], 1)
                pe.wait_ge(s["big_ready"], b + 1)
                for t in range(NT):
                    last = nc.tensor.transpose(psf[0][:, t * P:(t + 1) * P], big[:, t * P:(t + 1) * P], c.ident[:])
                last.then_inc(s["big_turned"], 1)
                pe.wait_ge(s["diag2_ready"], b + 1)
                for t in range(NT):
                    last = nc.tensor.matmul(psf[1][:, t * P:(t + 1) * P], c.ones[:], diag2[:, t * P:(t + 1) * P], start=True, stop=True)
                last.then_inc(s["row2_ps"], 1)
                for t in range(NT):
                    for k in range(MH):
                        if t == 0:
                            pe.wait_ge(s["hq_ready"], b * MH + k + 1)
                        last = nc.tensor.matmul(out_ps[:, t, :], hq[:, k, t * P:(t + 1) * P], w2t[:, k, :], start=k == 0, stop=k == MH - 1)
                last.then_inc(s["out_ready"], 1)

        @block.scalar
        def _(act):
            act.wait_ge(s["row_ps"], 1)
            act.wait_ge(s["tern_ready"], 2)
            nc.scalar.activation(row[:].rearrange("p b n -> p (b n)"), outf, ACT.Copy, scale=mean[:, 0:1]).then_inc(s["row_ready"], 1)
            with act.Fori(0, B) as b:
                for m in range(MH):
                    act.wait_ge(s["conv_ready"], b * MH + m + 1)
                    nc.scalar.activation(act_out[:, m, :], y[:], ACT.Silu).then_inc(s["silu_done"], 1)
                    act.wait_ge(s["silu_done"], b * MH + m + 1)
                    if m >= 2:
                        act.wait_ge(s["big_done"], b * MH + m - 1)
                    nc.scalar.activation(mag[:, m % 2, :], act_out[:, m, :], ACT.Abs).then_inc(s["mag_ready"], 1)

        @block.vector
        def _(dve):
            step = Tally(dve, s["step"])
            step.add(nc.vector.memset(h[:], 0.0))
            for t in range(TT):
                nc.vector.tensor_scalar(diag[:, t * P:(t + 1) * P], c.ident[:], step_size[:, t:t + 1], None, ALU.mult).then_inc(s["diag_ready"], 1)
            for i, (w, loaded) in enumerate(((w1, "w1_loaded"), (w2, "w2_loaded"))):
                dve.wait_ge(s[loaded], 16)
                nc.vector.tensor_reduce(part[:, i:i + 1], w[:], AX.XY, ALU.add, apply_absolute_value=True).then_inc(s["part_ready"], 1)
            dve.wait_ge(s["total_ready"], 1)
            step.add(nc.vector.tensor_scalar(mean[:], ps[0][:, 0, 0:2], 1.0 / (D * DH), 1e-5, ALU.mult, ALU.max))
            step.wait()
            step.add(nc.vector.reciprocal(scale[:], mean[:]))
            step.wait()
            for i, w in enumerate((w1, w2)):
                step.add(nc.vector.tensor_scalar(w[:], w[:], scale[:, i:i + 1], ROUND, ALU.mult, ALU.add))
            step.wait()
            for w in (w1, w2):
                step.add(nc.vector.tensor_scalar(w[:], w[:], -ROUND, -1.0, ALU.add, ALU.max))
            step.wait()
            for w, wt in ((w1, w1t), (w2, w2t)):
                nc.vector.tensor_scalar(wt[:], w[:], 1.0, None, ALU.min).then_inc(s["tern_ready"], 1)
            dve.wait_ge(s["conv_loaded"], 16)
            dve.wait_ge(s["row_ready"], 1)
            with dve.Fori(0, B) as b:
                body = Tally(dve, s["body_step"], 1 + 2 * MH + 4 + NT - 1 + 2 + 2 * MH + NT - 1, b)
                body.add(nc.vector.memset(big[:], 0.0))
                body.wait()

                def largest(m):
                    dve.wait_ge(s["mag_ready"], b * MH + m + 1)
                    if m >= 1:
                        dve.wait_ge(s["big_done"], b * MH + m)
                    nc.vector.tensor_tensor(big[:], mag[:, m % 2, :], big[:], ALU.max).then_inc(s["big_done"], 1)

                for m in range(MH):
                    dve.wait_ge(s["hid_ready"], b * MH + m + 1)
                    if m >= 1:
                        dve.wait_ge(s["conv_ready"], b * MH + m)
                    rowb = row[:, bass.ds(b, 1), :].rearrange("p o n -> p (o n)")
                    nc.vector.tensor_tensor(h[:, 1:S + 1], psf[m % 2], rowb, ALU.mult).then_inc(s["h_ready"], 1)
                    dve.wait_ge(s["h_ready"], b * MH + m + 1)
                    if m >= 1:
                        dve.wait_ge(s["silu_done"], b * MH + m)
                        largest(m - 1)
                    body.add(nc.vector.tensor_scalar(y[:], h[:, 1:S + 1], conv[:, m, 1:2], conv[:, m, 3:4], ALU.mult, ALU.add))
                    body.wait()
                    body.add(nc.vector.scalar_tensor_tensor(y[:], h[:, 0:S], conv[:, m, 0:1], y[:], ALU.mult, ALU.add))
                    body.wait()
                    nc.vector.scalar_tensor_tensor(y[:], h[:, 2:S + 2], conv[:, m, 2:3], y[:], ALU.mult, ALU.add).then_inc(s["conv_ready"], 1)
                largest(MH - 1)
                dve.wait_ge(s["big_done"], b * MH + MH)
                dve.sem_inc(s["big_ready"], 1)
                dve.wait_ge(s["big_turned"], b + 1)
                body.add(nc.vector.tensor_reduce(size[:], psf[0].rearrange("p (t n) -> p t n", t=NT), AX.X, ALU.max))
                body.wait()
                body.add(nc.vector.tensor_scalar(size[:], size[:], 1e-5, None, ALU.max))
                body.wait()
                body.add(nc.vector.reciprocal(inv[:], size[:]))
                body.wait()
                body.add(nc.vector.tensor_scalar(inv[:], inv[:], 127.0, None, ALU.mult))
                body.wait()
                for t in range(NT):
                    ins = nc.vector.tensor_scalar(diag2[:, t * P:(t + 1) * P], c.ident[:], inv[:, t:t + 1], None, ALU.mult)
                    if t < NT - 1:
                        body.add(ins)
                ins.then_inc(s["diag2_ready"], 1)
                body.add(nc.vector.tensor_scalar(back[:], size[:], mean[:, 1:2], 1.0 / 127.0, ALU.mult, ALU.mult))
                body.wait()
                body.add(nc.vector.tensor_scalar(back[:], back[:], c.gates[:, gate:gate + 1], None, ALU.mult))
                dve.wait_ge(s["row2_ps"], b + 1)
                for m in range(MH):
                    body.add(nc.vector.tensor_tensor(act_out[:, m, :], act_out[:, m, :], psf[1], ALU.mult))
                    body.wait()
                    body.add(nc.vector.tensor_scalar(act_out[:, m, :], act_out[:, m, :], ROUND, -ROUND, ALU.add, ALU.add))
                    body.wait()
                    nc.vector.tensor_scalar(hq[:, m, :], act_out[:, m, :], 127.0, -128.0, ALU.min, ALU.max).then_inc(s["hq_ready"], 1)
                dve.wait_ge(s["out_ready"], b + 1)
                for t in range(NT):
                    xs = x[:, bass.ds(b * NT + t, 1), :].rearrange("p o d -> p (o d)")
                    ins = nc.vector.scalar_tensor_tensor(xs, out_ps[:, t, :], back[:, t:t + 1], xs, ALU.mult, ALU.add)
                    if t < NT - 1:
                        body.add(ins)
                ins.then_inc(s["x_ready"], 1)
                body.close()
                pause(dve, s["x_ready"], b + 1, s["dve_passed"])




def moe(nc, c, name, x_in, x_out, gate, top, io, w, ln=None, base=None):
    E = EXPERTS
    DH = w["gate"].shape[1] // KD
    MH = DH // P
    ST = SLOTS // P
    TILES = slot_tiles(top)
    assert TILES % 2 == 1
    up = "up" in w
    n_w = 3 if up else 2
    HID = 4
    FAR = float(2 * TILES * SLOTS)
    slots_in, slots_out = io["slots_in"][0:TILES * SLOTS, :], io["slots_out"][0:TILES * SLOTS, :]
    with ExitStack() as ctx:
        def sb(n, shape, dt=F32):
            return ctx.enter_context(nc.sbuf_tensor(f"{name}_{n}", shape, dt))

        def ps(n, shape):
            return ctx.enter_context(nc.psum_tensor(f"{name}_{n}", shape, F32))

        xT = sb("xT", [P, KD, TOK])
        keep = normed(nc, ctx, c, f"{name}n", x_in, "plain", ln, ((xT, ln is not None),), keep_xn=True)
        x, xn = keep.x, keep.xn

        wr, br = sb("wr", [P, KD, E]), sb("br", [P, E])
        tile_no, part_no = sb("tile_no", [P, TILES]), sb("part_no", [P, 1])
        lg, rank = sb("lg", [P, TT, E]), sb("rank", [P, TT, E])
        cmp_ = sb("cmp", [P, E, TT, E])
        sel, slot, wt = sb("sel", [P, TT, E]), sb("slot", [P, TT, E]), sb("wt", [P, TT, E])
        lead, total = sb("lead", [P, TT]), sb("total", [P, TT])
        tiles_of_e, ends = sb("tiles_of_e", [P, E]), sb("ends", [P, E])
        passed_e = sb("passed_e", [P, TILES, E])
        expert = sb("expert", [P, TILES])
        expert_row = sb("expert_row", [P, TILES], U32)
        row_now = [sb(f"row_now{i}", [P, 1], U32) for i in range(2)]
        at, at_row = sb("at", [P, top, TT]), sb("at_row", [P, top, TT], U32)
        share = sb("share", [P, top, TT])
        weight_names = ("gate", "up", "down") if up else ("gate", "down")
        wb = [{n: sb(f"{n}{i}", [P, w[n].shape[1]]) for n in weight_names} for i in range(2)]
        xg = [sb(f"xg{i}", [P, ST, D]) for i in range(2)]
        xgT = [sb(f"xgT{i}", [P, KD, SLOTS]) for i in range(2)]
        hh = sb("hh", [P, MH, SLOTS])
        sg = sb("sg", [P, 2, SLOTS])
        y = [sb(f"y{i}", [P, ST, D]) for i in range(2)]
        yg = sb("yg", [P, TT, top, D])
        if base is not None:
            base_sb = sb("base", [P, TT, D])
        if ln is not None:
            lnw = sb("lnw", [P, KD, 2])
        hid = ps("hid", [P, HID, 2, SLOTS])
        turn = ps("turn", [P, KD, SLOTS])
        out_ps = [ps(f"out{i}", [P, ST, D]) for i in range(2)]
        routed = ps("routed", [P, 3, TT * E])

        names = ("r_loaded base_loaded lg_ps step shift_ready ex_ready sel_ready count_ready rows_ready row_taken slots_ready scattered "
                 "w_loaded0 w_loaded1 xg_loaded0 xg_loaded1 turned xgt_ready hid_ready silu_done h_ready down_done y_ready "
                 "y_stored0 y_stored1 share_ready added out_ready stored pe_passed pool_passed").split()
        s = {n: c.semaphore(f"{name}_{n}") for n in names}
        gathered = [c.semaphore(f"{name}_gathered{n}") for n in range(NC)]
        consts = [(wr, io[f"{name}_wr"].rearrange("(k p) e -> p k e", p=P)), (br, row_tile(io[f"{name}_br"], P)),
                  (tile_no, row_tile(io["tile_numbers"][0:TILES], P)), (part_no, io["part_numbers"])]
        if ln is not None:
            consts.append((lnw, ln))
        n_cst = 16 * len(consts)
        block = ctx.enter_context(nc.Block())

        @block.sync
        def _(sp):
            for dst, src in consts:
                sp.dma_start(dst[:], src).then_inc(s["r_loaded"], 16)
            if base is not None:
                sp.dma_start(base_sb[:], tiles_of(base, 0, TT)).then_inc(s["base_loaded"], 16)

            def load(first, i):
                sp.dma_start(xg[i][:], slots_in[bass.ds(first, SLOTS), :].rearrange("(t p) d -> p t d", p=P)).then_inc(s[f"xg_loaded{i}"], 16)

            def store(first, i):
                sp.dma_start(slots_out[bass.ds(first, SLOTS), :].rearrange("(t p) d -> p t d", p=P), y[i][:]).then_inc(s[f"y_stored{i}"], 16)

            sp.wait_ge(s["scattered"], 16 * TT * top)
            load(0, 0)
            load(SLOTS, 1)
            with sp.Fori(0, (TILES - 3) // 2) as r:
                for i in range(2):
                    v = r * 2 + i
                    ahead, here = sp.snap(v * SLOTS + 2 * SLOTS), sp.snap(v * SLOTS)
                    sp.wait_ge(s["turned"], v + 1)
                    load(ahead, i)
                    sp.wait_ge(s["y_ready"], v + 3)
                    store(here, i)
            for v in range(TILES - 3, TILES):
                if v + 2 < TILES:
                    sp.wait_ge(s["turned"], v + 1)
                    load((v + 2) * SLOTS, v % 2)
                sp.wait_ge(s["y_ready"], v + 3)
                store(v * SLOTS, v % 2)
            for n in range(NC):
                sp.wait_ge(s["out_ready"], n + 1)
                sp.dma_start(tiles_of(x_out, n * CH, CT), x[:, n * CT:(n + 1) * CT, :]).then_inc(s["stored"], 16)
            sp.wait_ge(s["stored"], 16 * NC)

        @block.gpsimd
        def _(pool):
            def fetch(v, i):
                nc.gpsimd.tensor_copy(row_now[i][:], expert_row[:, bass.ds(v, 1)]).then_inc(s["row_taken"], 1)
                pause(pool, s["row_taken"], v + 1, s["pool_passed"])
                for n in weight_names:
                    pool.indirect_dma_start(wb[i][n][:], None, w[n],
                                            bass.IndirectOffsetOnAxis(row_now[i][:], 0)).then_inc(s[f"w_loaded{i}"], 16)

            pool.wait_ge(s["rows_ready"], 1)
            fetch(0, 0)
            pool.wait_ge(c.cleared, 16)
            pool.wait_ge(s["slots_ready"], 1)
            for t in range(TT):
                for j in range(top):
                    pool.indirect_dma_start(slots_in, bass.IndirectOffsetOnAxis(at_row[:, j, t:t + 1], 0), xn[:, t, :],
                                            None).then_inc(s["scattered"], 16)
            fetch(1, 1)
            with pool.Fori(0, (TILES - 3) // 2) as r:
                for i in range(2):
                    v = r * 2 + i
                    pause(pool, s["down_done"], v + 1, s["pool_passed"])
                    fetch(v + 2, i)
            pool.wait_ge(s["down_done"], TILES - 2)
            fetch(TILES - 1, 0)
            pool.wait_ge(s["y_stored0"], 16 * (TILES // 2 + 2))
            pool.wait_ge(s["y_stored1"], 16 * (TILES // 2 + 1))
            for t in range(TT):
                for j in range(top):
                    pool.indirect_dma_start(yg[:, t, j, :], None, slots_out,
                                            bass.IndirectOffsetOnAxis(at_row[:, j, t:t + 1], 0)).then_inc(gathered[t // CT], 16)

        @block.tensor
        def _(pe):
            pe.wait_ge(s["r_loaded"], n_cst)
            for t in range(TT):
                for k in range(KD):
                    last = nc.tensor.matmul(routed[:, 0, t * E:(t + 1) * E], xT[:, k, t * P:(t + 1) * P], wr[:, k, :],
                                            start=k == 0, stop=k == KD - 1)
            last.then_inc(s["lg_ps"], 1)
            pe.wait_ge(s["sel_ready"], 1)
            flat = sel[:].rearrange("p t e -> p (t e)")
            nc.tensor.matmul(routed[:, 1, :], c.earlier[:], flat, start=True, stop=False)
            for d in range(1, TT):
                nc.tensor.matmul(routed[:, 1, d * E:], c.ones[:], flat[:, 0:(TT - d) * E], start=False, stop=d == TT - 1)
            for t in range(TT):
                last = nc.tensor.matmul(routed[:, 2, 0:E], c.ones[:], sel[:, t, :], start=t == 0, stop=t == TT - 1)
            last.then_inc(s["count_ready"], 1)

            def turn_tile(i):
                for k in range(KD):
                    for t in range(ST):
                        last = nc.tensor.transpose(turn[:, k, t * P:(t + 1) * P], xg[i][:, t, k * P:(k + 1) * P], c.ident[:])
                last.then_inc(s["turned"], 1)

            def tile(v, i, r, more):
                pe.wait_ge(s["xgt_ready"], v * KD + KD)
                pause(pe, s[f"w_loaded{i}"], r * 16 * n_w + 16 * n_w, s["pe_passed"])
                for m in range(MH):
                    pe.wait_ge(s["h_ready"], v * MH + m + 1)
                    for j in range(n_w - 1):
                        for k in range(KD):
                            col = k * DH + m * P
                            last = nc.tensor.matmul(hid[:, m % HID, j, :], wb[i][weight_names[j]][:, col:col + P], xgT[i][:, k, :],
                                                    start=k == 0, stop=k == KD - 1)
                    last.then_inc(s["hid_ready"], 1)
                if more:
                    pause(pe, s[f"xg_loaded{1 - i}"], (r + i) * 16 + 16, s["pe_passed"])
                    turn_tile(1 - i)
                pe.wait_ge(s["y_ready"], v + 1)
                for t in range(ST):
                    for k in range(MH):
                        if t == 0:
                            pe.wait_ge(s["h_ready"], v * MH + HID + k + 1)
                        last = nc.tensor.matmul(out_ps[i][:, t, :], hh[:, k, t * P:(t + 1) * P], wb[i]["down"][:, k * D:(k + 1) * D],
                                                start=k == 0, stop=k == MH - 1)
                last.then_inc(s["down_done"], 1)

            pe.wait_ge(s["xg_loaded0"], 16)
            turn_tile(0)
            with pe.Fori(0, TILES // 2) as r:
                for i in range(2):
                    tile(r * 2 + i, i, r, True)
            tile(TILES - 1, 0, TILES // 2, False)

        @block.scalar
        def _(act):
            act.wait_ge(s["r_loaded"], n_cst)
            if top > 1:
                act.wait_ge(s["shift_ready"], 1)
                nc.scalar.activation(wt[:], wt[:], ACT.Exp).then_inc(s["ex_ready"], 1)

            def spread(v, i):
                act.wait_ge(s["turned"], v + 1)
                for k in range(KD):
                    if ln is None:
                        ins = nc.scalar.activation(xgT[i][:, k, :], turn[:, k, :], ACT.Copy)
                    else:
                        ins = nc.scalar.activation(xgT[i][:, k, :], turn[:, k, :], ACT.Identity, scale=lnw[:, k, 0:1], bias=lnw[:, k, 1:2])
                    ins.then_inc(s["xgt_ready"], 1)

            def tile(v, i, more):
                for m in range(MH):
                    act.wait_ge(s["hid_ready"], v * MH + m + 1)
                    if up:
                        if m >= 2:
                            act.wait_ge(s["h_ready"], v * MH + HID + m - 1)
                        nc.scalar.activation(sg[:, m % 2, :], hid[:, m % HID, 0, :], ACT.Silu).then_inc(s["silu_done"], 1)
                    else:
                        nc.scalar.activation(hh[:, m, :], hid[:, m % HID, 0, :], ACT.Gelu_apprx_tanh).then_inc(s["h_ready"], 1)
                if more:
                    spread(v + 1, 1 - i)

            spread(0, 0)
            with act.Fori(0, TILES // 2) as r:
                for i in range(2):
                    tile(r * 2 + i, i, True)
            tile(TILES - 1, 0, False)

        @block.vector
        def _(dve):
            step = Tally(dve, s["step"])
            dve.sem_inc(s["h_ready"], HID)
            dve.sem_inc(s["y_ready"], 2)
            for i in range(2):
                dve.sem_inc(s[f"y_stored{i}"], 16)
            dve.wait_ge(s["r_loaded"], n_cst)
            dve.wait_ge(s["lg_ps"], 1)
            step.add(nc.vector.tensor_tensor(lg[:], routed[:, 0, :].rearrange("p (t e) -> p t e", e=E),
                                             br[:].unsqueeze(1).broadcast_to([P, TT, E]), ALU.add))
            step.wait()
            for f in range(E):
                n = f + 1
                step.add(nc.vector.tensor_tensor(cmp_[:, f, :, 0:n], lg[:, :, f:n].broadcast_to([P, TT, n]), lg[:, :, 0:n], ALU.is_gt))
                if n < E:
                    step.add(nc.vector.tensor_tensor(cmp_[:, f, :, n:E], lg[:, :, f:n].broadcast_to([P, TT, E - n]), lg[:, :, n:E], ALU.is_ge))
            if top > 1:
                step.add(nc.vector.tensor_reduce(lead[:], lg[:], AX.X, ALU.max))
            step.wait()
            step.add(nc.vector.tensor_reduce(rank[:], cmp_[:].rearrange("p f t e -> p t e f"), AX.X, ALU.add))
            step.wait()
            nc.vector.tensor_scalar(sel[:], rank[:], top - 0.5, None, ALU.is_lt).then_inc(s["sel_ready"], 1)
            dve.wait_ge(s["sel_ready"], 1)
            if top > 1:
                nc.vector.tensor_tensor(wt[:], lg[:], lead[:].unsqueeze(2).broadcast_to([P, TT, E]), ALU.subtract).then_inc(s["shift_ready"], 1)
            dve.wait_ge(s["count_ready"], 1)
            step.add(nc.vector.tensor_scalar(tiles_of_e[:], routed[:, 2, 0:E], 1.0 / SLOTS, (SLOTS - 0.5) / SLOTS - 0.5, ALU.mult, ALU.add))
            step.wait()
            step.add(nc.vector.tensor_scalar(tiles_of_e[:], tiles_of_e[:], ROUND, -ROUND, ALU.add, ALU.add))
            step.wait()
            step.add(nc.vector.tensor_copy(ends[:, 0:1], tiles_of_e[:, 0:1]))
            for e in range(1, E):
                step.wait()
                step.add(nc.vector.tensor_tensor(ends[:, e:e + 1], ends[:, e - 1:e], tiles_of_e[:, e:e + 1], ALU.add))
            step.wait()
            step.add(nc.vector.tensor_tensor(passed_e[:, :, 0:E - 1], tile_no[:].unsqueeze(2).broadcast_to([P, TILES, E - 1]),
                                             ends[:, 0:E - 1].unsqueeze(1).broadcast_to([P, TILES, E - 1]), ALU.is_ge))
            step.wait()
            step.add(nc.vector.tensor_reduce(expert[:], passed_e[:, :, 0:E - 1], AX.X, ALU.add))
            step.wait()
            step.add(nc.vector.tensor_scalar(expert[:], expert[:], float(P), part_no[:, 0:1], ALU.mult, ALU.add))
            step.wait()
            nc.vector.tensor_copy(expert_row[:], expert[:]).then_inc(s["rows_ready"], 1)
            step.add(nc.vector.tensor_tensor(ends[:], ends[:], tiles_of_e[:], ALU.subtract))
            step.wait()
            step.add(nc.vector.tensor_scalar(ends[:], ends[:], float(SLOTS), None, ALU.mult))
            step.wait()
            step.add(nc.vector.tensor_tensor(slot[:], routed[:, 1, :].rearrange("p (t e) -> p t e", e=E),
                                             ends[:].unsqueeze(1).broadcast_to([P, TT, E]), ALU.add))
            step.add(nc.vector.tensor_scalar(rank[:], sel[:], -FAR, FAR, ALU.mult, ALU.add))
            step.wait()
            step.add(nc.vector.tensor_tensor(rank[:], rank[:], slot[:], ALU.add))
            step.wait()
            step.add(nc.vector.tensor_reduce(at[:, 0, :], rank[:], AX.X, ALU.min))
            if top > 1:
                dve.wait_ge(s["shift_ready"], 1)
                step.add(nc.vector.tensor_tensor(lg[:], slot[:], sel[:], ALU.mult))
                step.wait()
                step.add(nc.vector.tensor_reduce(at[:, 1, :], lg[:], AX.X, ALU.max))
            step.wait()
            nc.vector.tensor_copy(at_row[:], at[:]).then_inc(s["slots_ready"], 1)
            if top > 1:
                dve.wait_ge(s["ex_ready"], 1)
                step.add(nc.vector.tensor_tensor(wt[:], wt[:], sel[:], ALU.mult))
                step.wait()
                step.add(nc.vector.tensor_reduce(total[:], wt[:], AX.X, ALU.add))
                step.wait()
                step.add(nc.vector.reciprocal(total[:], total[:]))
                step.wait()
                step.add(nc.vector.tensor_scalar(total[:], total[:], c.gates[:, gate:gate + 1], None, ALU.mult))
                step.wait()
                step.add(nc.vector.tensor_tensor(wt[:], wt[:], total[:].unsqueeze(2).broadcast_to([P, TT, E]), ALU.mult))
                for j in range(top):
                    step.wait()
                    step.add(nc.vector.tensor_tensor(lg[:], slot[:], at[:, j, :].unsqueeze(2).broadcast_to([P, TT, E]), ALU.is_equal))
                    step.wait()
                    step.add(nc.vector.tensor_tensor(lg[:], lg[:], wt[:], ALU.mult))
                    step.wait()
                    step.add(nc.vector.tensor_reduce(share[:, j, :], lg[:], AX.X, ALU.add))

            def tile(v, i, r):
                if up:
                    for m in range(MH):
                        dve.wait_ge(s["silu_done"], v * MH + m + 1)
                        nc.vector.tensor_tensor(hh[:, m, :], sg[:, m % 2, :], hid[:, m % HID, 1, :], ALU.mult).then_inc(s["h_ready"], 1)
                dve.wait_ge(s["down_done"], v + 1)
                dve.wait_ge(s[f"y_stored{i}"], r * 16 + 16)
                nc.vector.tensor_copy(y[i][:], out_ps[i][:]).then_inc(s["y_ready"], 1)

            with dve.Fori(0, TILES // 2) as r:
                for i in range(2):
                    tile(r * 2 + i, i, r)
            tile(TILES - 1, 0, TILES // 2)
            g = c.gates[:, gate:gate + 1]
            if base is not None:
                dve.wait_ge(s["base_loaded"], 16)
                step.add(nc.vector.scalar_tensor_tensor(x[:], x[:], g, base_sb[:], ALU.mult, ALU.add))
            for n in range(NC):
                dve.wait_ge(gathered[n], 16 * CT * top)
                for t in range(n * CT, (n + 1) * CT):
                    for j in range(top):
                        if t == n * CT:
                            step.wait()
                        scale = share[:, j, t:t + 1] if top > 1 else g
                        ins = nc.vector.scalar_tensor_tensor(x[:, t, :], yg[:, t, j, :], scale, x[:, t, :], ALU.mult, ALU.add)
                        if j < top - 1 or t < (n + 1) * CT - 1:
                            step.add(ins)
                        if j < top - 1 and t > n * CT:
                            step.wait()
                ins.then_inc(s["out_ready"], 1)


def pack64(wq, wk, wv, wo):
    pairs = wq.shape[1] // P
    return np.stack([np.stack([by_partition(w[:, i * P:(i + 1) * P]) for w in (wq, wk, wv)], 1) for i in range(pairs)]), by_partition(wo)


def columns(*vectors):
    return np.stack([v.reshape(-1, P).T for v in vectors], 2)


def pack16(wq, bq, wk, bk, wv, bv, wo, bo):
    def dims_first(m):
        return m.reshape(m.shape[0], 2, 8, 16).transpose(0, 1, 3, 2).reshape(m.shape[0], D)

    zero = np.zeros(D, np.float32)
    bias = [dims_first((zero if v is None else v).reshape(1, D)).reshape(2, P).T for v in (bq, bk)]
    values = np.zeros((D, 16, 32), np.float32)
    values[:, :, 0:16] = wv.reshape(D, 16, 16)
    row = np.zeros((16, 32), np.float32)
    row[:, 0:16] = (zero if bv is None else bv).reshape(16, 16)
    row[:, 16] = 1.0
    out = np.zeros((16, 32, D), np.float32)
    out[:, 0:16] = wo.reshape(16, 16, D)
    if bo is not None:
        out[0, 16] = bo
    return {"q": by_partition(dims_first(wq)), "k": by_partition(dims_first(wk)), "v": by_partition(values.reshape(D, 2 * D)),
            "o": by_partition(out.reshape(2 * D, D)), "bqk": np.concatenate(bias, 1), "bv": row.reshape(2 * D)}


def pack_experts(w):
    e, rows, n = w.shape
    return w.reshape(e, rows // P, P, n).transpose(0, 2, 1, 3).reshape(e * P, rows // P * n)


def numbers():
    return {"tile_numbers": np.arange(slot_tiles(2), dtype=np.float32), "part_numbers": np.arange(P, dtype=np.float32).reshape(P, 1)}


def by_partition(w):
    return w.reshape(-1, P, w.shape[1]).transpose(1, 0, 2)


def kernel(**inputs):
    import concourse.bacc as _bacc
    from concourse.bass_utils import run_bass_kernel_spmd as _run

    a = {k: np.ascontiguousarray(v) for k, v in inputs.items()}
    arrays = lay_out(a)
    nc = _bacc.Bacc("TRN2", target_bir_lowering=False, num_devices=1)
    io = {}
    feed = {}
    for n, v in arrays.items():
        v = np.ascontiguousarray(v)
        feed[f"in_{n}"] = v
        io[n] = nc.dram_tensor(f"in_{n}", v.shape, mybir.dt.from_np(v.dtype), kind="ExternalInput").ap()
    io["out"] = nc.dram_tensor("out_0", (TOK, D), F32, kind="ExternalOutput").ap()
    for i in range(8):
        io[f"x{i}"] = nc.dram_tensor(f"x_{i}", (TOK, D), F32, kind="Internal").ap()
    program(nc, io)
    r = _run(nc, [feed], core_ids=[0])
    return r.results[0]["out_0"].reshape(B, S, D)


def weights(io, name):
    return {k[len(name) + 1:]: v for k, v in io.items() if k.startswith(name + "_")}


def program(nc, io):
    with ExitStack() as ctx:
        c = setup(nc, ctx, io)
        io["scratch"] = nc.dram_tensor("scratch", (TT, P), F32, kind="Internal").ap()
        attention16(nc, c, "l0x", io["x"], io["x0"], weights(io, "l0x"), 0, ctx_t=io["ctx_t"], mask=io["mask0"],
                    slots=io["slots_in"])
        c.end_stage()
        ffn0(nc, c, "l0f", io["x0"], io["x1"], 4, io)
        c.end_stage()
        attention64(nc, c, "l1x", io["x1"], io["x2"], io["l1_qkv"], io["l1_wo"], 1, io["ctx"], io["mask1"], io["l1_ln"],
                    out_ln=(io["l1_go"], io["l1_bo"]))
        c.end_stage()
        ffn1(nc, c, "l1f", io["x2"], io["x3"], 5, io)
        c.end_stage()
        attention16(nc, c, "l2x", io["x3"], io["x4"], weights(io, "l2x"), 2, ctx_t=io["ctx_t"])
        c.end_stage()
        moe(nc, c, "l2f", io["x4"], io["x5"], 6, 2, io, weights(io, "l2e"))
        c.end_stage()
        attention64(nc, c, "l3x", io["x5"], io["x6"], io["l3_qkv"], io["l3_wo"], 3, io["ctx"], io["mask3"], io["l3_ln"],
                    rms=io["l3_gam"], out_b=io["l3_bo"])
        c.end_stage()
        attention16(nc, c, "l3a", io["x6"], io["x7"], weights(io, "l3a"), None, ln=io["l3_ln1"], twice=True)
        c.end_stage()
        moe(nc, c, "l3f", io["x7"], io["out"], 7, 1, io, weights(io, "l3e"), io["l3_ln2"], io["x6"])
        c.end_stage()


def lay_out(a):
    arrays = {"x": a["x"].reshape(TOK, D), "ctx": a["ctx_1024"].reshape(B * SC, D), "ctx_t": a["ctx_1024"].reshape(B * SC, D).T,
              "g_xattn": a["g_xattn"], "g_ffn": a["g_ffn"], "mask0": a["mask_Bx1x1xS2_fk0"].reshape(B, SC),
              "mask1": a["mask_BxS2_bf1"], "mask3": a["mask_BxS2_bk0"]}
    n = "L0_xattn_"
    for k, v in pack16(*[a[n + k] for k in ("Wq", "bq", "Wk", "bk", "Wv", "bv", "Wo", "bo")]).items():
        arrays["l0x_" + k] = v
    n = "L0_ffn_"
    arrays["l0_gammas"] = columns(a[n + "light_gamma"], a[n + "heavy_gamma"])
    arrays["l0_token"] = a[n + "routing_token"]
    for k, m in (("w1l", "light_w1"), ("w2l", "light_w2"), ("w1h", "heavy_w1"), ("w2h", "heavy_w2"), ("b2l", "light_b2"), ("b2h", "heavy_b2")):
        arrays["l0_" + k] = a[n + m]
    arrays["l0_b1"] = np.concatenate([a[n + "light_b1"], a[n + "heavy_b1"]]).reshape(-1, P).T
    n = "L1_xattn_"
    wkv = a[n + "Wkv"]
    half = wkv.shape[1] // 2
    arrays["l1_qkv"], arrays["l1_wo"] = pack64(a[n + "Wq"], wkv[:, :half], wkv[:, half:], a[n + "Wout"])
    arrays["l1_ln"] = columns(a[n + "g_l"], a[n + "b_l"], a[n + "g_x"], a[n + "b_x"])
    arrays["l1_go"], arrays["l1_bo"] = a[n + "g_o"], a[n + "b_o"]
    n = "L1_ffn_"
    arrays["l1_w1"], arrays["l1_w2"] = a[n + "w1"].T, a[n + "w2"].T
    cw = a[n + "conv_w"]
    arrays["l1_conv"] = columns(cw[:, 0, 0], cw[:, 0, 1], cw[:, 0, 2], a[n + "conv_b"])
    n = "L2_xattn_"
    for k, v in pack16(*[a[n + k].T for k in ("Wq", "bq", "Wk", "bk", "Wv", "bv", "Wo", "bo")]).items():
        arrays["l2x_" + k] = v
    n = "L2_ffn_"
    for k, m in (("gate", "Wgate"), ("up", "Wup"), ("down", "Wdown")):
        arrays["l2e_" + k] = pack_experts(a[n + m].transpose(0, 2, 1))
    arrays["l2f_wr"], arrays["l2f_br"] = a[n + "wg"].T, a[n + "bg"]
    n = "L3_xattn_"
    wkv = a[n + "W_kv"]
    half = wkv.shape[1] // 2
    arrays["l3_qkv"], arrays["l3_wo"] = pack64(a[n + "W_q"], wkv[:, :half], wkv[:, half:], a[n + "W_out"])
    arrays["l3_ln"] = columns(a[n + "ln_l_g"], a[n + "ln_l_b"], a[n + "ln_x_g"], a[n + "ln_x_b"])
    arrays["l3_gam"] = np.stack([np.concatenate([a[n + "q_gamma"]] * 2), np.concatenate([a[n + "k_gamma"]] * 2)], 1)
    arrays["l3_bo"] = a[n + "b_out"]
    n = "L3_ffn_"
    w = a[n + "w_qkv"]
    for k, v in pack16(w[:, :D], None, w[:, D:2 * D], None, w[:, 2 * D:], None, a[n + "w_proj"], None).items():
        arrays["l3a_" + k] = v
    arrays["l3_ln1"] = columns(a[n + "ln1_w"], a[n + "ln1_b"])
    arrays["l3_ln2"] = columns(a[n + "ln2_w"], a[n + "ln2_b"])
    arrays["l3e_gate"], arrays["l3e_down"] = pack_experts(a[n + "w1"]), pack_experts(a[n + "w2"])
    arrays["l3f_wr"], arrays["l3f_br"] = a[n + "gate_w"], a[n + "gate_b"]
    arrays.update(numbers())
    return arrays
```
